# Optimizing a Trainium2 kernel written in Bass

```python
import numpy as np
import jax
import jax.numpy as jnp

def _softmax(x, axis=-1):
    return jax.nn.softmax(x, axis=axis)

def _gelu(x):
    return jax.nn.gelu(x, approximate=True)

def _silu(x):
    return jax.nn.silu(x)

def _sigmoid(x):
    return jax.nn.sigmoid(x)

def _layernorm(x, axis=-1, eps=1e-05):
    m = jnp.mean(x, axis=axis, keepdims=True)
    v = jnp.var(x, axis=axis, keepdims=True)
    return (x - m) / jnp.sqrt(v + eps)

def _scatter_add(tgt, idx, src, axis=0):
    return tgt.at[idx].add(src)

def _segment_sum(src, seg, n):
    return jax.ops.segment_sum(src, seg, n)
kernel_name = 'mk_seq_postln_d1_jaxref_r8_d78b64'

def setup_inputs(seed: int=0):
    np.random.seed(seed)
    _w = jnp.asarray

    def _L0_attn_setup():
        import jax, jax.numpy as jnp
        import numpy as np
        from jax import lax
        D_MODEL, D_STATE, D_CONV, D_INNER, DT_RANK = (128, 16, 4, 256, 64)
        B_SZ, L_SEQ = (2, 512)

        def _silu(v):
            return v * jax.nn.sigmoid(v)

        def _layernorm(v, w, b, eps=1e-05):
            mu = jnp.mean(v, axis=-1, keepdims=True)
            var = jnp.var(v, axis=-1, keepdims=True)
            return (v - mu) * lax.rsqrt(var + eps) * w + b

        def _selective_scan(u, delta, A, Bm, Cm, Dp):
            Bb, L, d_inner = u.shape
            N = A.shape[1]

            def step(h, inp):
                dt_t, u_t, B_t, C_t = inp
                A_bar = jnp.exp(dt_t[..., None] * A)
                h = A_bar * h + dt_t[..., None] * B_t[:, None, :] * u_t[..., None]
                y = jnp.sum(h * C_t[:, None, :], axis=-1)
                return (h, y)
            h0 = jnp.zeros((Bb, d_inner, N), u.dtype)
            xs = (jnp.swapaxes(delta, 0, 1), jnp.swapaxes(u, 0, 1), jnp.swapaxes(Bm, 0, 1), jnp.swapaxes(Cm, 0, 1))
            _, ys = lax.scan(step, h0, xs)
            y = jnp.swapaxes(ys, 0, 1)
            return y + u * Dp[None, None, :]
        key = jax.random.key(seed)
        ks = jax.random.split(key, 12)
        s = 0.02
        x = jax.random.normal(ks[0], (B_SZ, L_SEQ, D_MODEL), jnp.float32)
        norm_w = jnp.ones((D_MODEL,), jnp.float32)
        norm_b = jnp.zeros((D_MODEL,), jnp.float32)
        W_in = jax.random.normal(ks[1], (D_MODEL, 2 * D_INNER), jnp.float32) * s
        conv_w = jax.random.normal(ks[2], (D_INNER, 1, D_CONV), jnp.float32) * 0.5
        conv_b = jnp.zeros((D_INNER,), jnp.float32)
        W_x = jax.random.normal(ks[3], (D_INNER, DT_RANK + 2 * D_STATE), jnp.float32) * s
        W_dt = jax.random.normal(ks[4], (DT_RANK, D_INNER), jnp.float32) * s
        dt_init = jnp.exp(jax.random.uniform(ks[5], (D_INNER,)) * (np.log(0.1) - np.log(0.001)) + np.log(0.001))
        dt_init = jnp.clip(dt_init, 0.0001, None)
        b_dt = dt_init + jnp.log(-jnp.expm1(-dt_init))
        A_log = jnp.log(jnp.broadcast_to(jnp.arange(1, D_STATE + 1, dtype=jnp.float32)[None, :], (D_INNER, D_STATE)))
        D = jnp.ones((D_INNER,), jnp.float32)
        W_out = jax.random.normal(ks[6], (D_INNER, D_MODEL), jnp.float32) * s
        return {'x': x, 'norm_w': norm_w, 'norm_b': norm_b, 'W_in': W_in, 'conv_w': conv_w, 'conv_b': conv_b, 'W_x': W_x, 'W_dt': W_dt, 'b_dt': b_dt, 'A_log': A_log, 'D': D, 'W_out': W_out}
    _L0_attn_in = _L0_attn_setup()

    def _L0_ffn_setup():
        import jax, jax.numpy as jnp
        import numpy as np
        D = 128
        H = 4
        DF = 512
        E = 8
        EPS = 1e-05

        def _layer_norm(x, g, b):
            mu = jnp.mean(x, axis=-1, keepdims=True)
            var = jnp.mean(jnp.square(x - mu), axis=-1, keepdims=True)
            return (x - mu) * jax.lax.rsqrt(var + EPS) * g + b

        def _mha(x, Wqkv, bqkv, Wo, bo):
            S, B, _ = x.shape
            hd = D // H
            qkv = x @ Wqkv.T + bqkv
            q, k, v = jnp.split(qkv, 3, axis=-1)
            to_heads = lambda t: t.reshape(S, B, H, hd).transpose(1, 2, 0, 3)
            q, k, v = (to_heads(q), to_heads(k), to_heads(v))
            scores = jnp.einsum('bhqd,bhkd->bhqk', q, k) * (1.0 / np.sqrt(hd))
            att = jax.nn.softmax(scores, axis=-1)
            o = jnp.einsum('bhqk,bhkd->bhqd', att, v)
            o = o.transpose(2, 0, 1, 3).reshape(S, B, D)
            return o @ Wo.T + bo

        def _moe(x, Wg, W1, b1, W2, b2):
            S, B, _ = x.shape
            xf = x.reshape(S * B, D)
            logits = xf @ Wg.T
            idx = jnp.argmax(logits, axis=-1)
            out = jnp.zeros_like(xf)
            for e in range(E):
                m = (idx == e)[:, None].astype(xf.dtype)
                h = jax.nn.relu(xf @ W1[e] + b1[e])
                out = out + m * (h @ W2[e] + b2[e])
            return out.reshape(S, B, D)
        key = jax.random.key(seed)
        ks = jax.random.split(key, 16)
        S, B = (64, 8)
        s = lambda k, shape, fan: jax.random.normal(k, shape, jnp.float32) * (1.0 / np.sqrt(fan))
        return {'x': jax.random.normal(ks[0], (S, B, D), jnp.float32), 'Wqkv': s(ks[1], (3 * D, D), D), 'bqkv': jnp.zeros((3 * D,), jnp.float32), 'Wo': s(ks[2], (D, D), D), 'bo': jnp.zeros((D,), jnp.float32), 'g1': jnp.ones((D,), jnp.float32), 'be1': jnp.zeros((D,), jnp.float32), 'g2': jnp.ones((D,), jnp.float32), 'be2': jnp.zeros((D,), jnp.float32), 'Wg': s(ks[3], (E, D), D), 'W1': s(ks[4], (E, D, DF), D), 'b1': jnp.zeros((E, DF), jnp.float32), 'W2': s(ks[5], (E, DF, D), DF), 'b2': jnp.zeros((E, D), jnp.float32)}
    _L0_ffn_in = _L0_ffn_setup()
    _d = {'L0_attn_x': _L0_attn_in['x'], 'L0_attn_norm_w': _L0_attn_in['norm_w'], 'L0_attn_norm_b': _L0_attn_in['norm_b'], 'L0_attn_W_in': _L0_attn_in['W_in'], 'L0_attn_conv_w': _L0_attn_in['conv_w'], 'L0_attn_conv_b': _L0_attn_in['conv_b'], 'L0_attn_W_x': _L0_attn_in['W_x'], 'L0_attn_W_dt': _L0_attn_in['W_dt'], 'L0_attn_b_dt': _L0_attn_in['b_dt'], 'L0_attn_A_log': _L0_attn_in['A_log'], 'L0_attn_D': _L0_attn_in['D'], 'L0_attn_W_out': _L0_attn_in['W_out'], 'L0_ffn_Wqkv': _L0_ffn_in['Wqkv'], 'L0_ffn_bqkv': _L0_ffn_in['bqkv'], 'L0_ffn_Wo': _L0_ffn_in['Wo'], 'L0_ffn_bo': _L0_ffn_in['bo'], 'L0_ffn_g1': _L0_ffn_in['g1'], 'L0_ffn_be1': _L0_ffn_in['be1'], 'L0_ffn_g2': _L0_ffn_in['g2'], 'L0_ffn_be2': _L0_ffn_in['be2'], 'L0_ffn_Wg': _L0_ffn_in['Wg'], 'L0_ffn_W1': _L0_ffn_in['W1'], 'L0_ffn_b1': _L0_ffn_in['b1'], 'L0_ffn_W2': _L0_ffn_in['W2'], 'L0_ffn_b2': _L0_ffn_in['b2']}
    _x0 = _d['L0_attn_x']
    _d['L0_attn_x'] = jax.random.normal(jax.random.fold_in(jax.random.key(seed), 1), (8, 512, 128), dtype=_x0.dtype)
    del _x0
    return _d

def reference(L0_attn_x, L0_attn_norm_w, L0_attn_norm_b, L0_attn_W_in, L0_attn_conv_w, L0_attn_conv_b, L0_attn_W_x, L0_attn_W_dt, L0_attn_b_dt, L0_attn_A_log, L0_attn_D, L0_attn_W_out, L0_ffn_Wqkv, L0_ffn_bqkv, L0_ffn_Wo, L0_ffn_bo, L0_ffn_g1, L0_ffn_be1, L0_ffn_g2, L0_ffn_be2, L0_ffn_Wg, L0_ffn_W1, L0_ffn_b1, L0_ffn_W2, L0_ffn_b2):

    def _L0_attn_ref(x, norm_w, norm_b, W_in, conv_w, conv_b, W_x, W_dt, b_dt, A_log, D, W_out):
        import jax, jax.numpy as jnp
        import numpy as np
        from jax import lax
        D_MODEL, D_STATE, D_CONV, D_INNER, DT_RANK = (128, 16, 4, 256, 64)
        B_SZ, L_SEQ = (2, 512)

        def _silu(v):
            return v * jax.nn.sigmoid(v)

        def _layernorm(v, w, b, eps=1e-05):
            mu = jnp.mean(v, axis=-1, keepdims=True)
            var = jnp.var(v, axis=-1, keepdims=True)
            return (v - mu) * lax.rsqrt(var + eps) * w + b

        def _selective_scan(u, delta, A, Bm, Cm, Dp):
            Bb, L, d_inner = u.shape
            N = A.shape[1]

            def step(h, inp):
                dt_t, u_t, B_t, C_t = inp
                A_bar = jnp.exp(dt_t[..., None] * A)
                h = A_bar * h + dt_t[..., None] * B_t[:, None, :] * u_t[..., None]
                y = jnp.sum(h * C_t[:, None, :], axis=-1)
                return (h, y)
            h0 = jnp.zeros((Bb, d_inner, N), u.dtype)
            xs = (jnp.swapaxes(delta, 0, 1), jnp.swapaxes(u, 0, 1), jnp.swapaxes(Bm, 0, 1), jnp.swapaxes(Cm, 0, 1))
            _, ys = lax.scan(step, h0, xs)
            y = jnp.swapaxes(ys, 0, 1)
            return y + u * Dp[None, None, :]
        residual = x
        xn = _layernorm(x, norm_w, norm_b)
        xz = xn @ W_in
        x_ssm, z = jnp.split(xz, 2, axis=-1)
        xt = jnp.swapaxes(x_ssm, 1, 2)
        xt = jnp.pad(xt, ((0, 0), (0, 0), (D_CONV - 1, 0)))
        xc = lax.conv_general_dilated(xt, conv_w, window_strides=(1,), padding='VALID', feature_group_count=D_INNER, dimension_numbers=('NCH', 'OIH', 'NCH'))
        xc = xc + conv_b[None, :, None]
        x_conv = jnp.swapaxes(_silu(xc), 1, 2)
        x_dbl = x_conv @ W_x
        dt_low, B_mat, C_mat = jnp.split(x_dbl, [DT_RANK, DT_RANK + D_STATE], axis=-1)
        delta = jax.nn.softplus(dt_low @ W_dt + b_dt)
        A = -jnp.exp(A_log)
        y = _selective_scan(x_conv, delta, A, B_mat, C_mat, D)
        y = y * _silu(z)
        return residual + y @ W_out

    def _L0_ffn_ref(x, Wqkv, bqkv, Wo, bo, g1, be1, g2, be2, Wg, W1, b1, W2, b2):
        import jax, jax.numpy as jnp
        import numpy as np
        D = 128
        H = 4
        DF = 512
        E = 8
        EPS = 1e-05

        def _layer_norm(x, g, b):
            mu = jnp.mean(x, axis=-1, keepdims=True)
            var = jnp.mean(jnp.square(x - mu), axis=-1, keepdims=True)
            return (x - mu) * jax.lax.rsqrt(var + EPS) * g + b

        def _mha(x, Wqkv, bqkv, Wo, bo):
            S, B, _ = x.shape
            hd = D // H
            qkv = x @ Wqkv.T + bqkv
            q, k, v = jnp.split(qkv, 3, axis=-1)
            to_heads = lambda t: t.reshape(S, B, H, hd).transpose(1, 2, 0, 3)
            q, k, v = (to_heads(q), to_heads(k), to_heads(v))
            scores = jnp.einsum('bhqd,bhkd->bhqk', q, k) * (1.0 / np.sqrt(hd))
            att = jax.nn.softmax(scores, axis=-1)
            o = jnp.einsum('bhqk,bhkd->bhqd', att, v)
            o = o.transpose(2, 0, 1, 3).reshape(S, B, D)
            return o @ Wo.T + bo

        def _moe(x, Wg, W1, b1, W2, b2):
            S, B, _ = x.shape
            xf = x.reshape(S * B, D)
            logits = xf @ Wg.T
            idx = jnp.argmax(logits, axis=-1)
            out = jnp.zeros_like(xf)
            for e in range(E):
                m = (idx == e)[:, None].astype(xf.dtype)
                h = jax.nn.relu(xf @ W1[e] + b1[e])
                out = out + m * (h @ W2[e] + b2[e])
            return out.reshape(S, B, D)
        y = _layer_norm(x + _mha(x, Wqkv, bqkv, Wo, bo), g1, be1)
        z = _layer_norm(y + _moe(y, Wg, W1, b1, W2, b2), g2, be2)
        return z
    x = L0_attn_x
    x = _layernorm(x + _L0_attn_ref(x, L0_attn_norm_w, L0_attn_norm_b, L0_attn_W_in, L0_attn_conv_w, L0_attn_conv_b, L0_attn_W_x, L0_attn_W_dt, L0_attn_b_dt, L0_attn_A_log, L0_attn_D, L0_attn_W_out), axis=-1)
    x = _layernorm(x + _L0_ffn_ref(x, L0_ffn_Wqkv, L0_ffn_bqkv, L0_ffn_Wo, L0_ffn_bo, L0_ffn_g1, L0_ffn_be1, L0_ffn_g2, L0_ffn_be2, L0_ffn_Wg, L0_ffn_W1, L0_ffn_b1, L0_ffn_W2, L0_ffn_b2), axis=-1)
    return x

_drawn_inputs = setup_inputs


def setup_inputs(seed=0):
    import zlib

    import numpy as np

    out = dict(_drawn_inputs(seed))
    spreads = {'L0_attn_norm_w': (1.0, 0.6),
     'L0_attn_norm_b': (0.0, 0.8),
     'L0_attn_conv_b': (0.0, 0.68),
     'L0_attn_D': (1.0, 0.6),
     'L0_ffn_bqkv': (0.0, 0.1),
     'L0_ffn_bo': (0.0, 0.1),
     'L0_ffn_g1': (1.0, 0.2),
     'L0_ffn_be1': (0.0, 0.1),
     'L0_ffn_g2': (1.0, 0.2),
     'L0_ffn_be2': (0.0, 0.1),
     'L0_ffn_b1': (0.0, 0.268),
     'L0_ffn_b2': (0.0, 0.1)}
    factors = {'L0_attn_W_in': 3.355,
     'L0_attn_conv_w': 3.436,
     'L0_attn_W_x': 8.0,
     'L0_attn_W_dt': 8.0,
     'L0_attn_b_dt': 8.0,
     'L0_attn_A_log': 8.0,
     'L0_attn_W_out': 3.094}
    for name, (base, spread) in spreads.items():
        noise = np.random.default_rng([zlib.crc32(name.encode()), seed]).standard_normal(out[name].shape)
        drawn = base * np.exp(spread * noise) if base else spread * noise
        out[name] = jnp.asarray(drawn.astype(out[name].dtype))
    for name, factor in factors.items():
        out[name] = (out[name] * factor).astype(out[name].dtype)
    return out
```

```python
import numpy as np
import concourse.bass as bass
from concourse import mybir
from contextlib import ExitStack

ALU = mybir.AluOpType
ACT = mybir.ActivationFunctionType
AX = mybir.AxisListType
F32 = mybir.dt.float32
BF16 = mybir.dt.bfloat16

P = 128
EPS = 1e-5
POOL_B = (2, 5, 8, 11, 14)
LAG = 2


def log1p_factors():
    k = np.arange(600)
    y = (1 - np.cos(np.pi * (k + 0.5) / 600)) / 2
    fit = np.polynomial.chebyshev.Chebyshev.fit(y, np.log1p(y) / y, 8, domain=[0, 1])
    c = fit.convert(kind=np.polynomial.Polynomial).coef
    r = sorted((z for z in np.roots(c[::-1]) if z.imag > 0), key=lambda z: z.real)
    return float(c[8]), [(float(-z.real), float(z.imag) ** 2) for z in r]


def build_mamba(nc, x, norm_w, norm_b, W_in, conv_w, conv_b, W_x, W_dt, b_dt, A_log, D, W_out, x1_d):
    NS, L, DM = x.shape
    DI = W_dt.shape[1]
    R = W_dt.shape[0]
    N = A_log.shape[1]
    KC = conv_w.shape[2]
    H = DI // P
    T = L // P
    LP = L + KC - 1
    NT = NS * T
    XL = 2
    TT = P // NS
    GT = P // TT
    x1_g = x1_d.rearrange("(t g) p d -> t g p d", g=GT)
    lead, quad = log1p_factors()

    with ExitStack() as ctx:
        def sb(name, shape, dt=F32):
            return ctx.enter_context(nc.sbuf_tensor(name, shape, dt))

        def ps(name, shape, dt=F32):
            return ctx.enter_context(nc.psum_tensor(name, shape, dt))

        def sem(name):
            return ctx.enter_context(nc.semaphore(name))

        ident = sb("ident", [P, P])
        sel = sb("sel", [96, 2 * N, P], BF16)
        win = sb("win", [P, 2 * DI])
        cwb = sb("cwb", [P, DI, KC])
        wtap = sb("wtap", [P, KC, DI])
        cb = sb("cb", [P, H])
        cbh = sb("cbh", [P, H])
        wx = sb("wx", [P, H, R + 2 * N])
        wbc = sb("wbc", [P, H, 3, 2 * N])
        wdt = sb("wdt", [R, DI])
        bdt = sb("bdt", [P, H])
        alog = sb("alog", [P, H, N])
        aneg = sb("aneg", [P, H, N])
        dsk = sb("dsk", [P, H])
        wout = sb("wout", [P, H, DM])
        nw = sb("nw", [P, 1])
        nb = sb("nb", [P, 1])
        mhalf = sb("mhalf", [P, NT])
        xall = sb("xall", [P, NT, DM])
        stats = sb("stats", [P, T, 6])
        mv = sb("mv", [P, T, 2])
        mean = sb("mean", [P, NT])
        ve = sb("ve", [P, NT])
        rstd = sb("rstd", [P, NT])
        xn = sb("xn", [P, 2, T, DM])
        xnT = sb("xnT", [P, NS, LP])
        u = sb("u", [P, 2 * H * L])
        zs = sb("zs", [P, 2 * H * L])
        delta = sb("delta", [P, 2 * H * L])
        dtu = sb("dtu", [P, 2 * H * L])
        bcs = sb("bcs", [96, 2 * L], BF16)
        th = sb("th", [P, 2, L])
        xh = sb("xh", [P, 2, L])
        dtl = sb("dtl", [R, L])
        r1 = sb("r1", [96, L])
        av = sb("av", [P, H, L])
        ey = sb("ey", [P, H, L])
        rv = sb("rv", [P, H, L])
        sq = sb("sq", [P, 4, H, L])
        bt = sb("bt", [P, 2, H, L])
        hb = sb("hb", [P, 4, H, L])
        hc = sb("hc", [P, 2, H, L])
        cs = sb("cs", [P, 2, L])
        bs = sb("bs", [P, L])
        yd = sb("yd", [P, H, L])
        yg = sb("yg", [P, H, L])
        ro = sb("ro", [P, T, DM])
        st2 = sb("st2", [P, T, 6])
        mv2 = sb("mv2", [P, T, 2])
        ve2 = sb("ve2", [P, T])
        rstd2 = sb("rstd2", [P, T])
        x1 = sb("x1", [P, T, DM])

        pB = ps("pB", [P, L])
        pC = ps("pC", [P, L])
        pA = ps("pA", [P, H, L])
        pY = ps("pY", [P, H, L])
        pre = ps("pre", [P, 2, L])

        s_w = sem("weights_loaded")
        s_x = [sem(f"x_loaded{q}") for q in range(XL)]
        s_id = sem("pool_consts")
        s_gate = sem("gate_passed")
        s_z = sem("pads_zeroed")
        s_prep = sem("weights_prepared")
        s_an = sem("a_exp")
        s_aneg = sem("aneg_ready")
        s_st = sem("stats_ready")
        s_mv = sem("meanvar_ready")
        s_mean = sem("mean_ready")
        s_ve = sem("var_eps_ready")
        s_rs = sem("rstd_ready")
        s_xn = sem("xn_ready")
        s_tp = sem("xn_transposed")
        s_xT = sem("xnT_ready")
        s_pre = sem("pre_psum_ready")
        s_pact = sem("pre_read_by_act")
        s_bcr = sem("bc_residual")
        s_th = sem("silu_inputs")
        s_silu = sem("silu_ready")
        s_dtl = sem("dtl_ready")
        s_bc1 = sem("bc_first_part")
        s_bc2 = sem("bc_second_parts")
        s_bc = sem("bc_parts_ready")
        s_v = sem("dt_exps")
        s_sq = sem("dt_squares")
        s_dl = sem("delta_ready")
        s_du = sem("dtu_ready")
        s_bb = sem("b_rows_ready")
        s_cc = sem("c_rows_ready")
        s_cs = sem("c_copied")
        s_bs = sem("b_copied")
        s_pb = sem("pool_b_ready")
        s_db = sem("vector_b_ready")
        s_a = sem("a_ready")
        s_h = sem("h_ready")
        s_hc = sem("hc_ready")
        s_hu = sem("hc_summed")
        s_yd = sem("yd_ready")
        s_yg = sem("yg_ready")
        s_o = sem("out_psum_ready")
        s_r = sem("residual_ready")
        s_st2 = sem("stats2_ready")
        s_mv2 = sem("meanvar2_ready")
        s_ve2 = sem("vareps2_ready")
        s_rs2 = sem("rstd2_ready")
        s_x1 = sem("x1_ready")
        s_x1d = sem("x1_stored")

        VEC_B = [n for n in range(N) if n not in POOL_B]
        s_cbh = sem("conv_bias_halved")
        s_qa = sem("dt_poly_steps")
        NPB = len(POOL_B)
        NVB = N - NPB

        def at(buf, i, n=1, off=0, width=L):
            par = i % 2
            size = H * L
            return buf[:, bass.ds(par * size + off, width)]

        def wait(eng, s, i, per, c):
            if isinstance(i, int) and i * per + c <= 0:
                return
            eng.wait_ge(s, i * per + c)

        a_bias = [sb(f"a_bias{k}", [P, 1]) for k in range(4)]

        block = ctx.enter_context(nc.Block())

        @block.sync
        def _(sp):
            with nc.allow_non_contiguous_dma(reason="small weights"):
                for q in range(XL):
                    sp.dma_start(xall[:, q * NT // XL:(q + 1) * NT // XL, :],
                                 x[q * NS // XL:(q + 1) * NS // XL].rearrange("s (t p) d -> p (s t) d", p=P)).then_inc(s_x[q], 16)
                    if q == 0:
                        sp.dma_start(win[:], W_in).then_inc(s_w, 16)
                        sp.dma_start(cwb[:].rearrange("p c k -> p (c k)"),
                                     conv_w.rearrange("c o k -> o (c k)").broadcast_to([P, DI * KC])).then_inc(s_w, 16)
                        sp.dma_start(nw[:], norm_w.rearrange("(p o) -> p o", o=1)).then_inc(s_w, 16)
                        sp.dma_start(nb[:], norm_b.rearrange("(p o) -> p o", o=1)).then_inc(s_w, 16)
                        sp.dma_start(cb[:], conv_b.rearrange("(h p) -> p h", p=P)).then_inc(s_w, 16)
                        sp.dma_start(wx[:], W_x.rearrange("(h p) n -> p h n", p=P)).then_inc(s_w, 16)
                        sp.dma_start(wdt[:], W_dt).then_inc(s_w, 16)
                        sp.dma_start(bdt[:], b_dt.rearrange("(h p) -> p h", p=P)).then_inc(s_w, 16)
                        sp.dma_start(alog[:], A_log.rearrange("(h p) n -> p h n", p=P)).then_inc(s_w, 16)
                        sp.dma_start(dsk[:], D.rearrange("(h p) -> p h", p=P)).then_inc(s_w, 16)
                        sp.dma_start(wout[:], W_out.rearrange("(h p) n -> p h n", p=P)).then_inc(s_w, 16)
                with sp.Fori(0, NS) as s:
                    sp.wait_ge(s_x1, (s + 1) * T)
                    for g in range(GT):
                        sp.dma_start(x1_g[:, g, bass.ds(s * TT, TT), :].rearrange("t p d -> p t d"),
                                     x1[g * TT:(g + 1) * TT]).then_inc(s_x1d, 16)
            sp.wait_ge(s_x1d, 16 * GT * NS)

        NWL = 11

        @block.gpsimd
        def _(pool):
            nc.gpsimd.memset(ident[:], 0.0).then_inc(s_id, 1)
            nc.gpsimd.memset(sel[:], 0.0).then_inc(s_id, 1)
            nc.gpsimd.memset(mhalf[:], -0.5).then_inc(s_id, 1)
            nc.gpsimd.memset(xnT[:, :, 0:KC - 1], 0.0).then_inc(s_id, 1)
            pool.wait_ge(s_id, 4)
            nc.gpsimd.affine_select(out=ident[:], in_=ident[:], compare_op=ALU.not_equal, fill=1.0, base=0,
                                    pattern=[[-1, P]], channel_multiplier=1).then_inc(s_id, 1)
            for part in range(3):
                nc.gpsimd.affine_select(out=sel[:], in_=sel[:], compare_op=ALU.not_equal, fill=1.0,
                                        base=-2 * N * part, pattern=[[-1, 2 * N], [0, P]],
                                        channel_multiplier=1).then_inc(s_id, 1)
                pool.wait_ge(s_id, 6 + part)
            with pool.Fori(0, NS) as s:
                pool.wait_ge(s_ve, s + 1)
                sl = bass.ds(s * T, T)
                nc.gpsimd.tensor_tensor(rstd[:, sl], ve[:, sl], mhalf[:, sl], ALU.pow).then_inc(s_rs, 1)

            def product_b(i, n):
                k = POOL_B.index(n)
                wait(pool, s_bs, i, NPB, k + 1)
                if k == 0:
                    pool.wait_ge(s_du, i + 1)
                wait(pool, s_h, i, H * N, H * (n - 1))
                pool.sem_inc(s_gate, 1)
                nc.gpsimd.tensor_tensor(bt[:, n % 2], at(dtu, i, width=H * L).rearrange("p (h t) -> p h t", h=H),
                                        bs[:].unsqueeze(1).to_broadcast([P, H, L]), ALU.mult).then_inc(s_pb, 1)

            def product_hc(i, n):
                wait(pool, s_cs, i, N, n + 1)
                wait(pool, s_h, i, H * N, H * (n + 1))
                wait(pool, s_hu, i, N, n - 1)
                nc.gpsimd.tensor_tensor(hc[:, n % 2], hb[:, n % 4],
                                        cs[:, n % 2].unsqueeze(1).to_broadcast([P, H, L]), ALU.mult).then_inc(s_hc, 1)

            def body(i, first=False, last=False):
                for n in range(N):
                    if n in POOL_B:
                        product_b(i, n)
                    if n >= 1:
                        product_hc(i, n - 1)
                    elif not first:
                        product_hc(i - 1, N - 1)
                    if n == 5 and not first:
                        gate(i - 1)
                    if n == 12 and not first:
                        rstd_out(i - 1)
                    if n == 14 and not last:
                        times_u(i + 1)
                if last:
                    product_hc(i, N - 1)

            def gate(i):
                pool.wait_ge(s_silu, 4 * i + 4)
                pool.wait_ge(s_yd, H * (i + 1))
                wait(pool, s_o, i, 1, 0)
                nc.gpsimd.tensor_tensor(yg[:].rearrange("p h t -> p (h t)"), yd[:].rearrange("p h t -> p (h t)"),
                                        at(zs, i, width=H * L), ALU.mult).then_inc(s_yg, 1)

            def rstd_out(i):
                pool.wait_ge(s_ve2, i + 1)
                nc.gpsimd.tensor_tensor(rstd2[:], ve2[:], mhalf[:, 0:T], ALU.pow).then_inc(s_rs2, 1)

            def times_u(i):
                pool.wait_ge(s_dl, i + 1)
                pool.wait_ge(s_silu, 4 * i + 2)
                nc.gpsimd.tensor_tensor(at(dtu, i, width=H * L), at(delta, i, width=H * L), at(u, i, width=H * L),
                                        ALU.mult).then_inc(s_du, 1)

            times_u(0)
            body(0, first=True)
            with pool.Fori(1, NS - 1) as i:
                body(i)
            body(NS - 1, last=True)
            gate(NS - 1)
            rstd_out(NS - 1)

        @block.scalar
        def _(act):
            nc.scalar.preload_act_table_set("exp_and_others")
            act.wait_ge(s_w, 16 * NWL)
            nc.scalar.activation(aneg[:], alog[:], ACT.Exp).then_inc(s_an, 1)
            nc.scalar.mul(cbh[:], cb[:], 0.5).then_inc(s_cbh, 1)
            act.wait_ge(s_an, 1)
            nc.scalar.mul(aneg[:], aneg[:], -1.0).then_inc(s_aneg, 1)
            act.wait_ge(s_aneg, 1)
            act.wait_ge(s_cbh, 1)
            act.wait_ge(s_id, 4)
            act.wait_ge(s_z, 4)
            with act.Fori(0, NS // 2) as s2:
                for k in range(2):
                    s = 2 * s2 + k
                    act.wait_ge(s_tp, T * (s + 1))
                    nc.scalar.activation(xnT[:, bass.ds(s, 1), KC - 1:LP].rearrange("p o t -> p (o t)"), pre[:, k],
                                         ACT.Identity, bias=nb[:, 0:1], scale=nw[:, 0:1]).then_inc(s_xT, 1)

            def silu_in(i, m):
                act.wait_ge(s_pre, 8 * i + (m + 1 if m < 2 else m + 5))
                wait(act, s_silu, i, 4, m - 1)
                if m < 2:
                    nc.scalar.activation(th[:, m % 2], pre[:, m % 2], ACT.Tanh, bias=cbh[:, m:m + 1],
                                         scale=0.5).then_inc(s_th, 1)
                    nc.scalar.activation(xh[:, m % 2], pre[:, m % 2], ACT.Identity, bias=cbh[:, m:m + 1],
                                         scale=0.5).then_inc(s_pact, 1)
                else:
                    nc.scalar.activation(th[:, m % 2], pre[:, m % 2], ACT.Tanh, scale=0.5).then_inc(s_th, 1)
                    nc.scalar.mul(xh[:, m % 2], pre[:, m % 2], 0.5).then_inc(s_pact, 1)

            def dt_low_copy(i):
                act.wait_ge(s_pre, 8 * i + 3)
                wait(act, s_pre, i, 8, -2)
                nc.scalar.copy(dtl[:], pre[0:R, 0]).then_inc(s_pact, 1)

            def bc_parts(i):
                act.wait_ge(s_pre, 8 * i + 4)
                here = bass.ds((i % 2) * L, L)
                nc.scalar.copy(bcs[:, here], pre[0:96, 1]).then_inc(s_bc1, 1)
                act.wait_ge(s_bcr, i + 1)
                for q in (1, 2):
                    nc.scalar.copy(bcs[32 * q:32 * q + 32, here], r1[32 * q:32 * q + 32]).then_inc(s_bc2, 1)

            def dt_exps(i, h):
                act.wait_ge(s_pre, 8 * i + 5 + h)
                wait(act, s_dl, i, 1, 0)
                b = bdt[:, h:h + 1]
                nc.scalar.activation(av[:, h], pre[:, h], ACT.Abs, bias=b).then_inc(s_v, 1)
                nc.scalar.activation(rv[:, h], pre[:, h], ACT.Relu, bias=b).then_inc(s_pact, 1)
                act.wait_ge(s_v, 4 * i + 2 * h + 1)
                nc.scalar.activation(ey[:, h], av[:, h], ACT.Exp, scale=-1.0).then_inc(s_v, 1)

            def dt_square(i, k):
                act.wait_ge(s_v, 4 * i + 4)
                wait(act, s_dl, i, 1, 0)
                nc.scalar.activation(sq[:, k], ey[:], ACT.Square, bias=a_bias[k][:, 0:1]).then_inc(s_sq, 1)

            def state(i, n):
                act.wait_ge(s_dl, i + 1)
                for h in range(H):
                    wait(act, s_h, i, H * N, H * (n - 1) + h + 1)
                    act.sem_inc(s_gate, 1)
                    nc.scalar.activation(pA[:, h], at(delta, i, off=h * L), ACT.Exp,
                                         scale=aneg[:, h, n:n + 1]).then_inc(s_a, 1)
                wait(act, s_cc, i, N, n + 1)
                wait(act, s_hc, i, N, n - 1)
                nc.scalar.copy(cs[:, n % 2], pC[:]).then_inc(s_cs, 1)
                if n + 1 in POOL_B:
                    k = POOL_B.index(n + 1)
                    wait(act, s_bb, i, N, n + 2)
                    wait(act, s_pb, i, NPB, k)
                    nc.scalar.copy(bs[:], pB[:]).then_inc(s_bs, 1)

            def body(i, last=False):
                for n in range(N):
                    state(i, n)
                    if last:
                        continue
                    if n in (2, 4):
                        silu_in(i + 1, n // 2 - 1)
                    if n == 6:
                        dt_low_copy(i + 1)
                    if n == 7:
                        bc_parts(i + 1)
                    if n in (8, 9):
                        dt_exps(i + 1, n - 8)
                    if n in (10, 11):
                        dt_square(i + 1, 2 * (n - 10))
                        dt_square(i + 1, 2 * (n - 10) + 1)
                    if n in (12, 13):
                        silu_in(i + 1, n - 10)

            for m in range(2):
                silu_in(0, m)
            dt_low_copy(0)
            bc_parts(0)
            for h in range(H):
                dt_exps(0, h)
            for k in range(4):
                dt_square(0, k)
            for m in range(2, 4):
                silu_in(0, m)
            body(0)
            with act.Fori(1, NS - 1) as i:
                body(i)
            body(NS - 1, last=True)

        @block.vector
        def _(dve):
            for k in range(4):
                nc.vector.memset(a_bias[k][:], quad[k][0]).then_inc(s_z, 1)

            def token_stats(s):
                for t in range(T):
                    nc.vector.bn_stats(stats[:, t], xall[:, bass.ds(s * T + t, 1)].rearrange("p o d -> p (o d)")).then_inc(s_st, 1)
                dve.wait_ge(s_st, T * s + T)
                dve.sem_inc(s_gate, 1)
                for t in range(T):
                    nc.vector.bn_aggr(mv[:, t], stats[:, t]).then_inc(s_mv, 1)
                dve.wait_ge(s_mv, T * s + T)
                nc.vector.tensor_copy(mean[:, bass.ds(s * T, T)], mv[:, :, 0]).then_inc(s_mean, 1)
                nc.vector.tensor_scalar(ve[:, bass.ds(s * T, T)], mv[:, :, 1], EPS, None, ALU.add).then_inc(s_ve, 1)

            for q in range(XL):
                dve.wait_ge(s_x[q], 16)
                with dve.Fori(q * NS // XL, (q + 1) * NS // XL) as s:
                    token_stats(s)
            dve.wait_ge(s_w, 16 * NWL)
            for k in range(KC):
                nc.vector.tensor_tensor(wtap[:, k], win[:, 0:DI], cwb[:, :, k], ALU.mult).then_inc(s_prep, 1)
            for j in range(3):
                nc.vector.tensor_copy(wbc[:, :, j], wx[:, :, R:R + 2 * N]).then_inc(s_prep, 1)

            def normalise(s, k):
                dve.wait_ge(s_rs, s + 1)
                dve.wait_ge(s_mean, s + 1)
                wait(dve, s_tp, s, T, -T)
                for t in range(T):
                    g = bass.ds(s * T + t, 1)
                    nc.vector.tensor_scalar(xn[:, k, t], xall[:, g].rearrange("p o d -> p (o d)"),
                                            mean[:, g], rstd[:, g], ALU.subtract, ALU.mult).then_inc(s_xn, 1)

            for k in range(2):
                normalise(k, k)
            with dve.Fori(1, NS // 2) as s2:
                for k in range(2):
                    normalise(2 * s2 + k, k)

            def silu(i, m):
                dve.wait_ge(s_th, 4 * i + m + 1)
                dve.wait_ge(s_pact, 7 * i + (m + 1 if m < 2 else m + 4))
                if m >= 2:
                    wait(dve, s_yg, i, 1, -1)
                else:
                    wait(dve, s_yd, i, H, -H)
                dst = at(u if m < 2 else zs, i, off=(m % 2) * L)
                nc.vector.scalar_tensor_tensor(dst, th[:, m % 2], 1.0, xh[:, m % 2], ALU.add,
                                               ALU.mult).then_inc(s_silu, 1)

            def bc_residual(i):
                dve.wait_ge(s_bc1, i + 1)
                wait(dve, s_bc, i, 1, 0)
                nc.vector.tensor_tensor(r1[:], pre[0:96, 1], bcs[:, bass.ds((i % 2) * L, L)],
                                        ALU.subtract).then_inc(s_bcr, 1)

            def bc_last(i):
                dve.wait_ge(s_bc2, 2 * i + 2)
                here = bass.ds((i % 2) * L, L)
                nc.vector.tensor_tensor(bcs[64:96, here], r1[64:96], bcs[64:96, here], ALU.subtract).then_inc(s_bc, 1)

            def dt_poly(i, k):
                dve.wait_ge(s_sq, 4 * i + k + 1)
                if k:
                    dve.wait_ge(s_qa, 4 * i + k)
                nc.vector.scalar_tensor_tensor(sq[:, k], sq[:, k], quad[k][1], ey[:] if k == 0 else sq[:, k - 1],
                                               ALU.add, ALU.mult).then_inc(s_qa, 1)
                if k == 3:
                    dve.wait_ge(s_qa, 4 * i + 4)
                    dve.wait_ge(s_pact, 7 * i + 5)
                    nc.vector.scalar_tensor_tensor(at(delta, i, width=H * L), sq[:, 3].rearrange("p h t -> p (h t)"),
                                                   lead, rv[:].rearrange("p h t -> p (h t)"), ALU.mult,
                                                   ALU.add).then_inc(s_dl, 1)

            def y_skip(i):
                dve.wait_ge(s_hu, N * (i + 1))
                wait(dve, s_yg, i, 1, 0)
                for h in range(H):
                    nc.vector.scalar_tensor_tensor(yd[:, h], at(u, i, off=h * L), dsk[:, h:h + 1], pY[:, h],
                                                   ALU.mult, ALU.add).then_inc(s_yd, 1)

            def residual(i):
                dve.wait_ge(s_o, i + 1)
                nc.vector.scalar_tensor_tensor(ro[:].rearrange("p t d -> p (t d)"),
                                               xall[:, bass.ds(i * T, T)].rearrange("p t d -> p (t d)"), 2.0, pre[:, 0],
                                               ALU.mult, ALU.add).then_inc(s_r, 1)
                dve.wait_ge(s_r, i + 1)
                for t in range(T):
                    nc.vector.bn_stats(st2[:, t], ro[:, t]).then_inc(s_st2, 1)
                dve.wait_ge(s_st2, T * (i + 1))
                dve.sem_inc(s_gate, 1)
                for t in range(T):
                    nc.vector.bn_aggr(mv2[:, t], st2[:, t]).then_inc(s_mv2, 1)
                dve.wait_ge(s_mv2, T * (i + 1))
                nc.vector.tensor_scalar(ve2[:], mv2[:, :, 1], EPS, None, ALU.add).then_inc(s_ve2, 1)

            def normalise_out(i):
                dve.wait_ge(s_rs2, i + 1)
                wait(dve, s_x1d, i, 16 * GT, 0)
                for t in range(T):
                    nc.vector.tensor_scalar(x1[:, t], ro[:, t], mv2[:, t, 0:1], rstd2[:, t:t + 1], ALU.subtract,
                                            ALU.mult).then_inc(s_x1, 1)

            def state(i, n):
                if n not in POOL_B:
                    k = VEC_B.index(n)
                    dve.wait_ge(s_bb, N * i + n + 1)
                    if k == 0:
                        dve.wait_ge(s_du, i + 1)
                    nc.vector.tensor_tensor(bt[:, n % 2], at(dtu, i, width=H * L).rearrange("p (h t) -> p h t", h=H),
                                            pB[:].unsqueeze(1).to_broadcast([P, H, L]), ALU.mult).then_inc(s_db, 1)
                    dve.wait_ge(s_db, NVB * i + k + 1)
                else:
                    dve.wait_ge(s_pb, NPB * i + POOL_B.index(n) + 1)
                wait(dve, s_hc, i, N, n - 3)
                for h in range(H):
                    dve.wait_ge(s_a, H * N * i + H * n + h + 1)
                    nc.vector.tensor_tensor_scan(hb[:, n % 4, h], pA[:, h], bt[:, n % 2, h], 0.0, ALU.mult,
                                                 ALU.add).then_inc(s_h, 1)

            def body(i, first=False, last=False):
                for n in range(N):
                    state(i, n)
                    if not first:
                        if n == 2:
                            y_skip(i - 1)
                        if n == 10:
                            residual(i - 1)
                        if n == 12:
                            normalise_out(i - 1)
                    if not last:
                        if n in (3, 5):
                            silu(i + 1, (n - 3) // 2)
                        if n == 7:
                            bc_residual(i + 1)
                        if n == 8:
                            bc_last(i + 1)
                        if n in (11, 12):
                            dt_poly(i + 1, 2 * (n - 11))
                            dt_poly(i + 1, 2 * (n - 11) + 1)
                        if n in (13, 14):
                            silu(i + 1, n - 11)

            silu(0, 0)
            silu(0, 1)
            bc_residual(0)
            bc_last(0)
            for k in range(4):
                dt_poly(0, k)
            silu(0, 2)
            silu(0, 3)
            body(0, first=True)
            with dve.Fori(1, NS - 1) as i:
                body(i)
            body(NS - 1, last=True)
            y_skip(NS - 1)
            residual(NS - 1)
            normalise_out(NS - 1)

        @block.tensor
        def _(pe):
            pe.wait_ge(s_id, 8)

            def transposes(s, k):
                wait(pe, s_xT, s, 1, -1)
                for t in range(T):
                    pe.wait_ge(s_xn, T * s + t + 1)
                    nc.tensor.transpose(pre[:, k, t * P:(t + 1) * P], xn[:, k, t], ident[:]).then_inc(s_tp, 1)

            for k in range(2):
                transposes(k, k)
            with pe.Fori(1, NS // 2) as s2:
                for k in range(2):
                    transposes(2 * s2 + k, k)
            pe.wait_ge(s_xT, NS)
            pe.wait_ge(s_prep, KC + 3)

            def tokens(i, k=0):
                return xnT[:, bass.ds(i, 1), k:k + L].rearrange("p o t -> p (o t)")

            def conv(i, h, taps):
                if 0 in taps:
                    wait(pe, s_pact, i, 7, h - 1)
                for k in taps:
                    mm = nc.tensor.matmul(pre[:, h], wtap[:, k, h * P:(h + 1) * P], tokens(i, k), start=(k == 0),
                                          stop=(k == KC - 1))
                if KC - 1 in taps:
                    mm.then_inc(s_pre, 1)

            def x_proj(i, bank):
                pe.wait_ge(s_silu, 4 * i + 2)
                pe.wait_ge(s_pact, 7 * i + 1 + bank)
                for h in range(H):
                    rows_of, w = (R, wx[:, h, 0:R]) if bank == 0 else (96, wbc[:, h].rearrange("p j n -> p (j n)"))
                    mm = nc.tensor.matmul(pre[0:rows_of, bank], w, at(u, i, off=h * L), start=(h == 0),
                                          stop=(h == H - 1))
                mm.then_inc(s_pre, 1)

            def dt_proj(i, h):
                pe.wait_ge(s_pact, 7 * i + 3)
                if h == 1:
                    pe.wait_ge(s_bcr, i + 1)
                nc.tensor.matmul(pre[:, h], wdt[:, h * P:(h + 1) * P], dtl[:], start=True, stop=True).then_inc(s_pre, 1)

            def z_proj(i, h):
                if h == 0:
                    wait(pe, s_r, i, 1, -1)
                pe.wait_ge(s_pact, 7 * i + 4 + h)
                nc.tensor.matmul(pre[:, h], win[:, DI + h * P:DI + (h + 1) * P], tokens(i, KC - 1), start=True,
                                 stop=True).then_inc(s_pre, 1)

            def out_proj(i, free):
                pe.wait_ge(s_yg, i + 1)
                pe.wait_ge(*free)
                for t in range(T):
                    for h in range(H):
                        mm = nc.tensor.matmul(pre[:, 0, t * P:(t + 1) * P], yg[:, h, t * P:(t + 1) * P], wout[:, h],
                                              start=(h == 0), stop=(h == H - 1))
                mm.then_inc(s_o, 1)

            def rows(i, n):
                here = bass.ds((i % 2) * L, L)
                if n == 0:
                    pe.wait_ge(s_bc, i + 1)
                m = (n - 1) % N
                j = i if n else i - 1
                if not (isinstance(j, int) and j < 0):
                    if m in POOL_B:
                        pe.wait_ge(s_bs, NPB * j + POOL_B.index(m) + 1)
                    else:
                        pe.wait_ge(s_db, NVB * j + VEC_B.index(m) + 1)
                nc.tensor.matmul(pB[:], sel[:, n], bcs[:, here], start=True, stop=True).then_inc(s_bb, 1)
                wait(pe, s_cs, i, N, n)
                nc.tensor.matmul(pC[:], sel[:, N + n], bcs[:, here], start=True, stop=True).then_inc(s_cc, 1)

            def sum_states(i, n):
                pe.wait_ge(s_hc, N * i + n + 1)
                if n == 0:
                    wait(pe, s_yd, i, H, 0)
                for h in range(H):
                    mm = nc.tensor.matmul(pY[:, h], ident[:], hc[:, n % 2, h], start=(n == 0), stop=(n == N - 1))
                mm.then_inc(s_hu, 1)

            def body(i, first=False, last=False):
                for n in range(N):
                    if n < N - 1:
                        rows(i, n + 1)
                    elif not last:
                        rows(i + 1, 0)
                    if n >= LAG:
                        sum_states(i, n - LAG)
                    elif not first:
                        sum_states(i - 1, N + n - LAG)
                    if not last:
                        if n < 4:
                            conv(i + 1, n // 2, range(KC // 2) if n % 2 == 0 else range(KC // 2, KC))
                        if n in (5, 6):
                            x_proj(i + 1, n - 5)
                        if n in (7, 8):
                            dt_proj(i + 1, n - 7)
                    if n == 9 and not first:
                        out_proj(i - 1, (s_pact, 7 * (i + 1) + 4) if not last else (s_pact, 7 * NS))
                    if n in (11, 12) and not last:
                        z_proj(i + 1, n - 11)

            for h in range(H):
                conv(0, h, range(KC))
            for h in range(2):
                x_proj(0, h)
            for h in range(H):
                dt_proj(0, h)
            for h in range(H):
                z_proj(0, h)
            rows(0, 0)
            body(0, first=True)
            with pe.Fori(1, NS - 1) as i:
                body(i)
            body(NS - 1, last=True)
            for n in range(N - LAG, N):
                sum_states(NS - 1, n)
            out_proj(NS - 1, (s_r, NS - 1))

I32 = mybir.dt.int32
U32 = mybir.dt.uint32
BIG = 2.0 ** 100


def wait_if(eng, s, i, per, c):
    if isinstance(i, int) and i * per + c <= 0:
        return
    eng.wait_ge(s, i * per + c)


def build_attention(nc, shared, x1_d, Wqkv, bqkv, Wo, bo, g1, be1, g2, be2, Wg, W1, b1, W2, b2, y_d):
    NG = x1_d.shape[0]
    DM = x1_d.shape[2]
    E = Wg.shape[0]
    G = 4
    NQ = NG // G
    S = 8
    TT = P // S
    HD = 32
    NH = DM // HD
    SCALE = 1.0 / float(np.sqrt(HD))
    T = G * P
    yall, lg = shared["yall"], shared["lg"]

    with ExitStack() as ctx:
        def sb(name, shape, dt=F32):
            return ctx.enter_context(nc.sbuf_tensor(name, shape, dt))

        def ps(name, shape, dt=F32):
            return ctx.enter_context(nc.psum_tensor(name, shape, dt))

        def sem(name):
            return ctx.enter_context(nc.semaphore(name))

        s_gate = sem("a_gate_passed")
        ident = sb("a_ident", [P, P])
        identb = sb("a_identb", [P, P], BF16)
        mask = sb("a_mask", [P, G, P], BF16)
        mhalf = sb("a_mhalf", [P, G])
        wnat = sb("a_wnat", [P, 4, DM])
        wgn = sb("a_wgn", [E, DM])
        wT = sb("a_wT", [P, 4, DM])
        wgT = sb("a_wgT", [P, E])
        bq = sb("a_bq", [P, 3])
        bqs = sb("a_bqs", [P, 1])
        bor = sb("a_bor", [1, DM])
        cst = sb("a_cst", [1, DM])
        ones = sb("a_ones", [1, P])
        g1b = sb("a_g1b", [P, DM])
        be1b = sb("a_be1b", [P, DM])
        xg = sb("a_xg", [P, 2, G, DM])
        xT = sb("a_xT", [P, T])
        qT = sb("a_qT", [P, T])
        kT = sb("a_kT", [P, T])
        v = sb("a_v", [P, G, NH, HD + 1])
        mx = sb("a_mx", [P, NH * G])
        sh = sb("a_sh", [P, NH * G, P])
        pr = sb("a_pr", [P, NH * G, P])
        prT = sb("a_prT", [P, NH * G, P])
        rin = sb("a_rin", [P, G * NH])
        on = sb("a_on", [P, G, DM])
        oT = sb("a_oT", [P, T])
        ro = sb("a_ro", [P, G, DM])
        st = sb("a_st", [P, G, 6])
        mv = sb("a_mv", [P, G, 2])
        ve = sb("a_ve", [P, G])
        rs = sb("a_rs", [P, G])
        yn = sb("a_yn", [P, G, DM])
        ym = sb("a_ym", [P, G, DM])
        yq = sb("a_yq", [P, G, DM])
        yT = sb("a_yT", [P, T])

        pS = ps("a_pS", [P, NH, G * P])
        pA = ps("a_pA", [P, T])
        pV = ps("a_pV", [P, T])
        pO = ps("a_pO", [P, 2, 512])

        s_w = sem("a_weights")
        s_mk = sem("a_masks")
        s_dc = sem("a_dve_consts")
        s_wt = sem("a_w_transposed")
        s_wc = sem("a_w_copied")
        s_cp = sem("a_const_psum")
        s_cc = sem("a_const_ready")
        s_xg = sem("a_x_loaded")
        s_pa = sem("a_pa_ready")
        s_par = sem("a_pa_read_by_act")
        s_out = sem("a_out_read")
        s_pv = sem("a_pv_ready")
        s_pvr = sem("a_pv_read")
        s_sc = sem("a_scores_ready")
        s_mx = sem("a_max_ready")
        s_sh = sem("a_shifted")
        s_ex = sem("a_exp_ready")
        s_pt = sem("a_probs_transposed")
        s_ptc = sem("a_probsT_copied")
        s_ptd = sem("a_probsT_copied_dve")
        s_o = sem("a_o_ready")
        s_rin = sem("a_recip_ready")
        s_on = sem("a_o_normalised")
        s_st = sem("a_stats")
        s_mv = sem("a_meanvar")
        s_ve = sem("a_vareps")
        s_rs = sem("a_rstd")
        s_yn = sem("a_normalised")
        s_ym = sem("a_scaled")
        s_y = sem("a_y_ready")
        s_ya = sem("a_y_kept")
        s_xg2 = [s_xg, sem("a_x_loaded1")]
        s_nw = 7

        block = ctx.enter_context(nc.Block())

        @block.sync
        def _(sp):
            with nc.allow_non_contiguous_dma(reason="small weights"):
                sp.dma_start(wnat[:, 0:3, :], Wqkv.rearrange("(j p) d -> p j d", p=P)).then_inc(s_w, 16)
                sp.dma_start(wnat[:, 3, :], Wo).then_inc(s_w, 16)
                sp.dma_start(wgn[:], Wg).then_inc(s_w, 16)
                sp.dma_start(bq[:], bqkv.rearrange("(j p) -> p j", p=P)).then_inc(s_w, 16)
                sp.dma_start(bor[:], bo.rearrange("(o d) -> o d", o=1)).then_inc(s_w, 16)
                sp.dma_start(g1b[:], g1.rearrange("(o d) -> o d", o=1).broadcast_to([P, DM])).then_inc(s_w, 16)
                sp.dma_start(be1b[:], be1.rearrange("(o d) -> o d", o=1).broadcast_to([P, DM])).then_inc(s_w, 16)

            def load(q, k):
                wait_if(sp, s_ya, q, 1, -1)
                sp.dma_start(xg[:, k], x1_d[bass.ds(q * G, G)].rearrange("g p d -> p g d")).then_inc(s_xg2[k], 16)

            for k in range(2):
                load(k, k)
            with sp.Fori(1, NQ // 2) as q2:
                for k in range(2):
                    load(2 * q2 + k, k)

        @block.gpsimd
        def _(pool):
            nc.gpsimd.memset(ident[:], 0.0).then_inc(s_mk, 1)
            nc.gpsimd.memset(mask[:], -BIG).then_inc(s_mk, 1)
            nc.gpsimd.memset(mhalf[:], -0.5).then_inc(s_mk, 1)
            nc.gpsimd.memset(ones[:], 1.0).then_inc(s_mk, 1)
            nc.gpsimd.memset(v[:, :, :, HD:HD + 1], 1.0).then_inc(s_mk, 1)
            pool.wait_ge(s_mk, 5)
            nc.gpsimd.affine_select(out=ident[:], in_=ident[:], compare_op=ALU.not_equal, fill=1.0, base=0,
                                    pattern=[[-1, P]], channel_multiplier=1).then_inc(s_mk, 1)
            pool.wait_ge(s_mk, 6)
            nc.gpsimd.tensor_copy(identb[:], ident[:]).then_inc(s_mk, 1)
            for d in range(-(S - 1), S):
                nc.gpsimd.affine_select(out=mask[:], in_=mask[:], compare_op=ALU.not_equal, fill=0.0, base=TT * d,
                                        pattern=[[0, G], [-1, P]], channel_multiplier=1).then_inc(s_mk, 1)
                pool.wait_ge(s_mk, 8 + d + S - 1)

            def norm(q):
                pool.wait_ge(s_ve, q + 1)
                nc.gpsimd.tensor_tensor(rs[:], ve[:], mhalf[:], ALU.pow).then_inc(s_rs, 1)
                pool.wait_ge(s_yn, G * (q + 1))
                nc.gpsimd.tensor_tensor(ym[:], yn[:], g1b[:].unsqueeze(1).to_broadcast([P, G, DM]),
                                        ALU.mult).then_inc(s_ym, 1)
                pool.wait_ge(s_ym, q + 1)
                wait_if(pool, s_pa, q, 6, 0)
                wait_if(pool, s_ya, q, 1, 0)
                nc.gpsimd.tensor_tensor(yq[:], ym[:], be1b[:].unsqueeze(1).to_broadcast([P, G, DM]),
                                        ALU.add).then_inc(s_y, 1)

            norm(0)
            with pool.Fori(1, NQ) as q:
                norm(q)

        NMK = 7 + 2 * S - 1

        @block.scalar
        def _(act):
            act.wait_ge(s_w, 16 * s_nw)
            nc.scalar.mul(bqs[:], bq[:, 0:1], SCALE).then_inc(s_cc, 1)
            act.wait_ge(s_wt, 4)
            nc.scalar.copy(wT[:].rearrange("p j d -> p (j d)"), pA[:]).then_inc(s_wc, 1)
            act.wait_ge(s_wt, 5)
            nc.scalar.copy(wgT[:], pV[:, 0:E]).then_inc(s_wc, 1)
            act.wait_ge(s_cc, 1)

            def quad(q, k):
                act.wait_ge(s_pa, 6 * q + 1)
                nc.scalar.copy(xT[:], pA[:]).then_inc(s_par, 1)
                act.wait_ge(s_pa, 6 * q + 2)
                nc.scalar.activation(qT[:], pA[:], ACT.Identity, bias=bqs[:, 0:1], scale=SCALE).then_inc(s_par, 1)
                act.wait_ge(s_pa, 6 * q + 3)
                nc.scalar.activation(kT[:], pA[:], ACT.Identity, bias=bq[:, 1:2]).then_inc(s_par, 1)
                act.wait_ge(s_sh, q + 1)
                wait_if(act, s_pt, q, 1, 0)
                nc.scalar.activation(pr[:], sh[:], ACT.Exp).then_inc(s_ex, 1)
                act.wait_ge(s_pt, q + 1)
                wait_if(act, s_o, q, 1, 0)
                nc.scalar.copy(prT[:, 0:2 * G], pS[:, 0:2].rearrange("p h (g k) -> p (h g) k", g=G)).then_inc(s_ptc, 1)
                act.wait_ge(s_pa, 6 * q + 4)
                nc.scalar.copy(oT[:], pA[:]).then_inc(s_par, 1)
                act.wait_ge(s_y, q + 1)
                nc.scalar.copy(yall[:, bass.ds(q * G, G)], yq[:]).then_inc(s_ya, 1)
                act.wait_ge(s_pa, 6 * q + 6)
                nc.scalar.copy(yT[:], pA[:]).then_inc(s_par, 1)

            quad(0, 0)
            with act.Fori(1, NQ) as q:
                quad(q, 0)

        @block.vector
        def _(dve):
            dve.wait_ge(s_cp, 1)
            nc.vector.tensor_tensor(cst[:], pV[0:1, 256:256 + DM], bor[:], ALU.add).then_inc(s_cc, 1)

            def quad(q):
                dve.wait_ge(s_pv, 2 * q + 1)
                wait_if(dve, s_o, q, 1, 0)
                nc.vector.tensor_copy(v[:, :, :, 0:HD], pV[:].rearrange("p (g h d) -> p g h d", g=G, h=NH)).then_inc(s_pvr, 1)
                dve.wait_ge(s_sc, q + 1)
                view = pS[:].rearrange("p h (g k) -> p (h g) k", g=G)
                nc.vector.tensor_reduce(mx[:], view, AX.X, ALU.max).then_inc(s_mx, 1)
                dve.wait_ge(s_mx, q + 1)
                wait_if(dve, s_ex, q, 1, 0)
                nc.vector.tensor_tensor(sh[:], view, mx[:].unsqueeze(2).to_broadcast([P, NH * G, P]),
                                        ALU.subtract).then_inc(s_sh, 1)
                dve.wait_ge(s_pt, q + 1)
                nc.vector.tensor_copy(prT[:, 2 * G:4 * G], pS[:, 2:4].rearrange("p h (g k) -> p (h g) k", g=G)).then_inc(s_ptd, 1)
                dve.wait_ge(s_o, q + 1)
                for j in range(2):
                    o3 = pO[:, j, 0:2 * NH * (HD + 1)].rearrange("p (g d) -> p g d", d=HD + 1)
                    nc.vector.reciprocal(rin[:, 2 * NH * j:2 * NH * (j + 1)], o3[:, :, HD]).then_inc(s_rin, 1)
                dve.wait_ge(s_rin, 2 * q + 2)
                for j in range(2):
                    o3 = pO[:, j, 0:2 * NH * (HD + 1)].rearrange("p (g d) -> p g d", d=HD + 1)
                    nc.vector.tensor_tensor(on[:, 2 * j:2 * j + 2].rearrange("p g (h d) -> p (g h) d", h=NH), o3[:, :, 0:HD],
                                            rin[:, 2 * NH * j:2 * NH * (j + 1)].unsqueeze(2).to_broadcast([P, 2 * NH, HD]),
                                            ALU.mult).then_inc(s_on, 1)
                dve.wait_ge(s_pa, 6 * q + 5)

            def after(q, k):
                nc.vector.tensor_tensor(ro[:].rearrange("p g d -> p (g d)"), pA[:], xg[:, k].rearrange("p g d -> p (g d)"),
                                        ALU.add).then_inc(s_out, 1)
                dve.wait_ge(s_out, q + 1)
                for t in range(G):
                    nc.vector.bn_stats(st[:, t], ro[:, t]).then_inc(s_st, 1)
                dve.wait_ge(s_st, G * (q + 1))
                dve.sem_inc(s_gate, 1)
                for t in range(G):
                    nc.vector.bn_aggr(mv[:, t], st[:, t]).then_inc(s_mv, 1)
                dve.wait_ge(s_mv, G * (q + 1))
                nc.vector.tensor_scalar(ve[:], mv[:, :, 1], EPS, None, ALU.add).then_inc(s_ve, 1)
                dve.wait_ge(s_rs, q + 1)
                wait_if(dve, s_ym, q, 1, 0)
                for t in range(G):
                    nc.vector.tensor_scalar(yn[:, t], ro[:, t], mv[:, t, 0:1], rs[:, t:t + 1], ALU.subtract,
                                            ALU.mult).then_inc(s_yn, 1)
                dve.wait_ge(s_pv, 2 * q + 2)
                nc.vector.tensor_copy(lg[:, bass.ds(q * G, G)], pV[:, 0:G * E].rearrange("p (g e) -> p g e", g=G)).then_inc(s_pvr, 1)

            for k in range(2):
                dve.wait_ge(s_xg2[k], 16)
                quad(k)
                after(k, k)
            with dve.Fori(1, NQ // 2) as q2:
                for k in range(2):
                    dve.wait_ge(s_xg2[k], 16 * q2 + 16)
                    quad(2 * q2 + k)
                    after(2 * q2 + k, k)

        @block.tensor
        def _(pe):
            pe.wait_ge(s_w, 16 * s_nw)
            pe.wait_ge(s_mk, NMK)
            for j in range(4):
                nc.tensor.transpose(pA[:, j * P:(j + 1) * P], wnat[:, j], ident[:]).then_inc(s_wt, 1)
            nc.tensor.transpose(pV[:, 0:E], wgn[:], ident[0:E, 0:E]).then_inc(s_wt, 1)
            pe.wait_ge(s_wc, 2)
            nc.tensor.matmul(pV[0:1, 256:256 + DM], bq[:, 2:3], wT[:, 3], start=True, stop=True).then_inc(s_cp, 1)
            pe.wait_ge(s_cc, 2)

            def quad(q, k, q2):
                pe.wait_ge(s_xg2[k], 16 * q2 + 16)
                wait_if(pe, s_par, q, 5, 0)
                for g in range(G):
                    mm = nc.tensor.transpose(pA[:, g * P:(g + 1) * P], xg[:, k, g], ident[:])
                mm.then_inc(s_pa, 1)
                pe.wait_ge(s_par, 5 * q + 1)
                nc.tensor.matmul(pA[:], wT[:, 0], xT[:], start=True, stop=True).then_inc(s_pa, 1)
                wait_if(pe, s_pvr, q, 2, 0)
                for g in range(G):
                    mm = nc.tensor.matmul(pV[:, g * P:(g + 1) * P], xT[:, g * P:(g + 1) * P], wT[:, 2], start=True, stop=True)
                mm.then_inc(s_pv, 1)
                pe.wait_ge(s_par, 5 * q + 2)
                nc.tensor.matmul(pA[:], wT[:, 1], xT[:], start=True, stop=True).then_inc(s_pa, 1)
                wait_if(pe, s_ptc, q, 1, 0)
                wait_if(pe, s_ptd, q, 1, 0)
                for h in range(NH):
                    nc.tensor.matmul(pS[:, h], identb[:], mask[:].rearrange("p g k -> p (g k)"), start=True, stop=False,
                                     skip_group_check=True)
                pe.wait_ge(s_par, 5 * q + 3)
                for g in range(G):
                    for h in range(NH):
                        c = slice(g * P, (g + 1) * P)
                        hh = slice(h * HD, (h + 1) * HD)
                        mm = nc.tensor.matmul(pS[:, h, c], qT[hh, c], kT[hh, c], start=False, stop=(g == G - 1),
                                              skip_group_check=True, tile_position=(h * HD, 0))
                mm.then_inc(s_sc, 1)
                pe.wait_ge(s_ex, q + 1)
                for h in range(NH):
                    for g in range(G):
                        mm = nc.tensor.transpose(pS[:, h, g * P:(g + 1) * P], pr[:, h * G + g], ident[:])
                mm.then_inc(s_pt, 1)
                pe.wait_ge(s_ptc, q + 1)
                pe.wait_ge(s_ptd, q + 1)
                pe.wait_ge(s_pvr, 2 * q + 1)
                wait_if(pe, s_on, q, 2, 0)
                for g in range(G):
                    for h in range(NH):
                        c = ((g % 2) * NH + h) * (HD + 1)
                        mm = nc.tensor.matmul(pO[:, g // 2, c:c + HD + 1], prT[:, h * G + g], v[:, g, h], start=True,
                                              stop=True)
                mm.then_inc(s_o, 1)
                pe.wait_ge(s_on, 2 * q + 2)
                for g in range(G):
                    mm = nc.tensor.transpose(pA[:, g * P:(g + 1) * P], on[:, g], ident[:])
                mm.then_inc(s_pa, 1)
                pe.wait_ge(s_par, 5 * q + 4)
                for g in range(G):
                    c = slice(g * P, (g + 1) * P)
                    nc.tensor.matmul(pA[:, c], oT[:, c], wT[:, 3], start=True, stop=False)
                    mm = nc.tensor.matmul(pA[:, c], ones[0:1, :], cst[0:1, :], start=False, stop=True)
                mm.then_inc(s_pa, 1)
                pe.wait_ge(s_y, q + 1)
                pe.wait_ge(s_out, q + 1)
                for g in range(G):
                    mm = nc.tensor.transpose(pA[:, g * P:(g + 1) * P], yq[:, g], ident[:])
                mm.then_inc(s_pa, 1)
                pe.wait_ge(s_par, 5 * q + 5)
                for g in range(G):
                    mm = nc.tensor.matmul(pV[:, g * E:(g + 1) * E], yT[:, g * P:(g + 1) * P], wgT[:], start=True, stop=True)
                mm.then_inc(s_pv, 1)

            for k in range(2):
                quad(k, k, 0)
            with pe.Fori(1, NQ // 2) as q2:
                for k in range(2):
                    quad(2 * q2 + k, k, q2)


def build_moe(nc, shared, x1_d, g2, be2, W1, b1, W2, b2, ysort_d, osort_d, out):
    NG, _, DM = x1_d.shape
    E, _, DF = W1.shape
    NT = ysort_d.shape[0] // P
    NB = DF // P
    S = out.shape[0]
    TT = P // S
    G = 4
    NQ = NG // G
    yall, lg = shared["yall"], shared["lg"]
    w1, w2, b1b, b2b = shared["w1"], shared["w2"], shared["b1b"], shared["b2b"]
    s_ew = shared["s_ew"]
    s_zf = shared["s_zf"]

    with ExitStack() as ctx:
        def sb(name, shape, dt=F32):
            return ctx.enter_context(nc.sbuf_tensor(name, shape, dt))

        def ps(name, shape, dt=F32):
            return ctx.enter_context(nc.psum_tensor(name, shape, dt))

        def sem(name):
            return ctx.enter_context(nc.semaphore(name))

        ident = sb("m_ident", [P, P])
        tri = sb("m_tri", [P, P], BF16)
        onesb = sb("m_onesb", [P, P], BF16)
        mhalf = sb("m_mhalf", [P, G])
        iot_i = sb("m_iota_i", [P, E], I32)
        iot8 = sb("m_iota8", [P, E])
        iot0 = sb("m_iota0", [P, E])
        thr_i = sb("m_thr_i", [P, NG], I32)
        thr = sb("m_thr", [P, NG])
        tl_i = sb("m_tl_i", [P, NT], I32)
        tl = sb("m_tl", [P, NT])
        rst = sb("m_reset", [P, E, NG])
        one8 = sb("m_one8", [P, E])
        mxl = sb("m_mxl", [P, NG])
        eq = sb("m_eq", [P, NG, E])
        cand = sb("m_cand", [P, NG, E])
        idx = sb("m_idx", [P, NG])
        oh = sb("m_oh", [P, NG, E], BF16)
        tot = sb("m_tot", [P, E, NG])
        inc = sb("m_inc", [P, E, NG])
        cmp_ = sb("m_cmp", [P, E, NG])
        nt = sb("m_nt", [P, E])
        ntc = sb("m_ntc", [P, E])
        base = sb("m_base", [P, E])
        place = sb("m_place", [P, NG, E])
        pos = sb("m_pos", [P, NG])
        pos_u = sb("m_pos_u", [P, NG], U32)
        ecmp = sb("m_ecmp", [P, NT, E])
        eid = sb("m_eid", [P, NT])
        eid_i = sb("m_eid_i", [P, NT], I32)
        pidx = sb("m_pidx", [P, 2, G], U32)
        ytile = sb("m_ytile", [P, 2, G, DM])
        ys = sb("m_ys", [P, 2, DM])
        yT = sb("m_yT", [P, 2, P])
        hh = sb("m_hh", [P, 2, DF])
        hT = sb("m_hT", [P, 2, NB, P])
        ob = sb("m_ob", [P, 2, DM])
        gp = sb("m_gp", [P, 2, G], U32)
        gb = sb("m_gb", [P, 2, G, DM])
        xg = sb("m_xg", [P, 2, G, DM])
        g2b = sb("m_g2b", [P, DM])
        be2b = sb("m_be2b", [P, DM])
        r2 = sb("m_r2", [P, G, DM])
        st = sb("m_st", [P, G, 6])
        mv = sb("m_mv", [P, G, 2])
        ve = sb("m_ve", [P, G])
        rs = sb("m_rs", [P, G])
        zn = sb("m_zn", [P, G, DM])
        zm = sb("m_zm", [P, G, DM])
        z = sb("m_z", [P, G, DM])
        fo = sb("m_fo", [P, 2, G, DM])

        pR = ps("m_pR", [P, NG * E])
        pT = ps("m_pT", [P, NG * E])
        pY = ps("m_pY", [P, 2, 512])
        pH = ps("m_pH", [P, 2, DF])
        pHT = ps("m_pHT", [P, 2, NB * P])

        s_gate = sem("m_gate_passed")
        s_k = sem("m_consts")
        s_kd = sem("m_dve_consts")
        s_w = sem("m_weights")
        s_c = sem("m_chain")
        s_oh = sem("m_onehot_ready")
        s_rk = sem("m_ranks_ready")
        s_pos = sem("m_positions_ready")
        s_eid = sem("m_expert_ids_ready")
        s_stg = sem("m_scatter_staged")
        s_scs = [sem(f"m_scattered{k}") for k in range(2)]
        s_ysl = [sem(f"m_tile_loaded{k}") for k in range(2)]
        s_ty = sem("m_tile_transposed")
        s_yc = sem("m_tileT_copied")
        s_h = sem("m_hidden_ready")
        s_hb = sem("m_hidden_biased")
        s_ht = sem("m_hidden_transposed")
        s_hc = sem("m_hiddenT_copied")
        s_o = sem("m_out_ready")
        s_ob = sem("m_out_biased")
        s_osd = [sem(f"m_out_stored{k}") for k in range(2)]
        s_gst = sem("m_gather_staged")
        s_g = [sem(f"m_gathered{k}") for k in range(2)]
        s_xg = [sem(f"m_x_loaded{k}") for k in range(2)]
        s_r2 = sem("m_res_ready")
        s_st = sem("m_stats")
        s_mv = sem("m_meanvar")
        s_ve = sem("m_vareps")
        s_rs = sem("m_rstd")
        s_zn = sem("m_normalised")
        s_zm = sem("m_scaled")
        s_z = sem("m_z_ready")
        s_fo = sem("m_final_ready")
        s_out = [sem(f"m_stored{k}") for k in range(2)]

        block = ctx.enter_context(nc.Block())
        NTP = NT // 2

        @block.sync
        def _(sp):
            sp.dma_start(g2b[:], g2.rearrange("(o d) -> o d", o=1).broadcast_to([P, DM])).then_inc(s_w, 16)
            sp.dma_start(be2b[:], be2.rearrange("(o d) -> o d", o=1).broadcast_to([P, DM])).then_inc(s_w, 16)
            for k in range(2):
                sp.wait_ge(s_scs[k], 16 * (NG // 2))

            def tile(j, k, j2):
                wait_if(sp, s_ty, j, 1, -1)
                sp.dma_start(ys[:, k], ysort_d[bass.ds(j * P, P), :]).then_inc(s_ysl[k], 16)

            def store(j, k):
                sp.wait_ge(s_ob, j + 1)
                sp.dma_start(osort_d[bass.ds(j * P, P), :], ob[:, k]).then_inc(s_osd[k], 16)

            for k in range(2):
                tile(k, k, 0)
            with sp.Fori(1, NTP) as j2:
                for k in range(2):
                    tile(2 * j2 + k, k, j2)
                    store(2 * j2 + k - 2, k)
            for k in range(2):
                store(NT - 2 + k, k)

            def xload(q, k):
                wait_if(sp, s_fo, q, 1, -1)
                sp.dma_start(xg[:, k], x1_d[bass.ds(q * G, G)].rearrange("g p d -> p g d")).then_inc(s_xg[k], 16)

            def put(q, k):
                sp.wait_ge(s_fo, q + 1)
                for s in range(S):
                    sp.dma_start(out[s, bass.ds(q * G * TT, G * TT), :].rearrange("(g t) d -> t g d", g=G),
                                 fo[s * TT:(s + 1) * TT, k]).then_inc(s_out[k], 16)

            for k in range(2):
                xload(k, k)
            with sp.Fori(1, NQ // 2) as q2:
                for k in range(2):
                    put(2 * q2 + k - 2, k)
                    xload(2 * q2 + k, k)
            for k in range(2):
                put(NQ - 2 + k, k)
            for k in range(2):
                sp.wait_ge(s_out[k], 16 * S * (NQ // 2))

        @block.gpsimd
        def _(pool):
            nc.gpsimd.memset(ident[:], 0.0).then_inc(s_k, 1)
            nc.gpsimd.memset(tri[:], 1.0).then_inc(s_k, 1)
            nc.gpsimd.memset(onesb[:], 1.0).then_inc(s_k, 1)
            nc.gpsimd.memset(mhalf[:], -0.5).then_inc(s_k, 1)
            nc.gpsimd.memset(rst[:], 1.0).then_inc(s_k, 1)
            nc.gpsimd.memset(one8[:], 1.0).then_inc(s_k, 1)
            nc.gpsimd.iota(iot_i[:], pattern=[[1, E]], base=0, channel_multiplier=0).then_inc(s_k, 1)
            nc.gpsimd.iota(thr_i[:], pattern=[[P, NG]], base=0, channel_multiplier=0).then_inc(s_k, 1)
            nc.gpsimd.iota(tl_i[:], pattern=[[1, NT]], base=0, channel_multiplier=0).then_inc(s_k, 1)
            pool.wait_ge(s_k, 9)
            nc.gpsimd.affine_select(out=ident[:], in_=ident[:], compare_op=ALU.not_equal, fill=1.0, base=0,
                                    pattern=[[-1, P]], channel_multiplier=1).then_inc(s_k, 1)
            nc.gpsimd.affine_select(out=tri[:], in_=tri[:], compare_op=ALU.is_ge, fill=0.0, base=-1,
                                    pattern=[[1, P]], channel_multiplier=-1).then_inc(s_k, 1)
            nc.gpsimd.memset(rst[:, :, 0:1], 0.0).then_inc(s_k, 1)
            pool.wait_ge(s_pos, 1)
            pool.wait_ge(s_zf, 16)

            with pool.Fori(0, NQ // 2) as q2:
                for k in range(2):
                    pool.wait_ge(s_stg, 4 * q2 + 2 * k + 2)
                    pool.sem_inc(s_gate, 1)
                    for t in range(G):
                        nc.gpsimd.indirect_dma_start(
                            out=ysort_d, out_offset=bass.IndirectOffsetOnAxis(ap=pidx[:, k, t:t + 1], axis=0),
                            in_=ytile[:, k, t], in_offset=None).then_inc(s_scs[k], 16)

            for k in range(2):
                pool.wait_ge(s_osd[k], 16 * NTP)

            def gather(q, k):
                pool.wait_ge(s_gst, q + 1)
                wait_if(pool, s_r2, q, 2, -3)
                pool.sem_inc(s_gate, 1)
                for t in range(G):
                    nc.gpsimd.indirect_dma_start(
                        out=gb[:, k, t], out_offset=None, in_=osort_d,
                        in_offset=bass.IndirectOffsetOnAxis(ap=gp[:, k, t:t + 1], axis=0)).then_inc(s_g[k], 16)

            def norms(q):
                pool.wait_ge(s_ve, 2 * q + 1)
                nc.gpsimd.tensor_tensor(rs[:], ve[:], mhalf[:], ALU.pow).then_inc(s_rs, 1)
                pool.wait_ge(s_zn, G * (q + 1))
                nc.gpsimd.tensor_tensor(zm[:], zn[:], g2b[:].unsqueeze(1).to_broadcast([P, G, DM]), ALU.mult).then_inc(s_zm, 1)
                pool.wait_ge(s_zm, q + 1)
                nc.gpsimd.tensor_tensor(z[:], zm[:], be2b[:].unsqueeze(1).to_broadcast([P, G, DM]), ALU.add).then_inc(s_z, 1)
                pool.wait_ge(s_ve, 2 * q + 2)
                nc.gpsimd.tensor_tensor(rs[:], ve[:], mhalf[:], ALU.pow).then_inc(s_rs, 1)

            pool.wait_ge(s_w, 32)
            gather(0, 0)
            gather(1, 1)
            norms(0)
            with pool.Fori(1, NQ // 2) as q2:
                gather(2 * q2, 0)
                norms(2 * q2 - 1)
                gather(2 * q2 + 1, 1)
                norms(2 * q2)
            norms(NQ - 1)

        @block.vector
        def _(dve):
            step = [0]

            def link(ins):
                step[0] += 1
                ins.then_inc(s_c, 1)
                dve.wait_ge(s_c, step[0])

            dve.wait_ge(s_k, 12)
            nc.vector.tensor_copy(iot0[:], iot_i[:]).then_inc(s_kd, 1)
            nc.vector.tensor_copy(thr[:], thr_i[:]).then_inc(s_kd, 1)
            nc.vector.tensor_copy(tl[:], tl_i[:]).then_inc(s_kd, 1)
            dve.wait_ge(s_kd, 3)
            link(nc.vector.tensor_scalar(iot8[:], iot0[:], float(E), None, ALU.add))
            link(nc.vector.tensor_reduce(mxl[:], lg[:], AX.X, ALU.max))
            link(nc.vector.tensor_tensor(eq[:], lg[:], mxl[:].unsqueeze(2).to_broadcast([P, NG, E]), ALU.is_equal))
            link(nc.vector.scalar_tensor_tensor(cand[:], eq[:], -float(E), iot8[:].unsqueeze(1).to_broadcast([P, NG, E]),
                                                ALU.mult, ALU.add))
            link(nc.vector.tensor_reduce(idx[:], cand[:], AX.X, ALU.min))
            nc.vector.tensor_tensor(oh[:], iot0[:].unsqueeze(1).to_broadcast([P, NG, E]),
                                    idx[:].unsqueeze(2).to_broadcast([P, NG, E]), ALU.is_equal).then_inc(s_oh, 1)
            dve.wait_ge(s_rk, 2)
            link(nc.vector.tensor_copy(tot[:], pT[:].rearrange("p (t e) -> p e t", e=E)))
            link(nc.vector.tensor_tensor_scan(inc[:].rearrange("p e t -> p (e t)"), rst[:].rearrange("p e t -> p (e t)"),
                                              tot[:].rearrange("p e t -> p (e t)"), 0.0, ALU.mult, ALU.add))
            link(nc.vector.tensor_tensor(tot[:], inc[:], tot[:], ALU.subtract))
            link(nc.vector.tensor_tensor(cmp_[:], inc[:, :, NG - 1:NG].to_broadcast([P, E, NG]),
                                         thr[:].unsqueeze(1).to_broadcast([P, E, NG]), ALU.is_gt))
            link(nc.vector.tensor_reduce(nt[:], cmp_[:], AX.X, ALU.add))
            link(nc.vector.tensor_tensor_scan(ntc[:], one8[:], nt[:], 0.0, ALU.mult, ALU.add))
            link(nc.vector.tensor_tensor(base[:], ntc[:], nt[:], ALU.subtract))
            link(nc.vector.scalar_tensor_tensor(cmp_[:], base[:].unsqueeze(2).to_broadcast([P, E, NG]), float(P), tot[:],
                                                ALU.mult, ALU.add))
            link(nc.vector.tensor_tensor(place[:], pR[:].rearrange("p (t e) -> p t e", e=E),
                                         cmp_[:].rearrange("p e t -> p t e"), ALU.add))
            link(nc.vector.tensor_tensor(place[:], place[:], oh[:], ALU.mult))
            link(nc.vector.tensor_reduce(pos[:], place[:], AX.X, ALU.add))
            link(nc.vector.tensor_copy(pos_u[:], pos[:]))
            link(nc.vector.tensor_tensor(ecmp[:], ntc[:].unsqueeze(1).to_broadcast([P, NT, E]),
                                         tl[:].unsqueeze(2).to_broadcast([P, NT, E]), ALU.is_le))
            link(nc.vector.tensor_reduce(eid[:], ecmp[:], AX.X, ALU.add))
            link(nc.vector.tensor_scalar(eid[:], eid[:], float(E - 1), None, ALU.min))
            nc.vector.tensor_copy(eid_i[:], eid[:]).then_inc(s_eid, 1)
            nc.vector.tensor_copy(pos[:], pos_u[:]).then_inc(s_pos, 1)

            def stage(q, k):
                nc.vector.tensor_copy(pidx[:, k], pos_u[:, bass.ds(q * G, G)]).then_inc(s_stg, 1)
                nc.vector.tensor_copy(ytile[:, k], yall[:, bass.ds(q * G, G)]).then_inc(s_stg, 1)

            for k in range(2):
                stage(k, k)
            with dve.Fori(1, NQ // 2) as q2:
                for k in range(2):
                    dve.wait_ge(s_scs[k], 16 * G * q2)
                    stage(2 * q2 + k, k)

            dve.wait_ge(s_eid, 1)
            dve.wait_ge(s_ew, 64)

            def hidden(j, k, e):
                dve.wait_ge(s_h, j + 1)
                wait_if(dve, s_ht, j, 1, -1)
                nc.vector.tensor_tensor(hh[:, k], pH[:, k], b1b[:, bass.ds(e, 1)].rearrange("p o f -> p (o f)"),
                                        ALU.add).then_inc(s_hb, 1)

            def outb(j, k, e, j2):
                dve.wait_ge(s_o, j + 1)
                if not isinstance(j2, int):
                    dve.wait_ge(s_osd[k], 16 * j2)
                nc.vector.tensor_tensor(ob[:, k], pY[:, k, P:2 * P], b2b[:, bass.ds(e, 1)].rearrange("p o f -> p (o f)"),
                                        ALU.add).then_inc(s_ob, 1)

            def pair(j2, j):
                es = [dve.value_load(eid_i[0:1, bass.ds(j + k, 1)], min_val=0, max_val=E - 1) for k in range(2)]
                hidden(j, 0, es[0])
                hidden(j + 1, 1, es[1])
                outb(j, 0, es[0], j2)
                outb(j + 1, 1, es[1], j2)

            pair(0, 0)
            with dve.Fori(1, NTP) as j2:
                pair(j2, 2 * j2)

            def stage_index(q, k):
                nc.vector.tensor_copy(gp[:, k], pos_u[:, bass.ds(q * G, G)]).then_inc(s_gst, 1)

            def stats(q, j, src):
                for t in range(G):
                    nc.vector.bn_stats(st[:, t], src[:, t]).then_inc(s_st, 1)
                dve.wait_ge(s_st, 2 * G * q + G * (j + 1))
                dve.sem_inc(s_gate, 1)
                for t in range(G):
                    nc.vector.bn_aggr(mv[:, t], st[:, t]).then_inc(s_mv, 1)
                dve.wait_ge(s_mv, 2 * G * q + G * (j + 1))
                nc.vector.tensor_scalar(ve[:], mv[:, :, 1], EPS, None, ALU.add).then_inc(s_ve, 1)
                dve.wait_ge(s_rs, 2 * q + j + 1)

            def final(q, k, q2):
                dve.wait_ge(s_g[k], 16 * G * q2 + 16 * G)
                wait_if(dve, s_fo, q, 1, 0)
                nc.vector.tensor_tensor(r2[:], gb[:, k], yall[:, bass.ds(q * G, G)], ALU.add).then_inc(s_r2, 1)
                dve.wait_ge(s_r2, 2 * q + 1)
                stats(q, 0, r2)
                for t in range(G):
                    nc.vector.tensor_scalar(zn[:, t], r2[:, t], mv[:, t, 0:1], rs[:, t:t + 1], ALU.subtract,
                                            ALU.mult).then_inc(s_zn, 1)
                dve.wait_ge(s_z, q + 1)
                dve.wait_ge(s_xg[k], 16 * q2 + 16)
                nc.vector.tensor_tensor(r2[:], z[:], xg[:, k], ALU.add).then_inc(s_r2, 1)
                dve.wait_ge(s_r2, 2 * q + 2)
                stats(q, 1, r2)
                if not isinstance(q2, int):
                    dve.wait_ge(s_out[k], 16 * S * q2)
                for t in range(G):
                    ins = nc.vector.tensor_scalar(fo[:, k, t], r2[:, t], mv[:, t, 0:1], rs[:, t:t + 1], ALU.subtract, ALU.mult)
                ins.then_inc(s_fo, 1)

            for k in range(2):
                stage_index(k, k)
            for k in range(2):
                final(k, k, 0)
                stage_index(2 + k, k)
            with dve.Fori(1, NQ // 2 - 1) as q2:
                for k in range(2):
                    final(2 * q2 + k, k, q2)
                    stage_index(2 * q2 + k + 2, k)
            with dve.Fori(NQ // 2 - 1, NQ // 2) as q2:
                for k in range(2):
                    final(2 * q2 + k, k, q2)

        @block.scalar
        def _(act):
            act.wait_ge(s_k, 12)

            def tile(j, k):
                act.wait_ge(s_ty, j + 1)
                wait_if(act, s_h, j, 1, -1)
                nc.scalar.copy(yT[:, k], pY[:, k, 0:P]).then_inc(s_yc, 1)

            def relu(j, k):
                act.wait_ge(s_ht, j + 1)
                wait_if(act, s_o, j, 1, -1)
                nc.scalar.activation(hT[:, k], pHT[:, k].rearrange("p (b t) -> p b t", b=NB), ACT.Relu).then_inc(s_hc, 1)

            for k in range(2):
                tile(k, k)
            relu(0, 0)
            relu(1, 1)
            with act.Fori(1, NTP) as j2:
                for k in range(2):
                    tile(2 * j2 + k, k)
                for k in range(2):
                    relu(2 * j2 + k, k)

        @block.tensor
        def _(pe):
            pe.wait_ge(s_k, 12)
            pe.wait_ge(s_oh, 1)
            ohf = oh[:].rearrange("p t e -> p (t e)")
            nc.tensor.matmul(pR[:], tri[:], ohf, start=True, stop=True).then_inc(s_rk, 1)
            nc.tensor.matmul(pT[:], onesb[:], ohf, start=True, stop=True).then_inc(s_rk, 1)
            pe.wait_ge(s_eid, 1)
            pe.wait_ge(s_ew, 64)

            def turn(j, k, j2):
                pe.wait_ge(s_ysl[k], 16 * j2 + 16)
                wait_if(pe, s_ob, j, 1, -1)
                nc.tensor.transpose(pY[:, k, 0:P], ys[:, k], ident[:]).then_inc(s_ty, 1)

            def up(j, k, e):
                pe.wait_ge(s_yc, j + 1)
                wait_if(pe, s_hb, j, 1, -1)
                nc.tensor.matmul(pH[:, k], yT[:, k], w1[:, bass.ds(e, 1)].rearrange("p o f -> p (o f)"), start=True,
                                 stop=True).then_inc(s_h, 1)

            def turn_hidden(j, k):
                pe.wait_ge(s_hb, j + 1)
                wait_if(pe, s_hc, j, 1, -1)
                for b in range(NB):
                    mm = nc.tensor.transpose(pHT[:, k, b * P:(b + 1) * P], hh[:, k, b * P:(b + 1) * P], ident[:])
                mm.then_inc(s_ht, 1)

            def down(j, k, e):
                pe.wait_ge(s_hc, j + 1)
                for b in range(NB):
                    mm = nc.tensor.matmul(pY[:, k, P:2 * P], hT[:, k, b],
                                          w2[:, bass.ds(e, 1), b * DM:(b + 1) * DM].rearrange("p o d -> p (o d)"),
                                          start=(b == 0), stop=(b == NB - 1))
                mm.then_inc(s_o, 1)

            def pair(j2, j):
                es = [pe.value_load(eid_i[0:1, bass.ds(j + k, 1)], min_val=0, max_val=E - 1) for k in range(2)]
                for k in range(2):
                    turn(j + k, k, j2)
                for k in range(2):
                    up(j + k, k, es[k])
                for k in range(2):
                    turn_hidden(j + k, k)
                for k in range(2):
                    down(j + k, k, es[k])

            pair(0, 0)
            with pe.Fori(1, NTP) as j2:
                pair(j2, 2 * j2)



def build_ffn(nc, x1_d, Wqkv, bqkv, Wo, bo, g1, be1, g2, be2, Wg, W1, b1, W2, b2, out):
    NG, _, DM = x1_d.shape
    E, _, DF = W1.shape
    NT = -(-(NG + E - 1) // 2) * 2
    ysort_d = nc.dram_tensor("ysort", [NT * P, DM], F32).ap()
    osort_d = nc.dram_tensor("osort", [NT * P, DM], F32).ap()
    with ExitStack() as ctx:
        def sb(name, shape, dt=F32):
            return ctx.enter_context(nc.sbuf_tensor(name, shape, dt))

        shared = {
            "yall": sb("yall", [P, NG, DM]), "lg": sb("lg", [P, NG, E]),
            "w1": sb("w1", [P, E, DF]), "w2": sb("w2", [P, E, DF]),
            "b1b": sb("b1b", [P, E, DF]), "b2b": sb("b2b", [P, E, DM]),
            "s_ew": ctx.enter_context(nc.semaphore("expert_weights")),
            "s_zf": ctx.enter_context(nc.semaphore("zero_filled")),
        }
        zero = sb("zero", [P, DM])
        s_zm = ctx.enter_context(nc.semaphore("zero_ready"))
        with nc.Block() as block:
            @block.scalar
            def _(act):
                with nc.allow_non_contiguous_dma(reason="rows of weights"):
                    act.dma_start(shared["w1"][:], W1.rearrange("e p f -> p e f")).then_inc(shared["s_ew"], 16)
                    act.dma_start(shared["w2"][:].rearrange("p e (b d) -> p e b d", d=DM),
                                  W2.rearrange("e (b p) d -> p e b d", p=P)).then_inc(shared["s_ew"], 16)
                    act.dma_start(shared["b1b"][:].rearrange("p e f -> p (e f)"),
                                  b1.rearrange("(o e) f -> o (e f)", o=1).broadcast_to([P, E * DF])).then_inc(shared["s_ew"], 16)
                    act.dma_start(shared["b2b"][:].rearrange("p e f -> p (e f)"),
                                  b2.rearrange("(o e) f -> o (e f)", o=1).broadcast_to([P, E * DM])).then_inc(shared["s_ew"], 16)
                    act.wait_ge(s_zm, 1)
                    act.dma_start(ysort_d.rearrange("(t p) d -> p t d", p=P),
                                  zero[:].unsqueeze(1).to_broadcast([P, NT, DM])).then_inc(shared["s_zf"], 16)

            @block.vector
            def _(dve):
                nc.vector.memset(zero[:], 0.0).then_inc(s_zm, 1)

        build_attention(nc, shared, x1_d, Wqkv, bqkv, Wo, bo, g1, be1, g2, be2, Wg, W1, b1, W2, b2, None)
        build_moe(nc, shared, x1_d, g2, be2, W1, b1, W2, b2, ysort_d, osort_d, out)


def build(nc, ins, out):
    x = ins["L0_attn_x"]
    NS, L, DM = x.shape
    x1_d = nc.dram_tensor("x1_grouped", [NS * L // P, P, DM], F32).ap()
    build_mamba(nc, x, *(ins["L0_attn_" + n] for n in
                         ("norm_w", "norm_b", "W_in", "conv_w", "conv_b", "W_x", "W_dt", "b_dt", "A_log", "D", "W_out")), x1_d)
    build_ffn(nc, x1_d, *(ins["L0_ffn_" + n] for n in
                          ("Wqkv", "bqkv", "Wo", "bo", "g1", "be1", "g2", "be2", "Wg", "W1", "b1", "W2", "b2")), out)


_INS = ["L0_attn_x", "L0_attn_norm_w", "L0_attn_norm_b", "L0_attn_W_in", "L0_attn_conv_w", "L0_attn_conv_b",
        "L0_attn_W_x", "L0_attn_W_dt", "L0_attn_b_dt", "L0_attn_A_log", "L0_attn_D", "L0_attn_W_out", "L0_ffn_Wqkv",
        "L0_ffn_bqkv", "L0_ffn_Wo", "L0_ffn_bo", "L0_ffn_g1", "L0_ffn_be1", "L0_ffn_g2", "L0_ffn_be2", "L0_ffn_Wg",
        "L0_ffn_W1", "L0_ffn_b1", "L0_ffn_W2", "L0_ffn_b2"]


def kernel(**inputs):
    import concourse.bacc as bacc
    from concourse.bass_utils import run_bass_kernel_spmd

    nc = bacc.Bacc("TRN2", target_bir_lowering=False, num_devices=1)
    arrays, ins = {}, {}
    for name in _INS:
        a = np.ascontiguousarray(inputs[name])
        arrays[f"in_{name}"] = a
        ins[name] = nc.dram_tensor(f"in_{name}", a.shape, mybir.dt.from_np(a.dtype), kind="ExternalInput").ap()
    out = nc.dram_tensor("out", arrays["in_L0_attn_x"].shape, F32, kind="ExternalOutput").ap()
    build(nc, ins, out)
    r = run_bass_kernel_spmd(nc, [arrays], core_ids=[0])
    return r.results[0]["out"]
```

```python
import numpy as np
import concourse.bass as bass
from concourse import mybir
from contextlib import ExitStack

ALU = mybir.AluOpType
ACT = mybir.ActivationFunctionType
AX = mybir.AxisListType
F32 = mybir.dt.float32
BF16 = mybir.dt.bfloat16

P = 128
EPS = 1e-5
POOL_B = (2, 5, 8, 11, 14)
LAG = 2


def log1p_factors():
    k = np.arange(600)
    y = (1 - np.cos(np.pi * (k + 0.5) / 600)) / 2
    fit = np.polynomial.chebyshev.Chebyshev.fit(y, np.log1p(y) / y, 8, domain=[0, 1])
    c = fit.convert(kind=np.polynomial.Polynomial).coef
    r = sorted((z for z in np.roots(c[::-1]) if z.imag > 0), key=lambda z: z.real)
    return float(c[8]), [(float(-z.real), float(z.imag) ** 2) for z in r]


def build_mamba(nc, x, norm_w, norm_b, W_in, conv_w, conv_b, W_x, W_dt, b_dt, A_log, D, W_out, x1_d):
    NS, L, DM = x.shape
    DI = W_dt.shape[1]
    R = W_dt.shape[0]
    N = A_log.shape[1]
    KC = conv_w.shape[2]
    H = DI // P
    T = L // P
    LP = L + KC - 1
    NT = NS * T
    XL = 2
    TT = P // NS
    GT = P // TT
    x1_g = x1_d.rearrange("(t g) p d -> t g p d", g=GT)
    lead, quad = log1p_factors()

    with ExitStack() as ctx:
        def sb(name, shape, dt=F32):
            return ctx.enter_context(nc.sbuf_tensor(name, shape, dt))

        def ps(name, shape, dt=F32):
            return ctx.enter_context(nc.psum_tensor(name, shape, dt))

        def sem(name):
            return ctx.enter_context(nc.semaphore(name))

        ident = sb("ident", [P, P])
        sel = sb("sel", [96, 2 * N, P], BF16)
        win = sb("win", [P, 2 * DI])
        cwb = sb("cwb", [P, DI, KC])
        wtap = sb("wtap", [P, KC, DI])
        cb = sb("cb", [P, H])
        cbh = sb("cbh", [P, H])
        wx = sb("wx", [P, H, R + 2 * N])
        wbc = sb("wbc", [P, H, 3, 2 * N])
        wdt = sb("wdt", [R, DI])
        bdt = sb("bdt", [P, H])
        alog = sb("alog", [P, H, N])
        aneg = sb("aneg", [P, H, N])
        dsk = sb("dsk", [P, H])
        wout = sb("wout", [P, H, DM])
        nw = sb("nw", [P, 1])
        nb = sb("nb", [P, 1])
        mhalf = sb("mhalf", [P, NT])
        xall = sb("xall", [P, NT, DM])
        stats = sb("stats", [P, T, 6])
        mv = sb("mv", [P, T, 2])
        mean = sb("mean", [P, NT])
        ve = sb("ve", [P, NT])
        rstd = sb("rstd", [P, NT])
        xn = sb("xn", [P, 2, T, DM])
        xnT = sb("xnT", [P, NS, LP])
        u = sb("u", [P, 2 * H * L])
        zs = sb("zs", [P, 2 * H * L])
        delta = sb("delta", [P, 2 * H * L])
        dtu = sb("dtu", [P, 2 * H * L])
        bcs = sb("bcs", [96, 2 * L], BF16)
        th = sb("th", [P, 2, L])
        xh = sb("xh", [P, 2, L])
        dtl = sb("dtl", [R, L])
        r1 = sb("r1", [96, L])
        av = sb("av", [P, H, L])
        ey = sb("ey", [P, H, L])
        rv = sb("rv", [P, H, L])
        sq = sb("sq", [P, 4, H, L])
        bt = sb("bt", [P, 2, H, L])
        hb = sb("hb", [P, 4, H, L])
        hc = sb("hc", [P, 2, H, L])
        cs = sb("cs", [P, 2, L])
        bs = sb("bs", [P, L])
        yd = sb("yd", [P, H, L])
        yg = sb("yg", [P, H, L])
        ro = sb("ro", [P, T, DM])
        st2 = sb("st2", [P, T, 6])
        mv2 = sb("mv2", [P, T, 2])
        ve2 = sb("ve2", [P, T])
        rstd2 = sb("rstd2", [P, T])
        x1 = sb("x1", [P, T, DM])

        pB = ps("pB", [P, L])
        pC = ps("pC", [P, L])
        pA = ps("pA", [P, H, L])
        pY = ps("pY", [P, H, L])
        pre = ps("pre", [P, 2, L])

        s_w = sem("weights_loaded")
        s_x = [sem(f"x_loaded{q}") for q in range(XL)]
        s_id = sem("pool_consts")
        s_gate = sem("gate_passed")
        s_z = sem("pads_zeroed")
        s_prep = sem("weights_prepared")
        s_an = sem("a_exp")
        s_aneg = sem("aneg_ready")
        s_st = sem("stats_ready")
        s_mv = sem("meanvar_ready")
        s_mean = sem("mean_ready")
        s_ve = sem("var_eps_ready")
        s_rs = sem("rstd_ready")
        s_xn = sem("xn_ready")
        s_tp = sem("xn_transposed")
        s_xT = sem("xnT_ready")
        s_pre = sem("pre_psum_ready")
        s_pact = sem("pre_read_by_act")
        s_bcr = sem("bc_residual")
        s_th = sem("silu_inputs")
        s_silu = sem("silu_ready")
        s_dtl = sem("dtl_ready")
        s_bc1 = sem("bc_first_part")
        s_bc2 = sem("bc_second_parts")
        s_bc = sem("bc_parts_ready")
        s_v = sem("dt_exps")
        s_sq = sem("dt_squares")
        s_dl = sem("delta_ready")
        s_du = sem("dtu_ready")
        s_bb = sem("b_rows_ready")
        s_cc = sem("c_rows_ready")
        s_cs = sem("c_copied")
        s_bs = sem("b_copied")
        s_pb = sem("pool_b_ready")
        s_db = sem("vector_b_ready")
        s_a = sem("a_ready")
        s_h = sem("h_ready")
        s_hc = sem("hc_ready")
        s_hu = sem("hc_summed")
        s_yd = sem("yd_ready")
        s_yg = sem("yg_ready")
        s_o = sem("out_psum_ready")
        s_r = sem("residual_ready")
        s_st2 = sem("stats2_ready")
        s_mv2 = sem("meanvar2_ready")
        s_ve2 = sem("vareps2_ready")
        s_rs2 = sem("rstd2_ready")
        s_x1 = sem("x1_ready")
        s_x1d = sem("x1_stored")

        VEC_B = [n for n in range(N) if n not in POOL_B]
        s_cbh = sem("conv_bias_halved")
        s_qa = sem("dt_poly_steps")
        NPB = len(POOL_B)
        NVB = N - NPB

        def at(buf, i, n=1, off=0, width=L):
            par = i % 2
            size = H * L
            return buf[:, bass.ds(par * size + off, width)]

        def wait(eng, s, i, per, c):
            if isinstance(i, int) and i * per + c <= 0:
                return
            eng.wait_ge(s, i * per + c)

        a_bias = [sb(f"a_bias{k}", [P, 1]) for k in range(4)]

        block = ctx.enter_context(nc.Block())

        @block.sync
        def _(sp):
            with nc.allow_non_contiguous_dma(reason="small weights"):
                for q in range(XL):
                    sp.dma_start(xall[:, q * NT // XL:(q + 1) * NT // XL, :],
                                 x[q * NS // XL:(q + 1) * NS // XL].rearrange("s (t p) d -> p (s t) d", p=P)).then_inc(s_x[q], 16)
                    if q == 0:
                        sp.dma_start(win[:], W_in).then_inc(s_w, 16)
                        sp.dma_start(cwb[:].rearrange("p c k -> p (c k)"),
                                     conv_w.rearrange("c o k -> o (c k)").broadcast_to([P, DI * KC])).then_inc(s_w, 16)
                        sp.dma_start(nw[:], norm_w.rearrange("(p o) -> p o", o=1)).then_inc(s_w, 16)
                        sp.dma_start(nb[:], norm_b.rearrange("(p o) -> p o", o=1)).then_inc(s_w, 16)
                        sp.dma_start(cb[:], conv_b.rearrange("(h p) -> p h", p=P)).then_inc(s_w, 16)
                        sp.dma_start(wx[:], W_x.rearrange("(h p) n -> p h n", p=P)).then_inc(s_w, 16)
                        sp.dma_start(wdt[:], W_dt).then_inc(s_w, 16)
                        sp.dma_start(bdt[:], b_dt.rearrange("(h p) -> p h", p=P)).then_inc(s_w, 16)
                        sp.dma_start(alog[:], A_log.rearrange("(h p) n -> p h n", p=P)).then_inc(s_w, 16)
                        sp.dma_start(dsk[:], D.rearrange("(h p) -> p h", p=P)).then_inc(s_w, 16)
                        sp.dma_start(wout[:], W_out.rearrange("(h p) n -> p h n", p=P)).then_inc(s_w, 16)
                with sp.Fori(0, NS) as s:
                    sp.wait_ge(s_x1, (s + 1) * T)
                    for g in range(GT):
                        sp.dma_start(x1_g[:, g, bass.ds(s * TT, TT), :].rearrange("t p d -> p t d"),
                                     x1[g * TT:(g + 1) * TT]).then_inc(s_x1d, 16)
            sp.wait_ge(s_x1d, 16 * GT * NS)

        NWL = 11

        @block.gpsimd
        def _(pool):
            nc.gpsimd.memset(ident[:], 0.0).then_inc(s_id, 1)
            nc.gpsimd.memset(sel[:], 0.0).then_inc(s_id, 1)
            nc.gpsimd.memset(mhalf[:], -0.5).then_inc(s_id, 1)
            nc.gpsimd.memset(xnT[:, :, 0:KC - 1], 0.0).then_inc(s_id, 1)
            pool.wait_ge(s_id, 4)
            nc.gpsimd.affine_select(out=ident[:], in_=ident[:], compare_op=ALU.not_equal, fill=1.0, base=0,
                                    pattern=[[-1, P]], channel_multiplier=1).then_inc(s_id, 1)
            for part in range(3):
                nc.gpsimd.affine_select(out=sel[:], in_=sel[:], compare_op=ALU.not_equal, fill=1.0,
                                        base=-2 * N * part, pattern=[[-1, 2 * N], [0, P]],
                                        channel_multiplier=1).then_inc(s_id, 1)
                pool.wait_ge(s_id, 6 + part)
            with pool.Fori(0, NS) as s:
                pool.wait_ge(s_ve, s + 1)
                sl = bass.ds(s * T, T)
                nc.gpsimd.tensor_tensor(rstd[:, sl], ve[:, sl], mhalf[:, sl], ALU.pow).then_inc(s_rs, 1)

            def product_b(i, n):
                k = POOL_B.index(n)
                wait(pool, s_bs, i, NPB, k + 1)
                if k == 0:
                    pool.wait_ge(s_du, i + 1)
                wait(pool, s_h, i, H * N, H * (n - 1))
                pool.sem_inc(s_gate, 1)
                nc.gpsimd.tensor_tensor(bt[:, n % 2], at(dtu, i, width=H * L).rearrange("p (h t) -> p h t", h=H),
                                        bs[:].unsqueeze(1).to_broadcast([P, H, L]), ALU.mult).then_inc(s_pb, 1)

            def product_hc(i, n):
                wait(pool, s_cs, i, N, n + 1)
                wait(pool, s_h, i, H * N, H * (n + 1))
                wait(pool, s_hu, i, N, n - 1)
                nc.gpsimd.tensor_tensor(hc[:, n % 2], hb[:, n % 4],
                                        cs[:, n % 2].unsqueeze(1).to_broadcast([P, H, L]), ALU.mult).then_inc(s_hc, 1)

            def body(i, first=False, last=False):
                for n in range(N):
                    if n in POOL_B:
                        product_b(i, n)
                    if n >= 1:
                        product_hc(i, n - 1)
                    elif not first:
                        product_hc(i - 1, N - 1)
                    if n == 5 and not first:
                        gate(i - 1)
                    if n == 12 and not first:
                        rstd_out(i - 1)
                    if n == 14 and not last:
                        times_u(i + 1)
                if last:
                    product_hc(i, N - 1)

            def gate(i):
                pool.wait_ge(s_silu, 4 * i + 4)
                pool.wait_ge(s_yd, H * (i + 1))
                wait(pool, s_o, i, 1, 0)
                nc.gpsimd.tensor_tensor(yg[:].rearrange("p h t -> p (h t)"), yd[:].rearrange("p h t -> p (h t)"),
                                        at(zs, i, width=H * L), ALU.mult).then_inc(s_yg, 1)

            def rstd_out(i):
                pool.wait_ge(s_ve2, i + 1)
                nc.gpsimd.tensor_tensor(rstd2[:], ve2[:], mhalf[:, 0:T], ALU.pow).then_inc(s_rs2, 1)

            def times_u(i):
                pool.wait_ge(s_dl, i + 1)
                pool.wait_ge(s_silu, 4 * i + 2)
                nc.gpsimd.tensor_tensor(at(dtu, i, width=H * L), at(delta, i, width=H * L), at(u, i, width=H * L),
                                        ALU.mult).then_inc(s_du, 1)

            times_u(0)
            body(0, first=True)
            with pool.Fori(1, NS - 1) as i:
                body(i)
            body(NS - 1, last=True)
            gate(NS - 1)
            rstd_out(NS - 1)

        @block.scalar
        def _(act):
            nc.scalar.preload_act_table_set("exp_and_others")
            act.wait_ge(s_w, 16 * NWL)
            nc.scalar.activation(aneg[:], alog[:], ACT.Exp).then_inc(s_an, 1)
            nc.scalar.mul(cbh[:], cb[:], 0.5).then_inc(s_cbh, 1)
            act.wait_ge(s_an, 1)
            nc.scalar.mul(aneg[:], aneg[:], -1.0).then_inc(s_aneg, 1)
            act.wait_ge(s_aneg, 1)
            act.wait_ge(s_cbh, 1)
            act.wait_ge(s_id, 4)
            act.wait_ge(s_z, 4)
            with act.Fori(0, NS // 2) as s2:
                for k in range(2):
                    s = 2 * s2 + k
                    act.wait_ge(s_tp, T * (s + 1))
                    nc.scalar.activation(xnT[:, bass.ds(s, 1), KC - 1:LP].rearrange("p o t -> p (o t)"), pre[:, k],
                                         ACT.Identity, bias=nb[:, 0:1], scale=nw[:, 0:1]).then_inc(s_xT, 1)

            def silu_in(i, m):
                act.wait_ge(s_pre, 8 * i + (m + 1 if m < 2 else m + 5))
                wait(act, s_silu, i, 4, m - 1)
                if m < 2:
                    nc.scalar.activation(th[:, m % 2], pre[:, m % 2], ACT.Tanh, bias=cbh[:, m:m + 1],
                                         scale=0.5).then_inc(s_th, 1)
                    nc.scalar.activation(xh[:, m % 2], pre[:, m % 2], ACT.Identity, bias=cbh[:, m:m + 1],
                                         scale=0.5).then_inc(s_pact, 1)
                else:
                    nc.scalar.activation(th[:, m % 2], pre[:, m % 2], ACT.Tanh, scale=0.5).then_inc(s_th, 1)
                    nc.scalar.mul(xh[:, m % 2], pre[:, m % 2], 0.5).then_inc(s_pact, 1)

            def dt_low_copy(i):
                act.wait_ge(s_pre, 8 * i + 3)
                wait(act, s_pre, i, 8, -2)
                nc.scalar.copy(dtl[:], pre[0:R, 0]).then_inc(s_pact, 1)

            def bc_parts(i):
                act.wait_ge(s_pre, 8 * i + 4)
                here = bass.ds((i % 2) * L, L)
                nc.scalar.copy(bcs[:, here], pre[0:96, 1]).then_inc(s_bc1, 1)
                act.wait_ge(s_bcr, i + 1)
                for q in (1, 2):
                    nc.scalar.copy(bcs[32 * q:32 * q + 32, here], r1[32 * q:32 * q + 32]).then_inc(s_bc2, 1)

            def dt_exps(i, h):
                act.wait_ge(s_pre, 8 * i + 5 + h)
                wait(act, s_dl, i, 1, 0)
                b = bdt[:, h:h + 1]
                nc.scalar.activation(av[:, h], pre[:, h], ACT.Abs, bias=b).then_inc(s_v, 1)
                nc.scalar.activation(rv[:, h], pre[:, h], ACT.Relu, bias=b).then_inc(s_pact, 1)
                act.wait_ge(s_v, 4 * i + 2 * h + 1)
                nc.scalar.activation(ey[:, h], av[:, h], ACT.Exp, scale=-1.0).then_inc(s_v, 1)

            def dt_square(i, k):
                act.wait_ge(s_v, 4 * i + 4)
                wait(act, s_dl, i, 1, 0)
                nc.scalar.activation(sq[:, k], ey[:], ACT.Square, bias=a_bias[k][:, 0:1]).then_inc(s_sq, 1)

            def state(i, n):
                act.wait_ge(s_dl, i + 1)
                for h in range(H):
                    wait(act, s_h, i, H * N, H * (n - 1) + h + 1)
                    act.sem_inc(s_gate, 1)
                    nc.scalar.activation(pA[:, h], at(delta, i, off=h * L), ACT.Exp,
                                         scale=aneg[:, h, n:n + 1]).then_inc(s_a, 1)
                wait(act, s_cc, i, N, n + 1)
                wait(act, s_hc, i, N, n - 1)
                nc.scalar.copy(cs[:, n % 2], pC[:]).then_inc(s_cs, 1)
                if n + 1 in POOL_B:
                    k = POOL_B.index(n + 1)
                    wait(act, s_bb, i, N, n + 2)
                    wait(act, s_pb, i, NPB, k)
                    nc.scalar.copy(bs[:], pB[:]).then_inc(s_bs, 1)

            def body(i, last=False):
                for n in range(N):
                    state(i, n)
                    if last:
                        continue
                    if n in (2, 4):
                        silu_in(i + 1, n // 2 - 1)
                    if n == 6:
                        dt_low_copy(i + 1)
                    if n == 7:
                        bc_parts(i + 1)
                    if n in (8, 9):
                        dt_exps(i + 1, n - 8)
                    if n in (10, 11):
                        dt_square(i + 1, 2 * (n - 10))
                        dt_square(i + 1, 2 * (n - 10) + 1)
                    if n in (12, 13):
                        silu_in(i + 1, n - 10)

            for m in range(2):
                silu_in(0, m)
            dt_low_copy(0)
            bc_parts(0)
            for h in range(H):
                dt_exps(0, h)
            for k in range(4):
                dt_square(0, k)
            for m in range(2, 4):
                silu_in(0, m)
            body(0)
            with act.Fori(1, NS - 1) as i:
                body(i)
            body(NS - 1, last=True)

        @block.vector
        def _(dve):
            for k in range(4):
                nc.vector.memset(a_bias[k][:], quad[k][0]).then_inc(s_z, 1)

            def token_stats(s):
                for t in range(T):
                    nc.vector.bn_stats(stats[:, t], xall[:, bass.ds(s * T + t, 1)].rearrange("p o d -> p (o d)")).then_inc(s_st, 1)
                dve.wait_ge(s_st, T * s + T)
                dve.sem_inc(s_gate, 1)
                for t in range(T):
                    nc.vector.bn_aggr(mv[:, t], stats[:, t]).then_inc(s_mv, 1)
                dve.wait_ge(s_mv, T * s + T)
                nc.vector.tensor_copy(mean[:, bass.ds(s * T, T)], mv[:, :, 0]).then_inc(s_mean, 1)
                nc.vector.tensor_scalar(ve[:, bass.ds(s * T, T)], mv[:, :, 1], EPS, None, ALU.add).then_inc(s_ve, 1)

            for q in range(XL):
                dve.wait_ge(s_x[q], 16)
                with dve.Fori(q * NS // XL, (q + 1) * NS // XL) as s:
                    token_stats(s)
            dve.wait_ge(s_w, 16 * NWL)
            for k in range(KC):
                nc.vector.tensor_tensor(wtap[:, k], win[:, 0:DI], cwb[:, :, k], ALU.mult).then_inc(s_prep, 1)
            for j in range(3):
                nc.vector.tensor_copy(wbc[:, :, j], wx[:, :, R:R + 2 * N]).then_inc(s_prep, 1)

            def normalise(s, k):
                dve.wait_ge(s_rs, s + 1)
                dve.wait_ge(s_mean, s + 1)
                wait(dve, s_tp, s, T, -T)
                for t in range(T):
                    g = bass.ds(s * T + t, 1)
                    nc.vector.tensor_scalar(xn[:, k, t], xall[:, g].rearrange("p o d -> p (o d)"),
                                            mean[:, g], rstd[:, g], ALU.subtract, ALU.mult).then_inc(s_xn, 1)

            for k in range(2):
                normalise(k, k)
            with dve.Fori(1, NS // 2) as s2:
                for k in range(2):
                    normalise(2 * s2 + k, k)

            def silu(i, m):
                dve.wait_ge(s_th, 4 * i + m + 1)
                dve.wait_ge(s_pact, 7 * i + (m + 1 if m < 2 else m + 4))
                if m >= 2:
                    wait(dve, s_yg, i, 1, -1)
                else:
                    wait(dve, s_yd, i, H, -H)
                dst = at(u if m < 2 else zs, i, off=(m % 2) * L)
                nc.vector.scalar_tensor_tensor(dst, th[:, m % 2], 1.0, xh[:, m % 2], ALU.add,
                                               ALU.mult).then_inc(s_silu, 1)

            def bc_residual(i):
                dve.wait_ge(s_bc1, i + 1)
                wait(dve, s_bc, i, 1, 0)
                nc.vector.tensor_tensor(r1[:], pre[0:96, 1], bcs[:, bass.ds((i % 2) * L, L)],
                                        ALU.subtract).then_inc(s_bcr, 1)

            def bc_last(i):
                dve.wait_ge(s_bc2, 2 * i + 2)
                here = bass.ds((i % 2) * L, L)
                nc.vector.tensor_tensor(bcs[64:96, here], r1[64:96], bcs[64:96, here], ALU.subtract).then_inc(s_bc, 1)

            def dt_poly(i, k):
                dve.wait_ge(s_sq, 4 * i + k + 1)
                if k:
                    dve.wait_ge(s_qa, 4 * i + k)
                nc.vector.scalar_tensor_tensor(sq[:, k], sq[:, k], quad[k][1], ey[:] if k == 0 else sq[:, k - 1],
                                               ALU.add, ALU.mult).then_inc(s_qa, 1)
                if k == 3:
                    dve.wait_ge(s_qa, 4 * i + 4)
                    dve.wait_ge(s_pact, 7 * i + 5)
                    nc.vector.scalar_tensor_tensor(at(delta, i, width=H * L), sq[:, 3].rearrange("p h t -> p (h t)"),
                                                   lead, rv[:].rearrange("p h t -> p (h t)"), ALU.mult,
                                                   ALU.add).then_inc(s_dl, 1)

            def y_skip(i):
                dve.wait_ge(s_hu, N * (i + 1))
                wait(dve, s_yg, i, 1, 0)
                for h in range(H):
                    nc.vector.scalar_tensor_tensor(yd[:, h], at(u, i, off=h * L), dsk[:, h:h + 1], pY[:, h],
                                                   ALU.mult, ALU.add).then_inc(s_yd, 1)

            def residual(i):
                dve.wait_ge(s_o, i + 1)
                nc.vector.scalar_tensor_tensor(ro[:].rearrange("p t d -> p (t d)"),
                                               xall[:, bass.ds(i * T, T)].rearrange("p t d -> p (t d)"), 2.0, pre[:, 0],
                                               ALU.mult, ALU.add).then_inc(s_r, 1)
                dve.wait_ge(s_r, i + 1)
                for t in range(T):
                    nc.vector.bn_stats(st2[:, t], ro[:, t]).then_inc(s_st2, 1)
                dve.wait_ge(s_st2, T * (i + 1))
                dve.sem_inc(s_gate, 1)
                for t in range(T):
                    nc.vector.bn_aggr(mv2[:, t], st2[:, t]).then_inc(s_mv2, 1)
                dve.wait_ge(s_mv2, T * (i + 1))
                nc.vector.tensor_scalar(ve2[:], mv2[:, :, 1], EPS, None, ALU.add).then_inc(s_ve2, 1)

            def normalise_out(i):
                dve.wait_ge(s_rs2, i + 1)
                wait(dve, s_x1d, i, 16 * GT, 0)
                for t in range(T):
                    nc.vector.tensor_scalar(x1[:, t], ro[:, t], mv2[:, t, 0:1], rstd2[:, t:t + 1], ALU.subtract,
                                            ALU.mult).then_inc(s_x1, 1)

            def state(i, n):
                if n not in POOL_B:
                    k = VEC_B.index(n)
                    dve.wait_ge(s_bb, N * i + n + 1)
                    if k == 0:
                        dve.wait_ge(s_du, i + 1)
                    nc.vector.tensor_tensor(bt[:, n % 2], at(dtu, i, width=H * L).rearrange("p (h t) -> p h t", h=H),
                                            pB[:].unsqueeze(1).to_broadcast([P, H, L]), ALU.mult).then_inc(s_db, 1)
                    dve.wait_ge(s_db, NVB * i + k + 1)
                else:
                    dve.wait_ge(s_pb, NPB * i + POOL_B.index(n) + 1)
                wait(dve, s_hc, i, N, n - 3)
                for h in range(H):
                    dve.wait_ge(s_a, H * N * i + H * n + h + 1)
                    nc.vector.tensor_tensor_scan(hb[:, n % 4, h], pA[:, h], bt[:, n % 2, h], 0.0, ALU.mult,
                                                 ALU.add).then_inc(s_h, 1)

            def body(i, first=False, last=False):
                for n in range(N):
                    state(i, n)
                    if not first:
                        if n == 2:
                            y_skip(i - 1)
                        if n == 10:
                            residual(i - 1)
                        if n == 12:
                            normalise_out(i - 1)
                    if not last:
                        if n in (3, 5):
                            silu(i + 1, (n - 3) // 2)
                        if n == 7:
                            bc_residual(i + 1)
                        if n == 8:
                            bc_last(i + 1)
                        if n in (11, 12):
                            dt_poly(i + 1, 2 * (n - 11))
                            dt_poly(i + 1, 2 * (n - 11) + 1)
                        if n in (13, 14):
                            silu(i + 1, n - 11)

            silu(0, 0)
            silu(0, 1)
            bc_residual(0)
            bc_last(0)
            for k in range(4):
                dt_poly(0, k)
            silu(0, 2)
            silu(0, 3)
            body(0, first=True)
            with dve.Fori(1, NS - 1) as i:
                body(i)
            body(NS - 1, last=True)
            y_skip(NS - 1)
            residual(NS - 1)
            normalise_out(NS - 1)

        @block.tensor
        def _(pe):
            pe.wait_ge(s_id, 8)

            def transposes(s, k):
                wait(pe, s_xT, s, 1, -1)
                for t in range(T):
                    pe.wait_ge(s_xn, T * s + t + 1)
                    nc.tensor.transpose(pre[:, k, t * P:(t + 1) * P], xn[:, k, t], ident[:]).then_inc(s_tp, 1)

            for k in range(2):
                transposes(k, k)
            with pe.Fori(1, NS // 2) as s2:
                for k in range(2):
                    transposes(2 * s2 + k, k)
            pe.wait_ge(s_xT, NS)
            pe.wait_ge(s_prep, KC + 3)

            def tokens(i, k=0):
                return xnT[:, bass.ds(i, 1), k:k + L].rearrange("p o t -> p (o t)")

            def conv(i, h, taps):
                if 0 in taps:
                    wait(pe, s_pact, i, 7, h - 1)
                for k in taps:
                    mm = nc.tensor.matmul(pre[:, h], wtap[:, k, h * P:(h + 1) * P], tokens(i, k), start=(k == 0),
                                          stop=(k == KC - 1))
                if KC - 1 in taps:
                    mm.then_inc(s_pre, 1)

            def x_proj(i, bank):
                pe.wait_ge(s_silu, 4 * i + 2)
                pe.wait_ge(s_pact, 7 * i + 1 + bank)
                for h in range(H):
                    rows_of, w = (R, wx[:, h, 0:R]) if bank == 0 else (96, wbc[:, h].rearrange("p j n -> p (j n)"))
                    mm = nc.tensor.matmul(pre[0:rows_of, bank], w, at(u, i, off=h * L), start=(h == 0),
                                          stop=(h == H - 1))
                mm.then_inc(s_pre, 1)

            def dt_proj(i, h):
                pe.wait_ge(s_pact, 7 * i + 3)
                if h == 1:
                    pe.wait_ge(s_bcr, i + 1)
                nc.tensor.matmul(pre[:, h], wdt[:, h * P:(h + 1) * P], dtl[:], start=True, stop=True).then_inc(s_pre, 1)

            def z_proj(i, h):
                if h == 0:
                    wait(pe, s_r, i, 1, -1)
                pe.wait_ge(s_pact, 7 * i + 4 + h)
                nc.tensor.matmul(pre[:, h], win[:, DI + h * P:DI + (h + 1) * P], tokens(i, KC - 1), start=True,
                                 stop=True).then_inc(s_pre, 1)

            def out_proj(i, free):
                pe.wait_ge(s_yg, i + 1)
                pe.wait_ge(*free)
                for t in range(T):
                    for h in range(H):
                        mm = nc.tensor.matmul(pre[:, 0, t * P:(t + 1) * P], yg[:, h, t * P:(t + 1) * P], wout[:, h],
                                              start=(h == 0), stop=(h == H - 1))
                mm.then_inc(s_o, 1)

            def rows(i, n):
                here = bass.ds((i % 2) * L, L)
                if n == 0:
                    pe.wait_ge(s_bc, i + 1)
                m = (n - 1) % N
                j = i if n else i - 1
                if not (isinstance(j, int) and j < 0):
                    if m in POOL_B:
                        pe.wait_ge(s_bs, NPB * j + POOL_B.index(m) + 1)
                    else:
                        pe.wait_ge(s_db, NVB * j + VEC_B.index(m) + 1)
                nc.tensor.matmul(pB[:], sel[:, n], bcs[:, here], start=True, stop=True).then_inc(s_bb, 1)
                wait(pe, s_cs, i, N, n)
                nc.tensor.matmul(pC[:], sel[:, N + n], bcs[:, here], start=True, stop=True).then_inc(s_cc, 1)

            def sum_states(i, n):
                pe.wait_ge(s_hc, N * i + n + 1)
                if n == 0:
                    wait(pe, s_yd, i, H, 0)
                for h in range(H):
                    mm = nc.tensor.matmul(pY[:, h], ident[:], hc[:, n % 2, h], start=(n == 0), stop=(n == N - 1))
                mm.then_inc(s_hu, 1)

            def body(i, first=False, last=False):
                for n in range(N):
                    if n < N - 1:
                        rows(i, n + 1)
                    elif not last:
                        rows(i + 1, 0)
                    if n >= LAG:
                        sum_states(i, n - LAG)
                    elif not first:
                        sum_states(i - 1, N + n - LAG)
                    if not last:
                        if n < 4:
                            conv(i + 1, n // 2, range(KC // 2) if n % 2 == 0 else range(KC // 2, KC))
                        if n in (5, 6):
                            x_proj(i + 1, n - 5)
                        if n in (7, 8):
                            dt_proj(i + 1, n - 7)
                    if n == 9 and not first:
                        out_proj(i - 1, (s_pact, 7 * (i + 1) + 4) if not last else (s_pact, 7 * NS))
                    if n in (11, 12) and not last:
                        z_proj(i + 1, n - 11)

            for h in range(H):
                conv(0, h, range(KC))
            for h in range(2):
                x_proj(0, h)
            for h in range(H):
                dt_proj(0, h)
            for h in range(H):
                z_proj(0, h)
            rows(0, 0)
            body(0, first=True)
            with pe.Fori(1, NS - 1) as i:
                body(i)
            body(NS - 1, last=True)
            for n in range(N - LAG, N):
                sum_states(NS - 1, n)
            out_proj(NS - 1, (s_r, NS - 1))

I32 = mybir.dt.int32
U32 = mybir.dt.uint32
BIG = 2.0 ** 100


def wait_if(eng, s, i, per, c):
    if isinstance(i, int) and i * per + c <= 0:
        return
    eng.wait_ge(s, i * per + c)


def build_attention(nc, shared, x1_d, Wqkv, bqkv, Wo, bo, g1, be1, g2, be2, Wg, W1, b1, W2, b2, y_d):
    NG = x1_d.shape[0]
    DM = x1_d.shape[2]
    E = Wg.shape[0]
    G = 2
    NQ = NG // G
    S = 8
    TT = P // S
    HD = 32
    NH = DM // HD
    SCALE = 1.0 / float(np.sqrt(HD))
    T = G * P
    C = HD + 1
    yall, lg = shared["yall"], shared["lg"]

    with ExitStack() as ctx:
        def sb(name, shape, dt=F32):
            return ctx.enter_context(nc.sbuf_tensor(name, shape, dt))

        def ps(name, shape, dt=F32):
            return ctx.enter_context(nc.psum_tensor(name, shape, dt))

        def sem(name):
            return ctx.enter_context(nc.semaphore(name))

        s_gate = sem("a_gate_passed")
        ident = sb("a_ident", [P, P])
        identb = sb("a_identb", [P, P], BF16)
        mask = sb("a_mask", [P, G, P], BF16)
        mhalf = sb("a_mhalf", [P, G])
        wnat = sb("a_wnat", [P, 4, DM])
        wgn = sb("a_wgn", [E, DM])
        wT = sb("a_wT", [P, 4, DM])
        wgT = sb("a_wgT", [P, E])
        bq = sb("a_bq", [P, 3])
        bqs = sb("a_bqs", [P, 1])
        bor = sb("a_bor", [1, DM])
        cst = sb("a_cst", [1, DM])
        cstb = sb("a_cstb", [P, DM])
        ones = sb("a_ones", [1, P])
        g1b = sb("a_g1b", [P, DM])
        be1b = sb("a_be1b", [P, DM])
        xg = sb("a_xg", [P, 2, G, DM])
        xb = sb("a_xb", [P, 2, G, DM])
        xT = sb("a_xT", [P, T])
        qT = sb("a_qT", [P, T])
        kT = sb("a_kT", [P, T])
        v = sb("a_v", [P, 2, G, NH, C])
        mx = sb("a_mx", [P, NH, G])
        sh = sb("a_sh", [P, NH, T])
        pr = sb("a_pr", [P, NH, T])
        prT = sb("a_prT", [P, NH, T])
        rin = sb("a_rin", [P, G * NH])
        on = sb("a_on", [P, G, DM])
        oT = sb("a_oT", [P, T])
        ro = sb("a_ro", [P, G, DM])
        st = sb("a_st", [P, G, 6])
        mv = sb("a_mv", [P, G, 2])
        ve = sb("a_ve", [P, G])
        rs = sb("a_rs", [P, G])
        yn = sb("a_yn", [P, G, DM])
        ym = sb("a_ym", [P, G, DM])
        yq = sb("a_yq", [P, G, DM])
        yT = sb("a_yT", [P, T])

        pS = ps("a_pS", [P, NH, 2, T])
        pA = ps("a_pA", [P, 2, T])
        pV = ps("a_pV", [P, 512])
        pO = ps("a_pO", [P, 512])
        pB = ps("a_pB", [P, 512])

        s_w = sem("a_weights")
        s_mk = sem("a_masks")
        s_wt = sem("a_w_transposed")
        s_wc = sem("a_w_copied")
        s_cp = sem("a_const_psum")
        s_cc = sem("a_const_ready")
        s_xg = [sem("a_x_loaded0"), sem("a_x_loaded1")]
        s_xb = sem("a_x_with_const")
        s_xt = sem("a_x_transposed")
        s_xtc = sem("a_xT_copied")
        s_qk = sem("a_qk_ready")
        s_qkc = sem("a_qk_copied")
        s_v = sem("a_v_ready")
        s_vc = sem("a_v_copied")
        s_sc = sem("a_scores_ready")
        s_mx = sem("a_max_ready")
        s_sh = sem("a_shifted")
        s_ex = sem("a_exp_ready")
        s_pt = sem("a_probs_transposed")
        s_pta = sem("a_probsT_copied_act")
        s_ptd = sem("a_probsT_copied_dve")
        s_o = sem("a_o_ready")
        s_rin = sem("a_recip_ready")
        s_on = sem("a_o_normalised")
        s_ot = sem("a_o_transposed")
        s_otc = sem("a_oT_copied")
        s_po = sem("a_out_ready")
        s_out = sem("a_out_read")
        s_st = sem("a_stats")
        s_mv = sem("a_meanvar")
        s_ve = sem("a_vareps")
        s_rs = sem("a_rstd")
        s_yn = sem("a_normalised")
        s_ym = sem("a_scaled")
        s_y = sem("a_y_ready")
        s_ya = sem("a_y_kept")
        s_yt = sem("a_y_transposed")
        s_ytc = sem("a_yT_copied")
        s_l = sem("a_logits_ready")
        s_lc = sem("a_logits_copied")
        NW = 7

        block = ctx.enter_context(nc.Block())

        def steps(eng, step):
            for k in range(2):
                step(k, k, 0, True, k >= 1, False)
            with eng.Fori(1, NQ // 2) as q2:
                for k in range(2):
                    step(2 * q2 + k, k, q2, True, True, True)
            for k in range(2):
                step(NQ + k, k, NQ // 2, False, k == 0, True)

        @block.sync
        def _(sp):
            with nc.allow_non_contiguous_dma(reason="small weights"):
                sp.dma_start(wnat[:, 0:3, :], Wqkv.rearrange("(j p) d -> p j d", p=P)).then_inc(s_w, 16)
                sp.dma_start(wnat[:, 3, :], Wo).then_inc(s_w, 16)
                sp.dma_start(wgn[:], Wg).then_inc(s_w, 16)
                sp.dma_start(bq[:], bqkv.rearrange("(j p) -> p j", p=P)).then_inc(s_w, 16)
                sp.dma_start(bor[:], bo.rearrange("(o d) -> o d", o=1)).then_inc(s_w, 16)
                sp.dma_start(g1b[:], g1.rearrange("(o d) -> o d", o=1).broadcast_to([P, DM])).then_inc(s_w, 16)
                sp.dma_start(be1b[:], be1.rearrange("(o d) -> o d", o=1).broadcast_to([P, DM])).then_inc(s_w, 16)

            def load(i, k):
                wait_if(sp, s_xt, i, 1, -1)
                wait_if(sp, s_xb, i, 1, -1)
                sp.dma_start(xg[:, k], x1_d[bass.ds(i * G, G)].rearrange("g p d -> p g d")).then_inc(s_xg[k], 16)

            for k in range(2):
                load(k, k)
            with sp.Fori(1, NQ // 2) as q2:
                for k in range(2):
                    load(2 * q2 + k, k)

        @block.gpsimd
        def _(pool):
            nc.gpsimd.memset(ident[:], 0.0).then_inc(s_mk, 1)
            nc.gpsimd.memset(mask[:], -BIG).then_inc(s_mk, 1)
            nc.gpsimd.memset(mhalf[:], -0.5).then_inc(s_mk, 1)
            nc.gpsimd.memset(ones[:], 1.0).then_inc(s_mk, 1)
            nc.gpsimd.memset(v[:, :, :, :, HD:C], 1.0).then_inc(s_mk, 1)
            pool.wait_ge(s_mk, 5)
            nc.gpsimd.affine_select(out=ident[:], in_=ident[:], compare_op=ALU.not_equal, fill=1.0, base=0,
                                    pattern=[[-1, P]], channel_multiplier=1).then_inc(s_mk, 1)
            pool.wait_ge(s_mk, 6)
            nc.gpsimd.tensor_copy(identb[:], ident[:]).then_inc(s_mk, 1)
            for d in range(-(S - 1), S):
                nc.gpsimd.affine_select(out=mask[:], in_=mask[:], compare_op=ALU.not_equal, fill=0.0, base=TT * d,
                                        pattern=[[0, G], [-1, P]], channel_multiplier=1).then_inc(s_mk, 1)
                pool.wait_ge(s_mk, 8 + d + S - 1)
            pool.wait_ge(s_cc, 3)

            def step(i, k, q2, first, second, third):
                if first:
                    pool.wait_ge(s_xg[k], 16 * q2 + 16)
                    wait_if(pool, s_out, i, 1, -1)
                    nc.gpsimd.tensor_tensor(xb[:, k], xg[:, k], cstb[:].unsqueeze(1).to_broadcast([P, G, DM]),
                                            ALU.add).then_inc(s_xb, 1)
                if second:
                    pool.wait_ge(s_ve, i)
                    nc.gpsimd.tensor_tensor(rs[:], ve[:], mhalf[:], ALU.pow).then_inc(s_rs, 1)
                    pool.wait_ge(s_yn, i * G)
                    nc.gpsimd.tensor_tensor(ym[:], yn[:], g1b[:].unsqueeze(1).to_broadcast([P, G, DM]),
                                            ALU.mult).then_inc(s_ym, 1)
                    pool.wait_ge(s_ym, i)
                    wait_if(pool, s_yt, i, 1, -1)
                    wait_if(pool, s_ya, i, 1, -1)
                    nc.gpsimd.tensor_tensor(yq[:], ym[:], be1b[:].unsqueeze(1).to_broadcast([P, G, DM]),
                                            ALU.add).then_inc(s_y, 1)

            steps(pool, step)

        NMK = 7 + 2 * S - 1

        @block.scalar
        def _(act):
            act.wait_ge(s_w, 16 * NW)
            nc.scalar.mul(bqs[:], bq[:, 0:1], SCALE).then_inc(s_cc, 1)
            act.wait_ge(s_wt, 4)
            nc.scalar.copy(wT[:].rearrange("p j d -> p (j d)"), pO[:]).then_inc(s_wc, 1)
            act.wait_ge(s_wt, 5)
            nc.scalar.copy(wgT[:], pV[:, 0:E]).then_inc(s_wc, 1)
            act.wait_ge(s_cp, 2)
            nc.scalar.copy(cstb[:], pB[:, 0:DM]).then_inc(s_cc, 1)
            act.wait_ge(s_cc, 3)

            def step(i, k, q2, first, second, third):
                if first:
                    act.wait_ge(s_xt, i + 1)
                    wait_if(act, s_v, i, 1, 0)
                    nc.scalar.copy(xT[:], pB[:, 0:T]).then_inc(s_xtc, 1)
                if second:
                    act.wait_ge(s_pt, i)
                    wait_if(act, s_o, i, 1, -1)
                    nc.scalar.copy(prT[:, 0:2], pS[:, 0:2, 1]).then_inc(s_pta, 1)
                if first:
                    act.wait_ge(s_qk, i + 1)
                    wait_if(act, s_sc, i, 1, 0)
                    nc.scalar.activation(qT[:], pA[:, 0], ACT.Identity, bias=bqs[:, 0:1], scale=SCALE).then_inc(s_qkc, 1)
                    nc.scalar.activation(kT[:], pA[:, 1], ACT.Identity, bias=bq[:, 1:2]).then_inc(s_qkc, 1)
                if third:
                    act.wait_ge(s_yt, i - 1)
                    wait_if(act, s_l, i, 1, -2)
                    nc.scalar.copy(yT[:], pB[:, 0:T]).then_inc(s_ytc, 1)
                    nc.scalar.copy(yall[:, bass.ds((i - 2) * G, G)], yq[:]).then_inc(s_ya, 1)
                if second:
                    act.wait_ge(s_ot, i)
                    wait_if(act, s_po, i, 1, -1)
                    nc.scalar.copy(oT[:], pB[:, 0:T]).then_inc(s_otc, 1)
                if first:
                    act.wait_ge(s_sh, i + 1)
                    wait_if(act, s_pt, i, 1, 0)
                    nc.scalar.activation(pr[:], sh[:], ACT.Exp).then_inc(s_ex, 1)

            steps(act, step)

        @block.vector
        def _(dve):
            dve.wait_ge(s_cp, 1)
            nc.vector.tensor_tensor(cst[:], pV[0:1, 256:256 + DM], bor[:], ALU.add).then_inc(s_cc, 1)
            dve.wait_ge(s_mk, NMK)

            def step(i, k, q2, first, second, third):
                if second:
                    dve.wait_ge(s_pt, i)
                    wait_if(dve, s_o, i, 1, -1)
                    nc.vector.tensor_copy(prT[:, 2:4], pS[:, 2:4, 1]).then_inc(s_ptd, 1)
                if first:
                    dve.wait_ge(s_v, i + 1)
                    wait_if(dve, s_o, i, 1, -1)
                    nc.vector.tensor_copy(v[:, k, :, :, 0:HD],
                                          pV[:, 0:T].rearrange("p (g h d) -> p g h d", g=G, h=NH)).then_inc(s_vc, 1)
                if second:
                    dve.wait_ge(s_o, i)
                    o3 = pO[:, 0:G * NH * C].rearrange("p (g d) -> p g d", d=C)
                    nc.vector.reciprocal(rin[:], o3[:, :, HD]).then_inc(s_rin, 1)
                    dve.wait_ge(s_rin, i)
                    wait_if(dve, s_ot, i, 1, -1)
                    nc.vector.tensor_tensor(on[:].rearrange("p g (h d) -> p (g h) d", h=NH), o3[:, :, 0:HD],
                                            rin[:].unsqueeze(2).to_broadcast([P, G * NH, HD]), ALU.mult).then_inc(s_on, 1)
                if first:
                    dve.wait_ge(s_sc, i + 1)
                    view = pS[:, :, 0].rearrange("p h (g k) -> p h g k", g=G)
                    nc.vector.tensor_reduce(mx[:], view, AX.X, ALU.max).then_inc(s_mx, 1)
                    dve.wait_ge(s_mx, i + 1)
                    wait_if(dve, s_ex, i, 1, 0)
                    nc.vector.tensor_tensor(sh[:].rearrange("p h (g k) -> p h g k", g=G), view,
                                            mx[:].unsqueeze(3).to_broadcast([P, NH, G, P]), ALU.subtract).then_inc(s_sh, 1)
                if third:
                    dve.wait_ge(s_l, i - 1)
                    nc.vector.tensor_copy(lg[:, bass.ds((i - 2) * G, G)],
                                          pV[:, T:T + G * E].rearrange("p (g e) -> p g e", g=G)).then_inc(s_lc, 1)
                if second:
                    dve.wait_ge(s_po, i)
                    dve.wait_ge(s_xb, i)
                    nc.vector.tensor_tensor(ro[:].rearrange("p g d -> p (g d)"), pO[:, 0:T],
                                            xb[:, 1 - k].rearrange("p g d -> p (g d)"), ALU.add).then_inc(s_out, 1)
                    dve.wait_ge(s_out, i)
                    for t in range(G):
                        nc.vector.bn_stats(st[:, t], ro[:, t]).then_inc(s_st, 1)
                    dve.wait_ge(s_st, i * G)
                    dve.sem_inc(s_gate, 1)
                    for t in range(G):
                        nc.vector.bn_aggr(mv[:, t], st[:, t]).then_inc(s_mv, 1)
                    dve.wait_ge(s_mv, i * G)
                    nc.vector.tensor_scalar(ve[:], mv[:, :, 1], EPS, None, ALU.add).then_inc(s_ve, 1)
                    dve.wait_ge(s_rs, i)
                    wait_if(dve, s_ym, i, 1, -1)
                    for t in range(G):
                        nc.vector.tensor_scalar(yn[:, t], ro[:, t], mv[:, t, 0:1], rs[:, t:t + 1], ALU.subtract,
                                                ALU.mult).then_inc(s_yn, 1)

            steps(dve, step)

        @block.tensor
        def _(pe):
            pe.wait_ge(s_w, 16 * NW)
            pe.wait_ge(s_mk, NMK)
            for j in range(4):
                nc.tensor.transpose(pO[:, j * P:(j + 1) * P], wnat[:, j], ident[:]).then_inc(s_wt, 1)
            nc.tensor.transpose(pV[:, 0:E], wgn[:], ident[0:E, 0:E]).then_inc(s_wt, 1)
            pe.wait_ge(s_wc, 2)
            nc.tensor.matmul(pV[0:1, 256:256 + DM], bq[:, 2:3], wT[:, 3], start=True, stop=True).then_inc(s_cp, 1)
            pe.wait_ge(s_cc, 2)
            nc.tensor.matmul(pB[:, 0:DM], ones[0:1, :], cst[0:1, :], start=True, stop=True).then_inc(s_cp, 1)
            pe.wait_ge(s_cc, 3)

            def step(i, k, q2, first, second, third):
                if first:
                    pe.wait_ge(s_xg[k], 16 * q2 + 16)
                    wait_if(pe, s_otc, i, 1, -1)
                    for g in range(G):
                        mm = nc.tensor.transpose(pB[:, g * P:(g + 1) * P], xg[:, k, g], ident[:])
                    mm.then_inc(s_xt, 1)
                if second:
                    pe.wait_ge(s_ex, i)
                    for h in range(NH):
                        for g in range(G):
                            mm = nc.tensor.transpose(pS[:, h, 1, g * P:(g + 1) * P], pr[:, h, g * P:(g + 1) * P], ident[:])
                    mm.then_inc(s_pt, 1)
                if first:
                    pe.wait_ge(s_xtc, i + 1)
                    wait_if(pe, s_qkc, i, 2, 0)
                    for j in range(2):
                        mm = nc.tensor.matmul(pA[:, j], wT[:, j], xT[:], start=True, stop=True)
                    mm.then_inc(s_qk, 1)
                    wait_if(pe, s_vc, i, 1, 0)
                    wait_if(pe, s_lc, i, 1, -2)
                    for g in range(G):
                        mm = nc.tensor.matmul(pV[:, g * P:(g + 1) * P], xT[:, g * P:(g + 1) * P], wT[:, 2], start=True,
                                              stop=True)
                    mm.then_inc(s_v, 1)
                if second:
                    pe.wait_ge(s_pta, i)
                    pe.wait_ge(s_ptd, i)
                    wait_if(pe, s_out, i, 1, -1)
                    for g in range(G):
                        for h in range(NH):
                            c = (g * NH + h) * C
                            mm = nc.tensor.matmul(pO[:, c:c + C], prT[:, h, g * P:(g + 1) * P], v[:, 1 - k, g, h],
                                                  start=True, stop=True)
                    mm.then_inc(s_o, 1)
                if third:
                    pe.wait_ge(s_y, i - 1)
                    if not first:
                        pe.wait_ge(s_otc, i - 1)
                    for g in range(G):
                        mm = nc.tensor.transpose(pB[:, g * P:(g + 1) * P], yq[:, g], ident[:])
                    mm.then_inc(s_yt, 1)
                if first:
                    pe.wait_ge(s_qkc, 2 * i + 2)
                    wait_if(pe, s_sh, i, 1, 0)
                    for h in range(NH):
                        nc.tensor.matmul(pS[:, h, 0], identb[:], mask[:].rearrange("p g k -> p (g k)"), start=True,
                                         stop=False, skip_group_check=True)
                    for g in range(G):
                        for h in range(NH):
                            c = slice(g * P, (g + 1) * P)
                            hh = slice(h * HD, (h + 1) * HD)
                            mm = nc.tensor.matmul(pS[:, h, 0, c], qT[hh, c], kT[hh, c], start=False, stop=(g == G - 1),
                                                  skip_group_check=True, tile_position=(h * HD, 0))
                    mm.then_inc(s_sc, 1)
                if third:
                    pe.wait_ge(s_ytc, i - 1)
                    if first:
                        pe.wait_ge(s_vc, i + 1)
                    else:
                        wait_if(pe, s_lc, i, 1, -2)
                    for g in range(G):
                        mm = nc.tensor.matmul(pV[:, T + g * E:T + (g + 1) * E], yT[:, g * P:(g + 1) * P], wgT[:], start=True,
                                              stop=True)
                    mm.then_inc(s_l, 1)
                if second:
                    if not third:
                        pe.wait_ge(s_xtc, i + 1)
                    pe.wait_ge(s_on, i)
                    for g in range(G):
                        mm = nc.tensor.transpose(pB[:, g * P:(g + 1) * P], on[:, g], ident[:])
                    mm.then_inc(s_ot, 1)
                    pe.wait_ge(s_otc, i)
                    for g in range(G):
                        c = slice(g * P, (g + 1) * P)
                        mm = nc.tensor.matmul(pO[:, c], oT[:, c], wT[:, 3], start=True, stop=True)
                    mm.then_inc(s_po, 1)

            steps(pe, step)


def build_moe(nc, shared, x1_d, g2, be2, W1, b1, W2, b2, ysort_d, osort_d, out):
    NG, _, DM = x1_d.shape
    E, _, DF = W1.shape
    NT = ysort_d.shape[0] // P
    NB = DF // P
    S = out.shape[0]
    TT = P // S
    G = 4
    NQ = NG // G
    yall, lg = shared["yall"], shared["lg"]
    w1, w2, b1b, b2b = shared["w1"], shared["w2"], shared["b1b"], shared["b2b"]
    s_ew = shared["s_ew"]
    s_zf = shared["s_zf"]

    with ExitStack() as ctx:
        def sb(name, shape, dt=F32):
            return ctx.enter_context(nc.sbuf_tensor(name, shape, dt))

        def ps(name, shape, dt=F32):
            return ctx.enter_context(nc.psum_tensor(name, shape, dt))

        def sem(name):
            return ctx.enter_context(nc.semaphore(name))

        ident = sb("m_ident", [P, P])
        tri = sb("m_tri", [P, P], BF16)
        onesb = sb("m_onesb", [P, P], BF16)
        mhalf = sb("m_mhalf", [P, G])
        iot_i = sb("m_iota_i", [P, E], I32)
        iot8 = sb("m_iota8", [P, E])
        iot0 = sb("m_iota0", [P, E])
        thr_i = sb("m_thr_i", [P, NG], I32)
        thr = sb("m_thr", [P, NG])
        tl_i = sb("m_tl_i", [P, NT], I32)
        tl = sb("m_tl", [P, NT])
        rst = sb("m_reset", [P, E, NG])
        one8 = sb("m_one8", [P, E])
        mxl = sb("m_mxl", [P, NG])
        eq = sb("m_eq", [P, NG, E])
        cand = sb("m_cand", [P, NG, E])
        idx = sb("m_idx", [P, NG])
        oh = sb("m_oh", [P, NG, E], BF16)
        tot = sb("m_tot", [P, E, NG])
        inc = sb("m_inc", [P, E, NG])
        cmp_ = sb("m_cmp", [P, E, NG])
        nt = sb("m_nt", [P, E])
        ntc = sb("m_ntc", [P, E])
        base = sb("m_base", [P, E])
        place = sb("m_place", [P, NG, E])
        pos = sb("m_pos", [P, NG])
        pos_u = sb("m_pos_u", [P, NG], U32)
        ecmp = sb("m_ecmp", [P, NT, E])
        eid = sb("m_eid", [P, NT])
        eid_i = sb("m_eid_i", [P, NT], I32)
        pidx = sb("m_pidx", [P, 2, G], U32)
        ytile = sb("m_ytile", [P, 2, G, DM])
        ys = sb("m_ys", [P, 2, DM])
        yT = sb("m_yT", [P, 2, P])
        hh = sb("m_hh", [P, 2, DF])
        hT = sb("m_hT", [P, 2, NB, P])
        ob = sb("m_ob", [P, 2, DM])
        gp = sb("m_gp", [P, 2, G], U32)
        gb = sb("m_gb", [P, 2, G, DM])
        xg = sb("m_xg", [P, 2, G, DM])
        g2b = sb("m_g2b", [P, DM])
        be2b = sb("m_be2b", [P, DM])
        ra, rb = [sb(f"m_r{c}", [P, G, DM]) for c in "ab"]
        sta, stb = [sb(f"m_st{c}", [P, G, 6]) for c in "ab"]
        mva, mvb = [sb(f"m_mv{c}", [P, G, 2]) for c in "ab"]
        vea, veb = [sb(f"m_ve{c}", [P, G]) for c in "ab"]
        rsa, rsb = [sb(f"m_rs{c}", [P, G]) for c in "ab"]
        zn = sb("m_zn", [P, G, DM])
        zm = sb("m_zm", [P, G, DM])
        z = sb("m_z", [P, G, DM])
        fo = sb("m_fo", [P, 2, G, DM])

        pR = ps("m_pR", [P, NG * E])
        pT = ps("m_pT", [P, NG * E])
        pY = ps("m_pY", [P, 2, 512])
        pH = ps("m_pH", [P, 2, DF])
        pHT = ps("m_pHT", [P, 2, NB * P])

        s_gate = sem("m_gate_passed")
        s_k = sem("m_consts")
        s_kd = sem("m_dve_consts")
        s_w = sem("m_weights")
        s_c = sem("m_chain")
        s_oh = sem("m_onehot_ready")
        s_rk = sem("m_ranks_ready")
        s_pos = sem("m_positions_ready")
        s_eid = sem("m_expert_ids_ready")
        s_stg = sem("m_scatter_staged")
        s_scs = [sem(f"m_scattered{k}") for k in range(2)]
        s_ysl = [sem(f"m_tile_loaded{k}") for k in range(2)]
        s_ty = sem("m_tile_transposed")
        s_yc = sem("m_tileT_copied")
        s_h = sem("m_hidden_ready")
        s_hb = sem("m_hidden_biased")
        s_ht = sem("m_hidden_transposed")
        s_hc = sem("m_hiddenT_copied")
        s_o = sem("m_out_ready")
        s_ob = sem("m_out_biased")
        s_osd = [sem(f"m_out_stored{k}") for k in range(2)]
        s_gst = sem("m_gather_staged")
        s_g = [sem(f"m_gathered{k}") for k in range(2)]
        s_xg = [sem(f"m_x_loaded{k}") for k in range(2)]
        s_ra, s_rb = [sem(f"m_res_ready_{c}") for c in "ab"]
        s_sta, s_stb = [sem(f"m_stats_{c}") for c in "ab"]
        s_mva, s_mvb = [sem(f"m_meanvar_{c}") for c in "ab"]
        s_vea, s_veb = [sem(f"m_vareps_{c}") for c in "ab"]
        s_rsa, s_rsb = [sem(f"m_rstd_{c}") for c in "ab"]
        s_zn = sem("m_normalised")
        s_zm = sem("m_scaled")
        s_z = sem("m_z_ready")
        s_fo = sem("m_final_ready")
        s_out = [sem(f"m_stored{k}") for k in range(2)]

        block = ctx.enter_context(nc.Block())
        NTP = NT // 2

        @block.sync
        def _(sp):
            sp.dma_start(g2b[:], g2.rearrange("(o d) -> o d", o=1).broadcast_to([P, DM])).then_inc(s_w, 16)
            sp.dma_start(be2b[:], be2.rearrange("(o d) -> o d", o=1).broadcast_to([P, DM])).then_inc(s_w, 16)
            for k in range(2):
                sp.wait_ge(s_scs[k], 16 * (NG // 2))

            def tile(j, k):
                wait_if(sp, s_ty, j, 1, -1)
                sp.dma_start(ys[:, k], ysort_d[bass.ds(j * P, P), :]).then_inc(s_ysl[k], 16)

            for k in range(2):
                tile(k, k)
            with sp.Fori(1, NTP) as n:
                for k in range(2):
                    tile(2 * n + k, k)

            def xload(q, k):
                wait_if(sp, s_rb, q, 1, -1)
                sp.dma_start(xg[:, k], x1_d[bass.ds(q * G, G)].rearrange("g p d -> p g d")).then_inc(s_xg[k], 16)

            def put(q, k):
                sp.wait_ge(s_fo, q + 1)
                for s in range(S):
                    sp.dma_start(out[s, bass.ds(q * G * TT, G * TT), :].rearrange("(g t) d -> t g d", g=G),
                                 fo[s * TT:(s + 1) * TT, k]).then_inc(s_out[k], 16)

            for k in range(2):
                xload(k, k)
            with sp.Fori(1, NQ // 2) as q2:
                for k in range(2):
                    xload(2 * q2 + k, k)
                    put(2 * q2 + k - 2, k)
            for k in range(2):
                put(NQ - 2 + k, k)
            for k in range(2):
                sp.wait_ge(s_out[k], 16 * S * (NQ // 2))

        def final_steps(eng, step):
            for k in range(2):
                step(k, k, 0, True, k >= 1, True)
            with eng.Fori(1, NQ // 2 - 1) as q2:
                for k in range(2):
                    step(2 * q2 + k, k, q2, True, True, True)
            for k in range(2):
                step(NQ - 2 + k, k, NQ // 2 - 1, True, True, False)
            step(NQ, 0, NQ // 2, False, True, False)

        @block.gpsimd
        def _(pool):
            nc.gpsimd.memset(ident[:], 0.0).then_inc(s_k, 1)
            nc.gpsimd.memset(tri[:], 1.0).then_inc(s_k, 1)
            nc.gpsimd.memset(onesb[:], 1.0).then_inc(s_k, 1)
            nc.gpsimd.memset(mhalf[:], -0.5).then_inc(s_k, 1)
            nc.gpsimd.memset(rst[:], 1.0).then_inc(s_k, 1)
            nc.gpsimd.memset(one8[:], 1.0).then_inc(s_k, 1)
            nc.gpsimd.iota(iot_i[:], pattern=[[1, E]], base=0, channel_multiplier=0).then_inc(s_k, 1)
            nc.gpsimd.iota(thr_i[:], pattern=[[P, NG]], base=0, channel_multiplier=0).then_inc(s_k, 1)
            nc.gpsimd.iota(tl_i[:], pattern=[[1, NT]], base=0, channel_multiplier=0).then_inc(s_k, 1)
            pool.wait_ge(s_k, 9)
            nc.gpsimd.affine_select(out=ident[:], in_=ident[:], compare_op=ALU.not_equal, fill=1.0, base=0,
                                    pattern=[[-1, P]], channel_multiplier=1).then_inc(s_k, 1)
            nc.gpsimd.affine_select(out=tri[:], in_=tri[:], compare_op=ALU.is_ge, fill=0.0, base=-1,
                                    pattern=[[1, P]], channel_multiplier=-1).then_inc(s_k, 1)
            nc.gpsimd.memset(rst[:, :, 0:1], 0.0).then_inc(s_k, 1)
            pool.wait_ge(s_pos, 1)
            pool.wait_ge(s_zf, 16)

            with pool.Fori(0, NQ // 2) as q2:
                for k in range(2):
                    pool.wait_ge(s_stg, 4 * q2 + 2 * k + 2)
                    pool.sem_inc(s_gate, 1)
                    for t in range(G):
                        nc.gpsimd.indirect_dma_start(
                            out=ysort_d, out_offset=bass.IndirectOffsetOnAxis(ap=pidx[:, k, t:t + 1], axis=0),
                            in_=ytile[:, k, t], in_offset=None).then_inc(s_scs[k], 16)

            for k in range(2):
                pool.wait_ge(s_osd[k], 16 * NTP)

            def gather(k, ts):
                for t in ts:
                    nc.gpsimd.indirect_dma_start(
                        out=gb[:, k, t], out_offset=None, in_=osort_d,
                        in_offset=bass.IndirectOffsetOnAxis(ap=gp[:, k, t:t + 1], axis=0)).then_inc(s_g[k], 16)

            def step(i, k, q2, first, second, more):
                if first:
                    pool.wait_ge(s_vea, i + 1)
                    wait_if(pool, s_zn, i, G, 0)
                    nc.gpsimd.tensor_tensor(rsa[:], vea[:], mhalf[:], ALU.pow).then_inc(s_rsa, 1)
                if second:
                    pool.wait_ge(s_veb, i)
                    wait_if(pool, s_fo, i, 1, -1)
                    nc.gpsimd.tensor_tensor(rsb[:], veb[:], mhalf[:], ALU.pow).then_inc(s_rsb, 1)
                if more:
                    pool.wait_ge(s_gst, i + 3)
                    pool.sem_inc(s_gate, 1)
                    gather(k, range(G // 2))
                if first:
                    pool.wait_ge(s_zm, i + 1)
                    wait_if(pool, s_rb, i, 1, 0)
                    nc.gpsimd.tensor_tensor(z[:], zm[:], be2b[:].unsqueeze(1).to_broadcast([P, G, DM]),
                                            ALU.add).then_inc(s_z, 1)
                if more:
                    gather(k, range(G // 2, G))

            pool.wait_ge(s_w, 32)
            pool.wait_ge(s_gst, 2)
            for k in range(2):
                gather(k, range(G))
            final_steps(pool, step)

        @block.vector
        def _(dve):
            step = [0]

            def link(ins):
                step[0] += 1
                ins.then_inc(s_c, 1)
                dve.wait_ge(s_c, step[0])

            dve.wait_ge(s_k, 12)
            nc.vector.tensor_copy(iot0[:], iot_i[:]).then_inc(s_kd, 1)
            nc.vector.tensor_copy(thr[:], thr_i[:]).then_inc(s_kd, 1)
            nc.vector.tensor_copy(tl[:], tl_i[:]).then_inc(s_kd, 1)
            dve.wait_ge(s_kd, 3)
            link(nc.vector.tensor_scalar(iot8[:], iot0[:], float(E), None, ALU.add))
            link(nc.vector.tensor_reduce(mxl[:], lg[:], AX.X, ALU.max))
            link(nc.vector.tensor_tensor(eq[:], lg[:], mxl[:].unsqueeze(2).to_broadcast([P, NG, E]), ALU.is_equal))
            link(nc.vector.scalar_tensor_tensor(cand[:], eq[:], -float(E), iot8[:].unsqueeze(1).to_broadcast([P, NG, E]),
                                                ALU.mult, ALU.add))
            link(nc.vector.tensor_reduce(idx[:], cand[:], AX.X, ALU.min))
            nc.vector.tensor_tensor(oh[:], iot0[:].unsqueeze(1).to_broadcast([P, NG, E]),
                                    idx[:].unsqueeze(2).to_broadcast([P, NG, E]), ALU.is_equal).then_inc(s_oh, 1)
            dve.wait_ge(s_rk, 2)
            link(nc.vector.tensor_copy(tot[:], pT[:].rearrange("p (t e) -> p e t", e=E)))
            link(nc.vector.tensor_tensor_scan(inc[:].rearrange("p e t -> p (e t)"), rst[:].rearrange("p e t -> p (e t)"),
                                              tot[:].rearrange("p e t -> p (e t)"), 0.0, ALU.mult, ALU.add))
            link(nc.vector.tensor_tensor(tot[:], inc[:], tot[:], ALU.subtract))
            link(nc.vector.tensor_tensor(cmp_[:], inc[:, :, NG - 1:NG].to_broadcast([P, E, NG]),
                                         thr[:].unsqueeze(1).to_broadcast([P, E, NG]), ALU.is_gt))
            link(nc.vector.tensor_reduce(nt[:], cmp_[:], AX.X, ALU.add))
            link(nc.vector.tensor_tensor_scan(ntc[:], one8[:], nt[:], 0.0, ALU.mult, ALU.add))
            link(nc.vector.tensor_tensor(base[:], ntc[:], nt[:], ALU.subtract))
            link(nc.vector.scalar_tensor_tensor(cmp_[:], base[:].unsqueeze(2).to_broadcast([P, E, NG]), float(P), tot[:],
                                                ALU.mult, ALU.add))
            link(nc.vector.tensor_tensor(place[:], pR[:].rearrange("p (t e) -> p t e", e=E),
                                         cmp_[:].rearrange("p e t -> p t e"), ALU.add))
            link(nc.vector.tensor_tensor(place[:], place[:], oh[:], ALU.mult))
            link(nc.vector.tensor_reduce(pos[:], place[:], AX.X, ALU.add))
            link(nc.vector.tensor_copy(pos_u[:], pos[:]))
            link(nc.vector.tensor_tensor(ecmp[:], ntc[:].unsqueeze(1).to_broadcast([P, NT, E]),
                                         tl[:].unsqueeze(2).to_broadcast([P, NT, E]), ALU.is_le))
            link(nc.vector.tensor_reduce(eid[:], ecmp[:], AX.X, ALU.add))
            link(nc.vector.tensor_scalar(eid[:], eid[:], float(E - 1), None, ALU.min))
            nc.vector.tensor_copy(eid_i[:], eid[:]).then_inc(s_eid, 1)
            nc.vector.tensor_copy(pos[:], pos_u[:]).then_inc(s_pos, 1)

            def stage(q, k):
                nc.vector.tensor_copy(pidx[:, k], pos_u[:, bass.ds(q * G, G)]).then_inc(s_stg, 1)
                nc.vector.tensor_copy(ytile[:, k], yall[:, bass.ds(q * G, G)]).then_inc(s_stg, 1)

            for k in range(2):
                stage(k, k)
            with dve.Fori(1, NQ // 2) as q2:
                for k in range(2):
                    dve.wait_ge(s_scs[k], 16 * G * q2)
                    stage(2 * q2 + k, k)

            dve.wait_ge(s_eid, 1)
            dve.wait_ge(s_ew, 64)

            def hidden(j, k, e):
                dve.wait_ge(s_h, j + 1)
                wait_if(dve, s_ht, j, 1, -1)
                nc.vector.tensor_tensor(hh[:, k], pH[:, k], b1b[:, bass.ds(e, 1)].rearrange("p o f -> p (o f)"),
                                        ALU.add).then_inc(s_hb, 1)

            def outb(j, k, e, j2):
                dve.wait_ge(s_o, j + 1)
                wait_if(dve, s_osd[k], j2, 16, 0)
                nc.vector.tensor_tensor(ob[:, k], pY[:, k, P:2 * P], b2b[:, bass.ds(e, 1)].rearrange("p o f -> p (o f)"),
                                        ALU.add).then_inc(s_ob, 1)

            def expert(j):
                return dve.value_load(eid_i[0:1, bass.ds(j, 1)], min_val=0, max_val=E - 1)

            def pair(n, last=False):
                if not last:
                    for k in range(2):
                        hidden(2 * n + 2 + k, k, expert(2 * n + 2 + k))
                for k in range(2):
                    outb(2 * n + k, k, expert(2 * n + k), n)

            for k in range(2):
                hidden(k, k, expert(k))
            pair(0)
            with dve.Fori(1, NTP - 1) as n:
                pair(n)
            pair(NTP - 1, last=True)

            def stage_index(q, k):
                nc.vector.tensor_copy(gp[:, k], pos_u[:, bass.ds(q * G, G)]).then_inc(s_gst, 1)

            def stats(n, src, st, s_st, mv, s_mv, ve, s_ve):
                for t in range(G):
                    nc.vector.bn_stats(st[:, t], src[:, t]).then_inc(s_st, 1)
                dve.wait_ge(s_st, G * n)
                dve.sem_inc(s_gate, 1)
                for t in range(G):
                    nc.vector.bn_aggr(mv[:, t], st[:, t]).then_inc(s_mv, 1)
                dve.wait_ge(s_mv, G * n)
                nc.vector.tensor_scalar(ve[:], mv[:, :, 1], EPS, None, ALU.add).then_inc(s_ve, 1)

            def step(i, k, q2, first, second, more):
                if first:
                    dve.wait_ge(s_g[k], 16 * G * q2 + 16 * G)
                    wait_if(dve, s_zn, i, G, 0)
                    nc.vector.tensor_tensor(ra[:], gb[:, k], yall[:, bass.ds(i * G, G)], ALU.add).then_inc(s_ra, 1)
                    dve.wait_ge(s_ra, i + 1)
                    if more:
                        stage_index(i + 2, k)
                    wait_if(dve, s_rsa, i, 1, 0)
                    stats(i + 1, ra, sta, s_sta, mva, s_mva, vea, s_vea)
                if second:
                    dve.wait_ge(s_z, i)
                    if k == 0:
                        dve.wait_ge(s_xg[1], 16 * q2)
                    else:
                        dve.wait_ge(s_xg[0], 16 * q2 + 16)
                    wait_if(dve, s_fo, i, 1, -1)
                    nc.vector.tensor_tensor(rb[:], z[:], xg[:, 1 - k], ALU.add).then_inc(s_rb, 1)
                    dve.wait_ge(s_rb, i)
                    wait_if(dve, s_rsb, i, 1, -1)
                    stats(i, rb, stb, s_stb, mvb, s_mvb, veb, s_veb)
                if first:
                    dve.wait_ge(s_rsa, i + 1)
                    wait_if(dve, s_zm, i, 1, 0)
                    for t in range(G):
                        nc.vector.tensor_scalar(zn[:, t], ra[:, t], mva[:, t, 0:1], rsa[:, t:t + 1], ALU.subtract,
                                                ALU.mult).then_inc(s_zn, 1)
                    dve.wait_ge(s_zn, G * (i + 1))
                    wait_if(dve, s_z, i, 1, 0)
                    nc.vector.tensor_tensor(zm[:], zn[:], g2b[:].unsqueeze(1).to_broadcast([P, G, DM]),
                                            ALU.mult).then_inc(s_zm, 1)
                if second:
                    dve.wait_ge(s_rsb, i)
                    if k == 0 and not (isinstance(q2, int) and q2 <= 1):
                        dve.wait_ge(s_out[1], 16 * S * (q2 - 1))
                    if k == 1 and not (isinstance(q2, int) and q2 == 0):
                        dve.wait_ge(s_out[0], 16 * S * q2)
                    for t in range(G):
                        ins = nc.vector.tensor_scalar(fo[:, 1 - k, t], rb[:, t], mvb[:, t, 0:1], rsb[:, t:t + 1],
                                                      ALU.subtract, ALU.mult)
                    ins.then_inc(s_fo, 1)

            dve.wait_ge(s_w, 32)
            for k in range(2):
                stage_index(k, k)
            final_steps(dve, step)

        @block.scalar
        def _(act):
            act.wait_ge(s_k, 12)

            def tile(j, k):
                act.wait_ge(s_ty, j + 1)
                wait_if(act, s_h, j, 1, -1)
                nc.scalar.copy(yT[:, k], pY[:, k, 0:P]).then_inc(s_yc, 1)

            def relu(j, k):
                act.wait_ge(s_ht, j + 1)
                wait_if(act, s_o, j, 1, -1)
                nc.scalar.activation(hT[:, k], pHT[:, k].rearrange("p (b t) -> p b t", b=NB), ACT.Relu).then_inc(s_hc, 1)

            def store(j, k):
                act.wait_ge(s_ob, j + 1)
                act.dma_start(osort_d[bass.ds(j * P, P), :], ob[:, k]).then_inc(s_osd[k], 16)

            def pair(n, first=False, last=False):
                for k in range(2):
                    if not last:
                        tile(2 * n + 2 + k, k)
                for k in range(2):
                    if not first:
                        store(2 * n - 2 + k, k)
                for k in range(2):
                    relu(2 * n + k, k)

            for k in range(2):
                tile(k, k)
            pair(0, first=True)
            with act.Fori(1, NTP - 1) as n:
                pair(n)
            pair(NTP - 1, last=True)
            for k in range(2):
                store(NT - 2 + k, k)

        @block.tensor
        def _(pe):
            pe.wait_ge(s_k, 12)
            pe.wait_ge(s_oh, 1)
            ohf = oh[:].rearrange("p t e -> p (t e)")
            nc.tensor.matmul(pR[:], tri[:], ohf, start=True, stop=True).then_inc(s_rk, 1)
            nc.tensor.matmul(pT[:], onesb[:], ohf, start=True, stop=True).then_inc(s_rk, 1)
            pe.wait_ge(s_eid, 1)
            pe.wait_ge(s_ew, 64)

            def turn(j, k, j2):
                pe.wait_ge(s_ysl[k], 16 * j2 + 16)
                wait_if(pe, s_ob, j, 1, -3)
                nc.tensor.transpose(pY[:, k, 0:P], ys[:, k], ident[:]).then_inc(s_ty, 1)

            def up(j, k, e):
                pe.wait_ge(s_yc, j + 1)
                wait_if(pe, s_hb, j, 1, -1)
                nc.tensor.matmul(pH[:, k], yT[:, k], w1[:, bass.ds(e, 1)].rearrange("p o f -> p (o f)"), start=True,
                                 stop=True).then_inc(s_h, 1)

            def turn_hidden(j, k):
                pe.wait_ge(s_hb, j + 1)
                wait_if(pe, s_hc, j, 1, -1)
                for b in range(NB):
                    mm = nc.tensor.transpose(pHT[:, k, b * P:(b + 1) * P], hh[:, k, b * P:(b + 1) * P], ident[:])
                mm.then_inc(s_ht, 1)

            def down(j, k, e):
                pe.wait_ge(s_hc, j + 1)
                for b in range(NB):
                    mm = nc.tensor.matmul(pY[:, k, P:2 * P], hT[:, k, b],
                                          w2[:, bass.ds(e, 1), b * DM:(b + 1) * DM].rearrange("p o d -> p (o d)"),
                                          start=(b == 0), stop=(b == NB - 1))
                mm.then_inc(s_o, 1)

            def expert(j):
                return pe.value_load(eid_i[0:1, bass.ds(j, 1)], min_val=0, max_val=E - 1)

            def pair(n, last=False):
                if not last:
                    for k in range(2):
                        turn(2 * n + 2 + k, k, n + 1)
                for k in range(2):
                    turn_hidden(2 * n + k, k)
                if not last:
                    for k in range(2):
                        up(2 * n + 2 + k, k, expert(2 * n + 2 + k))
                for k in range(2):
                    down(2 * n + k, k, expert(2 * n + k))

            for k in range(2):
                turn(k, k, 0)
            for k in range(2):
                up(k, k, expert(k))
            pair(0)
            with pe.Fori(1, NTP - 1) as n:
                pair(n)
            pair(NTP - 1, last=True)


def build_ffn(nc, x1_d, Wqkv, bqkv, Wo, bo, g1, be1, g2, be2, Wg, W1, b1, W2, b2, out):
    NG, _, DM = x1_d.shape
    E, _, DF = W1.shape
    NT = -(-(NG + E - 1) // 2) * 2
    ysort_d = nc.dram_tensor("ysort", [NT * P, DM], F32).ap()
    osort_d = nc.dram_tensor("osort", [NT * P, DM], F32).ap()
    with ExitStack() as ctx:
        def sb(name, shape, dt=F32):
            return ctx.enter_context(nc.sbuf_tensor(name, shape, dt))

        shared = {
            "yall": sb("yall", [P, NG, DM]), "lg": sb("lg", [P, NG, E]),
            "w1": sb("w1", [P, E, DF]), "w2": sb("w2", [P, E, DF]),
            "b1b": sb("b1b", [P, E, DF]), "b2b": sb("b2b", [P, E, DM]),
            "s_ew": ctx.enter_context(nc.semaphore("expert_weights")),
            "s_zf": ctx.enter_context(nc.semaphore("zero_filled")),
        }
        zero = sb("zero", [P, DM])
        s_zm = ctx.enter_context(nc.semaphore("zero_ready"))
        with nc.Block() as block:
            @block.scalar
            def _(act):
                with nc.allow_non_contiguous_dma(reason="rows of weights"):
                    act.dma_start(shared["w1"][:], W1.rearrange("e p f -> p e f")).then_inc(shared["s_ew"], 16)
                    act.dma_start(shared["w2"][:].rearrange("p e (b d) -> p e b d", d=DM),
                                  W2.rearrange("e (b p) d -> p e b d", p=P)).then_inc(shared["s_ew"], 16)
                    act.dma_start(shared["b1b"][:].rearrange("p e f -> p (e f)"),
                                  b1.rearrange("(o e) f -> o (e f)", o=1).broadcast_to([P, E * DF])).then_inc(shared["s_ew"], 16)
                    act.dma_start(shared["b2b"][:].rearrange("p e f -> p (e f)"),
                                  b2.rearrange("(o e) f -> o (e f)", o=1).broadcast_to([P, E * DM])).then_inc(shared["s_ew"], 16)
                    act.wait_ge(s_zm, 1)
                    act.dma_start(ysort_d.rearrange("(t p) d -> p t d", p=P),
                                  zero[:].unsqueeze(1).to_broadcast([P, NT, DM])).then_inc(shared["s_zf"], 16)

            @block.vector
            def _(dve):
                nc.vector.memset(zero[:], 0.0).then_inc(s_zm, 1)

        build_attention(nc, shared, x1_d, Wqkv, bqkv, Wo, bo, g1, be1, g2, be2, Wg, W1, b1, W2, b2, None)
        build_moe(nc, shared, x1_d, g2, be2, W1, b1, W2, b2, ysort_d, osort_d, out)


def build(nc, ins, out):
    x = ins["L0_attn_x"]
    NS, L, DM = x.shape
    x1_d = nc.dram_tensor("x1_grouped", [NS * L // P, P, DM], F32).ap()
    build_mamba(nc, x, *(ins["L0_attn_" + n] for n in
                         ("norm_w", "norm_b", "W_in", "conv_w", "conv_b", "W_x", "W_dt", "b_dt", "A_log", "D", "W_out")), x1_d)
    build_ffn(nc, x1_d, *(ins["L0_ffn_" + n] for n in
                          ("Wqkv", "bqkv", "Wo", "bo", "g1", "be1", "g2", "be2", "Wg", "W1", "b1", "W2", "b2")), out)


_INS = ["L0_attn_x", "L0_attn_norm_w", "L0_attn_norm_b", "L0_attn_W_in", "L0_attn_conv_w", "L0_attn_conv_b",
        "L0_attn_W_x", "L0_attn_W_dt", "L0_attn_b_dt", "L0_attn_A_log", "L0_attn_D", "L0_attn_W_out", "L0_ffn_Wqkv",
        "L0_ffn_bqkv", "L0_ffn_Wo", "L0_ffn_bo", "L0_ffn_g1", "L0_ffn_be1", "L0_ffn_g2", "L0_ffn_be2", "L0_ffn_Wg",
        "L0_ffn_W1", "L0_ffn_b1", "L0_ffn_W2", "L0_ffn_b2"]


def kernel(**inputs):
    import concourse.bacc as bacc
    from concourse.bass_utils import run_bass_kernel_spmd

    nc = bacc.Bacc("TRN2", target_bir_lowering=False, num_devices=1)
    arrays, ins = {}, {}
    for name in _INS:
        a = np.ascontiguousarray(inputs[name])
        arrays[f"in_{name}"] = a
        ins[name] = nc.dram_tensor(f"in_{name}", a.shape, mybir.dt.from_np(a.dtype), kind="ExternalInput").ap()
    out = nc.dram_tensor("out", arrays["in_L0_attn_x"].shape, F32, kind="ExternalOutput").ap()
    build(nc, ins, out)
    r = run_bass_kernel_spmd(nc, [arrays], core_ids=[0])
    return r.results[0]["out"]
```

```python
import numpy as np
import concourse.bass as bass
from concourse import mybir
from contextlib import ExitStack

ALU = mybir.AluOpType
ACT = mybir.ActivationFunctionType
AX = mybir.AxisListType
F32 = mybir.dt.float32
BF16 = mybir.dt.bfloat16

P = 128
EPS = 1e-5
POOL_B = (2, 5, 8, 10, 12, 14)
B_ORDER = (2, 0, 1, 5, 3, 4, 8, 6, 7, 10, 9, 12, 11, 14, 13, 15)
AHEAD = 2
CONV_AT = (0, 1, 2, 2)
X_PROJ_AT = (5, 6)
DT_PROJ_AT = (7, 9)
OUT_PROJ_AT = 9
Z_PROJ_AT = (11, 12)
SILU_IN_AT = (3, 5, 12, 13)
DT_LOW_AT = 7
BC_PARTS_AT = 8
DT_EXPS_AT = (9, 10)
SQUARES_AT = (10, 10, 11, 11)
RESIDUAL_AT = 10
NORM_OUT_AT = 13
SILU_AT = (3, 5, 13, 13)
BC_RESIDUAL_AT = 7
BC_LAST_AT = 9
POLY_AT = (10, 10, 11, 12)
GATE_AT = 3
RSTD_OUT_AT = 10
TIMES_U_AT = 14
LAG = 3
HCB = 4
CSB = 4


def log1p_factors():
    k = np.arange(600)
    y = (1 - np.cos(np.pi * (k + 0.5) / 600)) / 2
    fit = np.polynomial.chebyshev.Chebyshev.fit(y, np.log1p(y) / y, 8, domain=[0, 1])
    c = fit.convert(kind=np.polynomial.Polynomial).coef
    r = sorted((z for z in np.roots(c[::-1]) if z.imag > 0), key=lambda z: z.real)
    return float(c[8]), [(float(-z.real), float(z.imag) ** 2) for z in r]


def build_mamba(nc, x, norm_w, norm_b, W_in, conv_w, conv_b, W_x, W_dt, b_dt, A_log, D, W_out, x1_d, ident, load_next):
    NS, L, DM = x.shape
    DI = W_dt.shape[1]
    R = W_dt.shape[0]
    N = A_log.shape[1]
    KC = conv_w.shape[2]
    H = DI // P
    T = L // P
    LP = L + KC - 1
    NT = NS * T
    XL = 2
    TT = P // NS
    GT = P // TT
    x1_g = x1_d.rearrange("(t g) p d -> t g p d", g=GT)
    lead, quad = log1p_factors()

    with ExitStack() as ctx:
        def sb(name, shape, dt=F32):
            return ctx.enter_context(nc.sbuf_tensor(name, shape, dt))

        def ps(name, shape, dt=F32):
            return ctx.enter_context(nc.psum_tensor(name, shape, dt))

        def sem(name):
            return ctx.enter_context(nc.semaphore(name))

        sel = sb("sel", [96, 2 * N, P], BF16)
        win = sb("win", [P, 2 * DI])
        cwb = sb("cwb", [P, DI, KC])
        wtap = sb("wtap", [P, KC, DI])
        cb = sb("cb", [P, H])
        cbh = sb("cbh", [P, H])
        wx = sb("wx", [P, H, R + 2 * N])
        wbc = sb("wbc", [P, H, 3, 2 * N])
        wdt = sb("wdt", [R, DI])
        bdt = sb("bdt", [P, H])
        alog = sb("alog", [P, H, N])
        aneg = sb("aneg", [P, H, N])
        dsk = sb("dsk", [P, H])
        dmat = sb("dmat", [P, H, P])
        wout = sb("wout", [P, H, DM])
        nw = sb("nw", [P, 1])
        nb = sb("nb", [P, 1])
        mhalf = sb("mhalf", [P, NT])
        xall = sb("xall", [P, NT, DM])
        stats = sb("stats", [P, T, 6])
        mv = sb("mv", [P, T, 2])
        mean = sb("mean", [P, NT])
        ve = sb("ve", [P, NT])
        rstd = sb("rstd", [P, NT])
        xn = sb("xn", [P, 2, T, DM])
        xc = sb("xc", [P, T, DM])
        sel0 = sb("sel0", [96, 2 * N], BF16)
        xnT = sb("xnT", [P, NS, LP])
        u = sb("u", [P, 2 * H * L])
        zs = sb("zs", [P, 2 * H * L])
        delta = sb("delta", [P, 2 * H * L])
        dtu = sb("dtu", [P, 2 * H * L])
        bcs = sb("bcs", [96, 2 * L], BF16)
        th = sb("th", [P, 2, L])
        xh = sb("xh", [P, 2, L])
        dtl = sb("dtl", [R, L])
        r1 = sb("r1", [96, L])
        av = sb("av", [P, H, L])
        ey = sb("ey", [P, H, L])
        rv = sb("rv", [P, H, L])
        sq = sb("sq", [P, 4, H, L])
        bt = sb("bt", [P, 2, H, L])
        btp = sb("btp", [P, H, L])
        hb = sb("hb", [P, 4, H, L])
        hc = sb("hc", [P, HCB, H, L])
        cs = sb("cs", [P, CSB, L])
        bs = sb("bs", [P, L])
        yg = sb("yg", [P, H, L])
        ro = sb("ro", [P, T, DM])
        st2 = sb("st2", [P, T, 6])
        mv2 = sb("mv2", [P, T, 2])
        ve2 = sb("ve2", [P, T])
        rstd2 = sb("rstd2", [P, T])
        x1 = sb("x1", [P, T, DM])

        pB = ps("pB", [P, L])
        pC = ps("pC", [P, L])
        pA = ps("pA", [P, H, L])
        pY = ps("pY", [P, H, L])
        pre = ps("pre", [P, 2, L])

        s_w = sem("weights_loaded")
        s_x = [sem(f"x_loaded{q}") for q in range(XL)]
        s_id = sem("pool_consts")
        s_gate = sem("gate_passed")
        s_z = sem("pads_zeroed")
        s_prep = sem("weights_prepared")
        s_an = sem("a_exp")
        s_aneg = sem("aneg_ready")
        s_st = sem("stats_ready")
        s_mv = sem("meanvar_ready")
        s_mean = sem("mean_ready")
        s_ve = sem("var_eps_ready")
        s_rs = sem("rstd_ready")
        s_xn = sem("xn_ready")
        s_xnp = sem("xn_ready_pool")
        s_xc = sem("x_centred")
        s_sel = sem("selectors_ready")
        s_tp = sem("xn_transposed")
        s_xT = sem("xnT_ready")
        s_pre = sem("pre_psum_ready")
        s_pact = sem("pre_read_by_act")
        s_bcr = sem("bc_residual")
        s_th = sem("silu_inputs")
        s_silu = sem("silu_ready")
        s_bc1 = sem("bc_first_part")
        s_bc2 = sem("bc_second_parts")
        s_bc = sem("bc_parts_ready")
        s_v = sem("dt_exps")
        s_sq = sem("dt_squares")
        s_dl = sem("delta_ready")
        s_du = sem("dtu_ready")
        s_bb = sem("b_rows_ready")
        s_cc = sem("c_rows_ready")
        s_cs = sem("c_copied")
        s_bs = sem("b_copied")
        s_pb = sem("pool_b_ready")
        s_db = sem("vector_b_ready")
        s_a = sem("a_ready")
        s_h = sem("h_ready")
        s_hc = sem("hc_ready")
        s_hu = sem("hc_summed")
        s_dm = sem("d_matrix_ready")
        s_yg = sem("yg_ready")
        s_o = sem("out_psum_ready")
        s_r = sem("residual_ready")
        s_st2 = sem("stats2_ready")
        s_mv2 = sem("meanvar2_ready")
        s_ve2 = sem("vareps2_ready")
        s_rs2 = sem("rstd2_ready")
        s_x1 = sem("x1_ready")
        s_x1d = sem("x1_stored")

        VEC_B = [n for n in range(N) if n not in POOL_B]
        s_cbh = sem("conv_bias_halved")
        s_qa = sem("dt_poly_steps")
        NPB = len(POOL_B)
        NVB = N - NPB

        def at(buf, i, n=1, off=0, width=L):
            par = i % 2
            size = H * L
            return buf[:, bass.ds(par * size + off, width)]

        def wait(eng, s, i, per, c):
            if isinstance(i, int) and i * per + c <= 0:
                return
            eng.wait_ge(s, i * per + c)

        a_bias = [sb(f"a_bias{k}", [P, 1]) for k in range(4)]

        block = ctx.enter_context(nc.Block())

        @block.sync
        def _(sp):
            with nc.allow_non_contiguous_dma(reason="small weights"):
                for q in range(XL):
                    sp.dma_start(xall[:, q * NT // XL:(q + 1) * NT // XL, :],
                                 x[q * NS // XL:(q + 1) * NS // XL].rearrange("s (t p) d -> p (s t) d", p=P)).then_inc(s_x[q], 16)
                    if q == 0:
                        sp.dma_start(win[:], W_in).then_inc(s_w, 16)
                        sp.dma_start(cwb[:].rearrange("p c k -> p (c k)"),
                                     conv_w.rearrange("c o k -> o (c k)").broadcast_to([P, DI * KC])).then_inc(s_w, 16)
                        sp.dma_start(nw[:], norm_w.rearrange("(p o) -> p o", o=1)).then_inc(s_w, 16)
                        sp.dma_start(nb[:], norm_b.rearrange("(p o) -> p o", o=1)).then_inc(s_w, 16)
                        sp.dma_start(cb[:], conv_b.rearrange("(h p) -> p h", p=P)).then_inc(s_w, 16)
                        sp.dma_start(wx[:], W_x.rearrange("(h p) n -> p h n", p=P)).then_inc(s_w, 16)
                        sp.dma_start(wdt[:], W_dt).then_inc(s_w, 16)
                        sp.dma_start(bdt[:], b_dt.rearrange("(h p) -> p h", p=P)).then_inc(s_w, 16)
                        sp.dma_start(alog[:], A_log.rearrange("(h p) n -> p h n", p=P)).then_inc(s_w, 16)
                        sp.dma_start(dsk[:], D.rearrange("(h p) -> p h", p=P)).then_inc(s_w, 16)
                        sp.dma_start(wout[:], W_out.rearrange("(h p) n -> p h n", p=P)).then_inc(s_w, 16)
                load_next(sp)
                with sp.Fori(0, NS) as s:
                    sp.wait_ge(s_x1, (s + 1) * T)
                    for g in range(GT):
                        sp.dma_start(x1_g[:, g, bass.ds(s * TT, TT), :].rearrange("t p d -> p t d"),
                                     x1[g * TT:(g + 1) * TT]).then_inc(s_x1d, 16)
            sp.wait_ge(s_x1d, 16 * GT * NS)

        NWL = 11

        @block.gpsimd
        def _(pool):
            nc.gpsimd.memset(ident[:], 0.0).then_inc(s_id, 1)
            nc.gpsimd.memset(sel0[:], 0.0).then_inc(s_id, 1)
            nc.gpsimd.memset(mhalf[:], -0.5).then_inc(s_id, 1)
            nc.gpsimd.memset(xnT[:, :, 0:KC - 1], 0.0).then_inc(s_id, 1)
            pool.wait_ge(s_id, 4)
            nc.gpsimd.affine_select(out=ident[:], in_=ident[:], compare_op=ALU.not_equal, fill=1.0, base=0,
                                    pattern=[[-1, P]], channel_multiplier=1).then_inc(s_id, 1)
            for part in range(3):
                nc.gpsimd.affine_select(out=sel0[:], in_=sel0[:], compare_op=ALU.not_equal, fill=1.0,
                                        base=-2 * N * part, pattern=[[-1, 2 * N]],
                                        channel_multiplier=1).then_inc(s_id, 1)
                pool.wait_ge(s_id, 6 + part)

            def rstd_of(s):
                pool.wait_ge(s_ve, s + 1)
                sl = bass.ds(s * T, T)
                nc.gpsimd.tensor_tensor(rstd[:, sl], ve[:, sl], mhalf[:, sl], ALU.pow).then_inc(s_rs, 1)

            def normalise(s, k):
                rstd_of(s)
                pool.wait_ge(s_mean, s + 1)
                wait(pool, s_xnp, s, 1, -1)
                pool.sem_inc(s_gate, 1)
                sl = bass.ds(s * T, T)
                nc.gpsimd.tensor_tensor(xc[:], xall[:, sl], mean[:, sl].unsqueeze(2).to_broadcast([P, T, DM]),
                                        ALU.subtract).then_inc(s_xc, 1)
                pool.wait_ge(s_xc, s)
                pool.wait_ge(s_rs, s + 1)
                wait(pool, s_tp, s, T, -T)
                pool.sem_inc(s_gate, 1)
                nc.gpsimd.tensor_tensor(xn[:, k], xc[:], rstd[:, sl].unsqueeze(2).to_broadcast([P, T, DM]),
                                        ALU.mult).then_inc(s_xnp, 1)

            rstd_of(0)
            normalise(1, 1)
            with pool.Fori(1, NS // 2) as s2:
                for k in range(2):
                    normalise(2 * s2 + k, k)

            def product_b(i, n):
                k = POOL_B.index(n)
                wait(pool, s_bs, i, NPB, k + 1)
                if k == 0:
                    pool.wait_ge(s_du, i + 1)
                before = POOL_B[k - 1] if k else POOL_B[-1] - N
                wait(pool, s_h, i, H * N, H * (before + 1))
                pool.sem_inc(s_gate, 1)
                nc.gpsimd.tensor_tensor(btp[:], at(dtu, i, width=H * L).rearrange("p (h t) -> p h t", h=H),
                                        bs[:].unsqueeze(1).to_broadcast([P, H, L]), ALU.mult).then_inc(s_pb, 1)

            def product_hc(i, n):
                wait(pool, s_cs, i, N, n + 1)
                wait(pool, s_h, i, H * N, H * (n + 1))
                wait(pool, s_hu, i, N, n - HCB + 1)
                nc.gpsimd.tensor_tensor(hc[:, n % HCB], hb[:, n % 4],
                                        cs[:, n % CSB].unsqueeze(1).to_broadcast([P, H, L]), ALU.mult).then_inc(s_hc, 1)

            def body(i, first=False, last=False):
                for n in range(N):
                    if n + 2 in POOL_B:
                        product_b(i, n + 2)
                    if n >= 1:
                        product_hc(i, n - 1)
                    elif not first:
                        product_hc(i - 1, N - 1)
                    if n == RSTD_OUT_AT and not first:
                        rstd_out(i - 1)
                    if n == TIMES_U_AT and not last:
                        times_u(i + 1)
                if last:
                    product_hc(i, N - 1)

            def rstd_out(i):
                pool.wait_ge(s_ve2, i + 1)
                nc.gpsimd.tensor_tensor(rstd2[:], ve2[:], mhalf[:, 0:T], ALU.pow).then_inc(s_rs2, 1)

            def times_u(i):
                pool.wait_ge(s_dl, i + 1)
                pool.wait_ge(s_silu, 4 * i + 2)
                nc.gpsimd.tensor_tensor(at(dtu, i, width=H * L), at(delta, i, width=H * L), at(u, i, width=H * L),
                                        ALU.mult).then_inc(s_du, 1)

            times_u(0)
            body(0, first=True)
            with pool.Fori(1, NS - 1) as i:
                body(i)
            body(NS - 1, last=True)
            rstd_out(NS - 1)

        @block.scalar
        def _(act):
            nc.scalar.preload_act_table_set("exp_and_others")
            act.wait_ge(s_w, 16 * NWL)
            nc.scalar.activation(aneg[:], alog[:], ACT.Exp).then_inc(s_an, 1)
            nc.scalar.mul(cbh[:], cb[:], 0.5).then_inc(s_cbh, 1)
            act.wait_ge(s_an, 1)
            nc.scalar.mul(aneg[:], aneg[:], -1.0).then_inc(s_aneg, 1)
            act.wait_ge(s_aneg, 1)
            act.wait_ge(s_cbh, 1)
            act.wait_ge(s_id, 8)
            act.wait_ge(s_z, 4)

            def tokens_in(s, k):
                act.wait_ge(s_tp, T * (s + 1))
                nc.scalar.activation(xnT[:, bass.ds(s, 1), KC - 1:LP].rearrange("p o t -> p (o t)"), pY[:, k],
                                     ACT.Identity, bias=nb[:, 0:1], scale=nw[:, 0:1]).then_inc(s_xT, 1)

            def silu_in(i, m):
                act.wait_ge(s_pre, 8 * i + (m + 1 if m < 2 else m + 5))
                wait(act, s_silu, i, 4, m - 1)
                if m < 2:
                    nc.scalar.activation(th[:, m % 2], pre[:, m % 2], ACT.Tanh, bias=cbh[:, m:m + 1],
                                         scale=0.5).then_inc(s_th, 1)
                    nc.scalar.activation(xh[:, m % 2], pre[:, m % 2], ACT.Identity, bias=cbh[:, m:m + 1],
                                         scale=0.5).then_inc(s_pact, 1)
                else:
                    nc.scalar.activation(th[:, m % 2], pre[:, m % 2], ACT.Tanh, scale=0.5).then_inc(s_th, 1)
                    nc.scalar.mul(xh[:, m % 2], pre[:, m % 2], 0.5).then_inc(s_pact, 1)

            def dt_low_copy(i):
                act.wait_ge(s_pre, 8 * i + 3)
                wait(act, s_pre, i, 8, -2)
                nc.scalar.copy(dtl[:], pre[0:R, 0]).then_inc(s_pact, 1)

            def bc_parts(i):
                act.wait_ge(s_pre, 8 * i + 4)
                here = bass.ds((i % 2) * L, L)
                nc.scalar.copy(bcs[:, here], pre[0:96, 1]).then_inc(s_bc1, 1)
                act.wait_ge(s_bcr, i + 1)
                for q in (1, 2):
                    nc.scalar.copy(bcs[32 * q:32 * q + 32, here], r1[32 * q:32 * q + 32]).then_inc(s_bc2, 1)

            def dt_exps(i, h):
                act.wait_ge(s_pre, 8 * i + 5 + h)
                wait(act, s_dl, i, 1, 0)
                b = bdt[:, h:h + 1]
                nc.scalar.activation(av[:, h], pre[:, h], ACT.Abs, bias=b).then_inc(s_v, 1)
                nc.scalar.activation(rv[:, h], pre[:, h], ACT.Relu, bias=b).then_inc(s_pact, 1)
                act.wait_ge(s_v, 4 * i + 2 * h + 1)
                nc.scalar.activation(ey[:, h], av[:, h], ACT.Exp, scale=-1.0).then_inc(s_v, 1)

            def dt_square(i, k):
                act.wait_ge(s_v, 4 * i + 4)
                wait(act, s_dl, i, 1, 0)
                nc.scalar.activation(sq[:, k], ey[:], ACT.Square, bias=a_bias[k][:, 0:1]).then_inc(s_sq, 1)

            def state(i, n):
                wait(act, s_cc, i, N, n + 1)
                wait(act, s_hc, i, N, n - CSB + 1)
                nc.scalar.copy(cs[:, n % CSB], pC[:]).then_inc(s_cs, 1)
                act.wait_ge(s_dl, i + 1)
                for h in range(H):
                    wait(act, s_h, i, H * N, H * (n - 1) + h + 1)
                    act.sem_inc(s_gate, 1)
                    nc.scalar.activation(pA[:, h], at(delta, i, off=h * L), ACT.Exp,
                                         scale=aneg[:, h, n:n + 1]).then_inc(s_a, 1)

            def b_copy(i, n):
                p = n + AHEAD
                if p >= N:
                    i, p = i + 1, p - N
                if B_ORDER[p] in POOL_B:
                    wait(act, s_bb, i, N, p + 1)
                    wait(act, s_pb, i, NPB, POOL_B.index(B_ORDER[p]))
                    nc.scalar.copy(bs[:], pB[:]).then_inc(s_bs, 1)

            def body(i, last=False):
                for n in range(N):
                    if not last or n + AHEAD - 1 < N:
                        b_copy(i, n - 1)
                    state(i, n)
                    if last:
                        continue
                    for m in range(2):
                        if n == SILU_IN_AT[m]:
                            silu_in(i + 1, m)
                    if n == DT_LOW_AT:
                        dt_low_copy(i + 1)
                    if n == BC_PARTS_AT:
                        bc_parts(i + 1)
                    for h in range(H):
                        if n == DT_EXPS_AT[h]:
                            dt_exps(i + 1, h)
                    for k in range(4):
                        if n == SQUARES_AT[k]:
                            dt_square(i + 1, k)
                    for m in range(2, 4):
                        if n == SILU_IN_AT[m]:
                            silu_in(i + 1, m)

            tokens_in(0, 0)
            for h in range(H):
                nc.scalar.mul(dmat[:, h], ident[:], dsk[:, h:h + 1]).then_inc(s_dm, 1)
            nc.scalar.copy(sel[:], sel0[:].unsqueeze(2).to_broadcast([96, 2 * N, P])).then_inc(s_sel, 1)
            for m in range(2):
                silu_in(0, m)
            tokens_in(1, 1)
            dt_low_copy(0)
            bc_parts(0)
            tokens_in(2, 0)
            for h in range(H):
                dt_exps(0, h)
            for k in range(4):
                dt_square(0, k)
            tokens_in(3, 1)
            for m in range(2, 4):
                silu_in(0, m)
            with act.Fori(2, NS // 2) as s2:
                for k in range(2):
                    tokens_in(2 * s2 + k, k)
            b_copy(0, -AHEAD)
            body(0)
            with act.Fori(1, NS - 1) as i:
                body(i)
            body(NS - 1, last=True)

        @block.vector
        def _(dve):
            for k in range(4):
                nc.vector.memset(a_bias[k][:], quad[k][0]).then_inc(s_z, 1)

            def token_stats(s):
                for t in range(T):
                    nc.vector.bn_stats(stats[:, t], xall[:, bass.ds(s * T + t, 1)].rearrange("p o d -> p (o d)")).then_inc(s_st, 1)
                dve.wait_ge(s_st, T * s + T)
                dve.sem_inc(s_gate, 1)
                for t in range(T):
                    nc.vector.bn_aggr(mv[:, t], stats[:, t]).then_inc(s_mv, 1)
                dve.wait_ge(s_mv, T * s + T)
                nc.vector.tensor_copy(mean[:, bass.ds(s * T, T)], mv[:, :, 0]).then_inc(s_mean, 1)
                nc.vector.tensor_scalar(ve[:, bass.ds(s * T, T)], mv[:, :, 1], EPS, None, ALU.add).then_inc(s_ve, 1)

            dve.wait_ge(s_x[0], 16)
            token_stats(0)
            dve.wait_ge(s_w, 16 * NWL)
            for k in range(KC):
                nc.vector.tensor_tensor(wtap[:, k], win[:, 0:DI], cwb[:, :, k], ALU.mult).then_inc(s_prep, 1)
            dve.wait_ge(s_rs, 1)
            dve.wait_ge(s_mean, 1)
            for t in range(T):
                nc.vector.tensor_scalar(xn[:, 0, t], xall[:, t], mean[:, t:t + 1], rstd[:, t:t + 1], ALU.subtract,
                                        ALU.mult).then_inc(s_xn, 1)
            for j in range(3):
                nc.vector.tensor_copy(wbc[:, :, j], wx[:, :, R:R + 2 * N]).then_inc(s_prep, 1)
            with dve.Fori(1, NS // XL) as s:
                token_stats(s)
            for q in range(1, XL):
                dve.wait_ge(s_x[q], 16)
            token_stats(NS // XL)

            def silu(i, m):
                dve.wait_ge(s_th, 4 * i + m + 1)
                dve.wait_ge(s_pact, 7 * i + (m + 1 if m < 2 else m + 4))
                if m >= 2:
                    wait(dve, s_yg, i, 1, -1)
                else:
                    wait(dve, s_hu, i, N, -N)
                dst = at(u if m < 2 else zs, i, off=(m % 2) * L)
                nc.vector.scalar_tensor_tensor(dst, th[:, m % 2], 1.0, xh[:, m % 2], ALU.add,
                                               ALU.mult).then_inc(s_silu, 1)

            def bc_residual(i):
                dve.wait_ge(s_bc1, i + 1)
                wait(dve, s_bc, i, 1, 0)
                nc.vector.tensor_tensor(r1[:], pre[0:96, 1], bcs[:, bass.ds((i % 2) * L, L)],
                                        ALU.subtract).then_inc(s_bcr, 1)

            def bc_last(i):
                dve.wait_ge(s_bc2, 2 * i + 2)
                here = bass.ds((i % 2) * L, L)
                nc.vector.tensor_tensor(bcs[64:96, here], r1[64:96], bcs[64:96, here], ALU.subtract).then_inc(s_bc, 1)

            def dt_poly(i, k):
                dve.wait_ge(s_sq, 4 * i + k + 1)
                if k:
                    dve.wait_ge(s_qa, 4 * i + k)
                nc.vector.scalar_tensor_tensor(sq[:, k], sq[:, k], quad[k][1], ey[:] if k == 0 else sq[:, k - 1],
                                               ALU.add, ALU.mult).then_inc(s_qa, 1)
                if k == 3:
                    dve.wait_ge(s_qa, 4 * i + 4)
                    dve.wait_ge(s_pact, 7 * i + 5)
                    nc.vector.scalar_tensor_tensor(at(delta, i, width=H * L), sq[:, 3].rearrange("p h t -> p (h t)"),
                                                   lead, rv[:].rearrange("p h t -> p (h t)"), ALU.mult,
                                                   ALU.add).then_inc(s_dl, 1)

            def gate(i):
                dve.wait_ge(s_hu, N * (i + 1))
                dve.wait_ge(s_silu, 4 * i + 4)
                wait(dve, s_o, i, 1, 0)
                nc.vector.tensor_tensor(yg[:].rearrange("p h t -> p (h t)"), pY[:].rearrange("p h t -> p (h t)"),
                                        at(zs, i, width=H * L), ALU.mult).then_inc(s_yg, 1)

            def residual(i):
                dve.wait_ge(s_o, i + 1)
                nc.vector.scalar_tensor_tensor(ro[:].rearrange("p t d -> p (t d)"),
                                               xall[:, bass.ds(i * T, T)].rearrange("p t d -> p (t d)"), 2.0, pre[:, 0],
                                               ALU.mult, ALU.add).then_inc(s_r, 1)
                dve.wait_ge(s_r, i + 1)
                for t in range(T):
                    nc.vector.bn_stats(st2[:, t], ro[:, t]).then_inc(s_st2, 1)
                dve.wait_ge(s_st2, T * (i + 1))
                dve.sem_inc(s_gate, 1)
                for t in range(T):
                    nc.vector.bn_aggr(mv2[:, t], st2[:, t]).then_inc(s_mv2, 1)
                dve.wait_ge(s_mv2, T * (i + 1))
                nc.vector.tensor_scalar(ve2[:], mv2[:, :, 1], EPS, None, ALU.add).then_inc(s_ve2, 1)

            def normalise_out(i):
                dve.wait_ge(s_rs2, i + 1)
                wait(dve, s_x1d, i, 16 * GT, 0)
                for t in range(T):
                    nc.vector.tensor_scalar(x1[:, t], ro[:, t], mv2[:, t, 0:1], rstd2[:, t:t + 1], ALU.subtract,
                                            ALU.mult).then_inc(s_x1, 1)

            def state(i, n):
                if n not in POOL_B:
                    k = VEC_B.index(n)
                    dve.wait_ge(s_bb, N * i + B_ORDER.index(n) + 1)
                    if k == 0:
                        dve.wait_ge(s_du, i + 1)
                        wait(dve, s_h, i, H * N, 0)
                    nc.vector.tensor_tensor(bt[:, k % 2], at(dtu, i, width=H * L).rearrange("p (h t) -> p h t", h=H),
                                            pB[:].unsqueeze(1).to_broadcast([P, H, L]), ALU.mult).then_inc(s_db, 1)
                    dve.wait_ge(s_db, NVB * i + k + 1)
                    b_of = bt[:, k % 2]
                else:
                    b_of = btp[:]
                    dve.wait_ge(s_pb, NPB * i + POOL_B.index(n) + 1)
                wait(dve, s_hc, i, N, n - 3)
                for h in range(H):
                    dve.wait_ge(s_a, H * N * i + H * n + h + 1)
                    nc.vector.tensor_tensor_scan(hb[:, n % 4, h], pA[:, h], b_of[:, h], 0.0, ALU.mult,
                                                 ALU.add).then_inc(s_h, 1)

            def body(i, first=False, last=False):
                for n in range(N):
                    state(i, n)
                    if not first:
                        if n == GATE_AT:
                            gate(i - 1)
                        if n == RESIDUAL_AT:
                            residual(i - 1)
                        if n == NORM_OUT_AT:
                            normalise_out(i - 1)
                    if not last:
                        for m in range(2):
                            if n == SILU_AT[m]:
                                silu(i + 1, m)
                        if n == BC_RESIDUAL_AT:
                            bc_residual(i + 1)
                        if n == BC_LAST_AT:
                            bc_last(i + 1)
                        for k in range(4):
                            if n == POLY_AT[k]:
                                dt_poly(i + 1, k)
                        for m in range(2, 4):
                            if n == SILU_AT[m]:
                                silu(i + 1, m)

            silu(0, 0)
            silu(0, 1)
            for s in range(NS // XL + 1, NS - 1):
                token_stats(s)
            bc_residual(0)
            bc_last(0)
            token_stats(NS - 1)
            for k in range(4):
                dt_poly(0, k)
            silu(0, 2)
            silu(0, 3)
            body(0, first=True)
            with dve.Fori(1, NS - 1) as i:
                body(i)
            body(NS - 1, last=True)
            gate(NS - 1)
            residual(NS - 1)
            normalise_out(NS - 1)

        @block.tensor
        def _(pe):
            pe.wait_ge(s_id, 5)

            def transposes(s, k):
                wait(pe, s_xT, s, 1, -1)
                if not isinstance(s, int) or s > 0:
                    pe.wait_ge(s_xnp, s)
                for t in range(T):
                    if isinstance(s, int) and s == 0:
                        pe.wait_ge(s_xn, t + 1)
                    nc.tensor.transpose(pY[:, k, t * P:(t + 1) * P], xn[:, k, t], ident[:]).then_inc(s_tp, 1)

            def tokens(i, k=0):
                return xnT[:, bass.ds(i, 1), k:k + L].rearrange("p o t -> p (o t)")

            def conv(i, h, taps):
                if 0 in taps:
                    wait(pe, s_pact, i, 7, h - 1)
                for k in taps:
                    mm = nc.tensor.matmul(pre[:, h], wtap[:, k, h * P:(h + 1) * P], tokens(i, k), start=(k == 0),
                                          stop=(k == KC - 1))
                if KC - 1 in taps:
                    mm.then_inc(s_pre, 1)

            def x_proj(i, bank):
                pe.wait_ge(s_silu, 4 * i + 2)
                pe.wait_ge(s_pact, 7 * i + 1 + bank)
                for h in range(H):
                    rows_of, w = (R, wx[:, h, 0:R]) if bank == 0 else (96, wbc[:, h].rearrange("p j n -> p (j n)"))
                    mm = nc.tensor.matmul(pre[0:rows_of, bank], w, at(u, i, off=h * L), start=(h == 0),
                                          stop=(h == H - 1))
                mm.then_inc(s_pre, 1)

            def dt_proj(i, h):
                pe.wait_ge(s_pact, 7 * i + 3)
                if h == 1:
                    pe.wait_ge(s_bcr, i + 1)
                nc.tensor.matmul(pre[:, h], wdt[:, h * P:(h + 1) * P], dtl[:], start=True, stop=True).then_inc(s_pre, 1)

            def z_proj(i, h):
                if h == 0:
                    wait(pe, s_r, i, 1, -1)
                pe.wait_ge(s_pact, 7 * i + 4 + h)
                nc.tensor.matmul(pre[:, h], win[:, DI + h * P:DI + (h + 1) * P], tokens(i, KC - 1), start=True,
                                 stop=True).then_inc(s_pre, 1)

            def out_proj(i, free):
                pe.wait_ge(s_yg, i + 1)
                pe.wait_ge(*free)
                for t in range(T):
                    for h in range(H):
                        mm = nc.tensor.matmul(pre[:, 0, t * P:(t + 1) * P], yg[:, h, t * P:(t + 1) * P], wout[:, h],
                                              start=(h == 0), stop=(h == H - 1))
                mm.then_inc(s_o, 1)

            def row_b(i, p):
                here = bass.ds((i % 2) * L, L)
                if p == 0:
                    pe.wait_ge(s_bc, i + 1)
                m = B_ORDER[p - 1]
                j = i if p else i - 1
                if not (isinstance(j, int) and j < 0):
                    if m in POOL_B:
                        pe.wait_ge(s_bs, NPB * j + POOL_B.index(m) + 1)
                    else:
                        pe.wait_ge(s_db, NVB * j + VEC_B.index(m) + 1)
                nc.tensor.matmul(pB[:], sel[:, B_ORDER[p]], bcs[:, here], start=True, stop=True).then_inc(s_bb, 1)

            def row_c(i, n):
                wait(pe, s_cs, i, N, n)
                nc.tensor.matmul(pC[:], sel[:, N + n], bcs[:, bass.ds((i % 2) * L, L)], start=True,
                                 stop=True).then_inc(s_cc, 1)

            def sum_states(i, n):
                pe.wait_ge(s_hc, N * i + n + 1)
                if n == 0:
                    wait(pe, s_yg, i, 1, 0)
                for h in range(H):
                    mm = nc.tensor.matmul(pY[:, h], ident[:], hc[:, n % HCB, h], start=(n == 0), stop=False)
                    if n == N - 1:
                        mm = nc.tensor.matmul(pY[:, h], dmat[:, h], at(u, i, off=h * L), start=False, stop=True)
                mm.then_inc(s_hu, 1)

            def body(i, first=False, last=False):
                for n in range(N):
                    if n < N - 1:
                        row_c(i, n + 1)
                    elif not last:
                        row_c(i + 1, 0)
                    if n + AHEAD < N:
                        row_b(i, n + AHEAD)
                    elif not last:
                        row_b(i + 1, n + AHEAD - N)
                    if n >= LAG:
                        sum_states(i, n - LAG)
                    elif not first:
                        sum_states(i - 1, N + n - LAG)
                    if not last:
                        for q in range(4):
                            if n == CONV_AT[q]:
                                conv(i + 1, q // 2, range(KC // 2) if q % 2 == 0 else range(KC // 2, KC))
                        for q in range(2):
                            if n == X_PROJ_AT[q]:
                                x_proj(i + 1, q)
                            if n == DT_PROJ_AT[q]:
                                dt_proj(i + 1, q)
                    if n == OUT_PROJ_AT and not first:
                        out_proj(i - 1, (s_pact, 7 * (i + 1) + 4) if not last else (s_pact, 7 * NS))
                    for q in range(2):
                        if n == Z_PROJ_AT[q] and not last:
                            z_proj(i + 1, q)

            transposes(0, 0)
            pe.wait_ge(s_prep, KC)
            pe.wait_ge(s_xT, 1)
            for h in range(H):
                conv(0, h, range(KC))
            transposes(1, 1)
            pe.wait_ge(s_prep, KC + 3)
            for h in range(2):
                x_proj(0, h)
            transposes(2, 0)
            for h in range(H):
                dt_proj(0, h)
            transposes(3, 1)
            for h in range(H):
                z_proj(0, h)
            with pe.Fori(2, NS // 2) as s2:
                for k in range(2):
                    transposes(2 * s2 + k, k)
            pe.wait_ge(s_sel, 1)
            pe.wait_ge(s_dm, H)
            pe.wait_ge(s_xT, NS)
            for p in range(AHEAD):
                row_b(0, p)
            row_c(0, 0)
            body(0, first=True)
            with pe.Fori(1, NS - 1) as i:
                body(i)
            body(NS - 1, last=True)
            for n in range(N - LAG, N):
                sum_states(NS - 1, n)
            out_proj(NS - 1, (s_r, NS - 1))

I32 = mybir.dt.int32
U32 = mybir.dt.uint32
BIG = 2.0 ** 100


def wait_if(eng, s, i, per, c):
    if isinstance(i, int) and i * per + c <= 0:
        return
    eng.wait_ge(s, i * per + c)


def attention_weights(nc, ctx, DM, E):
    def sb(name, shape):
        return ctx.enter_context(nc.sbuf_tensor(name, shape, F32))

    return {
        "ident": sb("ident", [P, P]),
        "wnat": sb("a_wnat", [P, 4, DM]),
        "wgn": sb("a_wgn", [E, DM]),
        "bq": sb("a_bq", [P, 3]),
        "bor": sb("a_bor", [1, DM]),
        "g1b": sb("a_g1b", [P, DM]),
        "be1b": sb("a_be1b", [P, DM]),
        "s_w": ctx.enter_context(nc.semaphore("a_weights")),
    }


def load_attention_weights(nc, sp, aw, Wqkv, bqkv, Wo, bo, g1, be1, Wg):
    DM = Wo.shape[0]
    s_w = aw["s_w"]
    sp.dma_start(aw["wnat"][:, 0:3, :], Wqkv.rearrange("(j p) d -> p j d", p=P)).then_inc(s_w, 16)
    sp.dma_start(aw["wnat"][:, 3, :], Wo).then_inc(s_w, 16)
    sp.dma_start(aw["wgn"][:], Wg).then_inc(s_w, 16)
    sp.dma_start(aw["bq"][:], bqkv.rearrange("(j p) -> p j", p=P)).then_inc(s_w, 16)
    sp.dma_start(aw["bor"][:], bo.rearrange("(o d) -> o d", o=1)).then_inc(s_w, 16)
    sp.dma_start(aw["g1b"][:], g1.rearrange("(o d) -> o d", o=1).broadcast_to([P, DM])).then_inc(s_w, 16)
    sp.dma_start(aw["be1b"][:], be1.rearrange("(o d) -> o d", o=1).broadcast_to([P, DM])).then_inc(s_w, 16)


N_ATTENTION_WEIGHTS = 7


def build_attention(nc, shared, aw, x1_d, E, W1, b1, W2, b2, ysort_d, CAP, NT):
    NG = x1_d.shape[0]
    DM = x1_d.shape[2]
    G = 2
    NQ = NG // G
    S = 8
    TT = P // S
    HD = 32
    NH = DM // HD
    SCALE = 1.0 / float(np.sqrt(HD))
    T = G * P
    RK = T + G * E
    C = HD + 1
    NW = N_ATTENTION_WEIGHTS
    ES = E // (NQ // 2)
    ident, wnat, wgn, bq, bor, g1b, be1b, s_w = (aw[n] for n in ("ident", "wnat", "wgn", "bq", "bor", "g1b", "be1b", "s_w"))
    w1, w2, b1b, b2b, s_ew = (shared[n] for n in ("w1", "w2", "b1b", "b2b", "s_ew"))
    yall, run, expert, before, zero = (shared[n] for n in ("yall", "run", "expert", "before", "zero"))
    iot0, erow, thr, tl, one8 = (shared[n] for n in ("iot0", "erow", "thr", "tl", "one8"))
    pad_i, eid_i, trow_i, pos_u = (shared[n] for n in ("pad_i", "eid_i", "trow_i", "pos_u"))
    SPARE = E * CAP

    with ExitStack() as ctx:
        def sb(name, shape, dt=F32):
            return ctx.enter_context(nc.sbuf_tensor(name, shape, dt))

        def ps(name, shape, dt=F32):
            return ctx.enter_context(nc.psum_tensor(name, shape, dt))

        def sem(name):
            return ctx.enter_context(nc.semaphore(name))

        s_gate = sem("a_gate_passed")
        identb = sb("a_identb", [P, P], BF16)
        mask = sb("a_mask", [P, G, P], BF16)
        mhalf = sb("a_mhalf", [P, G])
        wT = sb("a_wT", [P, 4, DM])
        wgT = sb("a_wgT", [P, E])
        bqs = sb("a_bqs", [P, 1])
        cst = sb("a_cst", [1, DM])
        cstb = sb("a_cstb", [P, DM])
        ones = sb("a_ones", [1, P])
        xg = sb("a_xg", [P, 2, G, DM])
        xb = sb("a_xb", [P, 2, G, DM])
        xT = sb("a_xT", [P, T])
        qT = sb("a_qT", [P, T])
        kT = sb("a_kT", [P, T])
        v = sb("a_v", [P, 2, G, NH, C])
        mx = sb("a_mx", [P, NH, G])
        sh = sb("a_sh", [P, NH, T])
        pr = sb("a_pr", [P, NH, T])
        prT = sb("a_prT", [P, NH, T])
        rin = sb("a_rin", [P, G * NH])
        on = sb("a_on", [P, G, DM])
        oT = sb("a_oT", [P, T])
        ro = sb("a_ro", [P, G, DM])
        st = sb("a_st", [P, G, 6])
        mv = sb("a_mv", [P, G, 2])
        ve = sb("a_ve", [P, G])
        rs = sb("a_rs", [P, G])
        yn = sb("a_yn", [P, G, DM])
        ym = sb("a_ym", [P, G, DM])
        yq = sb("a_yq", [P, G, DM])
        yT = sb("a_yT", [P, T])
        tri = sb("a_tri", [P, P], BF16)
        onesb = sb("a_onesb", [P, P], BF16)
        iot8 = sb("a_iota8", [P, E])
        lg = sb("a_lg", [P, 2, G, E])
        mxl = sb("a_mxl", [P, G])
        eq = sb("a_eq", [P, G, E])
        cand = sb("a_cand", [P, G, E])
        idx = sb("a_idx", [P, 2, G])
        oh = sb("a_oh", [P, 2, G, E], BF16)
        rank = sb("a_rank", [P, G, E])
        mine = sb("a_mine", [P, G, E])
        rk = sb("a_rk", [P, G])
        pos = sb("a_pos", [P, G])
        cmp_ = sb("a_cmp", [P, E, NG])
        nt = sb("a_nt", [P, E])
        ntc = sb("a_ntc", [P, E])
        base = sb("a_base", [P, E])
        ended = sb("a_ended", [P, NT, E])
        begun = sb("a_begun", [P, NT, E])
        w = sb("a_w", [P, E])
        trow = sb("a_trow", [P, NT])
        pad = sb("a_pad", [P, E])
        eid = sb("a_eid", [P, NT])
        first_of = sb("a_first", [P, NG, E])
        row = sb("a_row", [P, NG])
        yst = sb("a_yst", [P, 2, G, DM])
        pidx = sb("a_pidx", [P, 2, G], U32)

        pS = ps("a_pS", [P, NH, 2, T])
        pA = ps("a_pA", [P, 2, T])
        pV = ps("a_pV", [P, 512])
        pO = ps("a_pO", [P, 512])
        pB = ps("a_pB", [P, 512])

        s_mk = sem("a_masks")
        s_wt = sem("a_w_transposed")
        s_wc = sem("a_w_copied")
        s_cp = sem("a_const_psum")
        s_cc = sem("a_const_ready")
        s_xg = [sem("a_x_loaded0"), sem("a_x_loaded1")]
        s_xb = sem("a_x_with_const")
        s_xt = sem("a_x_transposed")
        s_xtc = sem("a_xT_copied")
        s_qk = sem("a_qk_ready")
        s_qkc = sem("a_qk_copied")
        s_v = sem("a_v_ready")
        s_vc = sem("a_v_copied")
        s_sc = sem("a_scores_ready")
        s_mx = sem("a_max_ready")
        s_sh = sem("a_shifted")
        s_ex = sem("a_exp_ready")
        s_pt = sem("a_probs_transposed")
        s_pta = sem("a_probsT_copied_act")
        s_ptd = sem("a_probsT_copied_dve")
        s_o = sem("a_o_ready")
        s_rin = sem("a_recip_ready")
        s_on = sem("a_o_normalised")
        s_ot = sem("a_o_transposed")
        s_otc = sem("a_oT_copied")
        s_po = sem("a_out_ready")
        s_out = sem("a_out_read")
        s_st = sem("a_stats")
        s_mv = sem("a_meanvar")
        s_ve = sem("a_vareps")
        s_rs = sem("a_rstd")
        s_yn = sem("a_normalised")
        s_ym = sem("a_scaled")
        s_y = sem("a_y_ready")
        s_ya = sem("a_y_kept")
        s_yt = sem("a_y_transposed")
        s_ytc = sem("a_yT_copied")
        s_l = sem("a_logits_ready")
        s_lc = sem("a_logits_copied")
        s_rk = sem("a_route_consts")
        s_rd = sem("a_route_dve_consts")
        s_r3 = sem("a_expert_steps")
        s_oh = sem("a_expert_ready")
        s_rkd = sem("a_ranks_ready")
        s_r4 = sem("a_place_steps")
        s_pos = sem("a_place_ready")
        s_ys = sem("a_y_staged")
        s_c = sem("a_tile_steps")
        s_row = sem("a_tile_rows_ready")
        s_eid = sem("a_expert_ids_ready")
        s_pad = sem("a_padding_zeroed")
        s_sc4 = [sem("a_scattered0"), sem("a_scattered1")]

        block = ctx.enter_context(nc.Block())

        def is_last(i):
            return isinstance(i, int) and i >= NQ - 1

        def steps(eng, step):
            for i in range(4):
                step(i, i % 2, i // 2, True, i >= 1, i >= 2, i >= 3)
            with eng.Fori(2, NQ // 2 - 1) as q2:
                for k in range(2):
                    step(2 * q2 + k, k, q2, True, True, True, True)
            for i in range(NQ - 2, NQ + 3):
                step(i, i % 2, i // 2, i < NQ, i - 1 < NQ, i - 2 < NQ, True)

        def zero_padding(eng, e):
            r = eng.value_load(pad_i[0:1, e:e + 1], min_val=0, max_val=SPARE - P)
            eng.dma_start(ysort_d[bass.ds(r, P), :], zero[:]).then_inc(s_pad, 16)

        @block.sync
        def _(sp):
            def load(i, k):
                wait_if(sp, s_xt, i, 1, -1)
                wait_if(sp, s_xb, i, 1, -1)
                sp.dma_start(xg[:, k], x1_d[bass.ds(i * G, G)].rearrange("g p d -> p g d")).then_inc(s_xg[k], 16)

            def expert_weights(q2):
                es = bass.ds(q2 * ES, ES)
                with nc.allow_non_contiguous_dma(reason="rows of weights"):
                    sp.dma_start(w1[:, es], W1[es].rearrange("e p f -> p e f")).then_inc(s_ew, 16)
                    sp.dma_start(w2[:, es].rearrange("p e (b d) -> p e b d", d=DM),
                                 W2[es].rearrange("e (b p) d -> p e b d", p=P)).then_inc(s_ew, 16)

            for k in range(2):
                load(k, k)
            expert_weights(0)
            with sp.Fori(1, NQ // 2) as q2:
                for k in range(2):
                    load(2 * q2 + k, k)
                expert_weights(q2)
            sp.dma_start(b1b[:].rearrange("p e f -> p (e f)"),
                         b1.rearrange("(o e) f -> o (e f)", o=1).broadcast_to([P, b1.shape[0] * b1.shape[1]])).then_inc(s_ew, 16)
            sp.dma_start(b2b[:].rearrange("p e f -> p (e f)"),
                         b2.rearrange("(o e) f -> o (e f)", o=1).broadcast_to([P, b2.shape[0] * b2.shape[1]])).then_inc(s_ew, 16)

            sp.dma_start(ysort_d[SPARE:SPARE + (NT - NG) * P, :].rearrange("(t p) d -> p t d", p=P),
                         zero[:].unsqueeze(1).to_broadcast([P, NT - NG, DM])).then_inc(s_pad, 16)
            sp.wait_ge(s_row, 1)
            for e in range(E // 2):
                zero_padding(sp, e)
            sp.wait_ge(s_pad, 16 * (E + 1))

        @block.gpsimd
        def _(pool):
            nc.gpsimd.memset(mask[:], -BIG).then_inc(s_mk, 1)
            nc.gpsimd.memset(mhalf[:], -0.5).then_inc(s_mk, 1)
            nc.gpsimd.memset(ones[:], 1.0).then_inc(s_mk, 1)
            nc.gpsimd.memset(v[:, :, :, :, HD:C], 1.0).then_inc(s_mk, 1)
            nc.gpsimd.tensor_copy(identb[:], ident[:]).then_inc(s_mk, 1)
            pool.wait_ge(s_mk, 5)
            for d in range(-(S - 1), S):
                nc.gpsimd.affine_select(out=mask[:], in_=mask[:], compare_op=ALU.not_equal, fill=0.0, base=TT * d,
                                        pattern=[[0, G], [-1, P]], channel_multiplier=1).then_inc(s_mk, 1)
                pool.wait_ge(s_mk, 6 + d + S - 1)
            nc.gpsimd.memset(tri[:], 1.0).then_inc(s_rk, 1)
            nc.gpsimd.memset(onesb[:], 1.0).then_inc(s_rk, 1)
            pool.wait_ge(s_rk, 2)
            nc.gpsimd.affine_select(out=tri[:], in_=tri[:], compare_op=ALU.is_ge, fill=0.0, base=-1,
                                    pattern=[[1, P]], channel_multiplier=-1).then_inc(s_rk, 1)
            pool.wait_ge(s_cc, 3)

            def step(i, k, q2, first, second, third, fourth):
                if first:
                    pool.wait_ge(s_xg[k], 16 * q2 + 16)
                    wait_if(pool, s_out, i, 1, -1)
                    nc.gpsimd.tensor_tensor(xb[:, k], xg[:, k], cstb[:].unsqueeze(1).to_broadcast([P, G, DM]),
                                            ALU.add).then_inc(s_xb, 1)
                if second:
                    pool.wait_ge(s_ve, i)
                    nc.gpsimd.tensor_tensor(rs[:], ve[:], mhalf[:], ALU.pow).then_inc(s_rs, 1)
                    pool.wait_ge(s_yn, i * G)
                    nc.gpsimd.tensor_tensor(ym[:], yn[:], g1b[:].unsqueeze(1).to_broadcast([P, G, DM]),
                                            ALU.mult).then_inc(s_ym, 1)
                    pool.wait_ge(s_ym, i)
                    wait_if(pool, s_yt, i, 1, -1)
                    wait_if(pool, s_ys, i, 1, -1)
                    nc.gpsimd.tensor_tensor(yq[:], ym[:], be1b[:].unsqueeze(1).to_broadcast([P, G, DM]),
                                            ALU.add).then_inc(s_y, 1)
                if fourth:
                    pool.wait_ge(s_ys, i - 2)
                    pool.wait_ge(s_pos, 3 * i - 6)
                    pool.sem_inc(s_gate, 1)
                    for g in range(G):
                        nc.gpsimd.indirect_dma_start(
                            out=ysort_d, out_offset=bass.IndirectOffsetOnAxis(ap=pidx[:, 1 - k, g:g + 1], axis=0),
                            in_=yst[:, 1 - k, g], in_offset=None).then_inc(s_sc4[1 - k], 16)

            steps(pool, step)
            for k in range(2):
                pool.wait_ge(s_sc4[k], 16 * G * (NQ // 2))

        NMK = 5 + 2 * S - 1

        @block.scalar
        def _(act):
            act.wait_ge(s_w, 16 * NW)
            nc.scalar.mul(bqs[:], bq[:, 0:1], SCALE).then_inc(s_cc, 1)
            act.wait_ge(s_wt, 4)
            nc.scalar.copy(wT[:].rearrange("p j d -> p (j d)"), pO[:]).then_inc(s_wc, 1)
            act.wait_ge(s_wt, 5)
            nc.scalar.copy(wgT[:], pV[:, 0:E]).then_inc(s_wc, 1)
            act.wait_ge(s_cp, 2)
            nc.scalar.copy(cstb[:], pB[:, 0:DM]).then_inc(s_cc, 1)
            act.wait_ge(s_cc, 3)

            def x_copy(i):
                act.wait_ge(s_xt, i + 1)
                wait_if(act, s_v, i, 1, 0)
                nc.scalar.copy(xT[:], pA[:, 0]).then_inc(s_xtc, 1)

            x_copy(0)

            def step(i, k, q2, first, second, third, fourth):
                if first:
                    act.wait_ge(s_qk, i + 1)
                    wait_if(act, s_sc, i, 1, 0)
                    nc.scalar.activation(qT[:], pA[:, 0], ACT.Identity, bias=bqs[:, 0:1], scale=SCALE).then_inc(s_qkc, 1)
                    nc.scalar.activation(kT[:], pA[:, 1], ACT.Identity, bias=bq[:, 1:2]).then_inc(s_qkc, 1)
                if second:
                    act.wait_ge(s_pt, i)
                    wait_if(act, s_o, i, 1, -1)
                    nc.scalar.copy(prT[:, 0:2], pS[:, 0:2, 1]).then_inc(s_pta, 1)
                if third:
                    act.wait_ge(s_yt, i - 1)
                    wait_if(act, s_l, i, 1, -2)
                    nc.scalar.copy(yT[:], pB[:, 0:T]).then_inc(s_ytc, 1)
                    nc.scalar.copy(yall[:, bass.ds((i - 2) * G, G)], yq[:]).then_inc(s_ya, 1)
                if second:
                    act.wait_ge(s_ot, i)
                    wait_if(act, s_po, i, 1, -1)
                    nc.scalar.copy(oT[:], pB[:, 0:T]).then_inc(s_otc, 1)
                if first and not is_last(i):
                    x_copy(i + 1)
                if first:
                    act.wait_ge(s_sh, i + 1)
                    wait_if(act, s_pt, i, 1, 0)
                    nc.scalar.activation(pr[:], sh[:], ACT.Exp).then_inc(s_ex, 1)
                if third:
                    if not (isinstance(i, int) and i < 4):
                        act.wait_ge(s_sc4[k], 16 * G * (q2 - 1))
                    nc.scalar.copy(yst[:, k], yq[:]).then_inc(s_ys, 1)

            steps(act, step)
            act.wait_ge(s_row, 1)
            for e in range(E // 2, E):
                zero_padding(act, e)

        @block.vector
        def _(dve):
            dve.wait_ge(s_cp, 1)
            nc.vector.tensor_tensor(cst[:], pV[0:1, 256:256 + DM], bor[:], ALU.add).then_inc(s_cc, 1)
            dve.wait_ge(s_mk, NMK)
            nc.vector.memset(run[:], 0.0).then_inc(s_rd, 1)
            nc.vector.tensor_scalar(iot8[:], iot0[:], float(E), None, ALU.add).then_inc(s_rd, 1)
            dve.wait_ge(s_rd, 2)

            def expert_of(i, k):
                n = 4 * (i - 2)
                dve.wait_ge(s_lc, i - 1)
                nc.vector.tensor_reduce(mxl[:], lg[:, k], AX.X, ALU.max).then_inc(s_r3, 1)
                dve.wait_ge(s_r3, n + 1)
                nc.vector.tensor_tensor(eq[:], lg[:, k], mxl[:].unsqueeze(2).to_broadcast([P, G, E]),
                                        ALU.is_equal).then_inc(s_r3, 1)
                dve.wait_ge(s_r3, n + 2)
                nc.vector.scalar_tensor_tensor(cand[:], eq[:], -float(E), iot8[:].unsqueeze(1).to_broadcast([P, G, E]),
                                               ALU.mult, ALU.add).then_inc(s_r3, 1)
                dve.wait_ge(s_r3, n + 3)
                nc.vector.tensor_reduce(idx[:, k], cand[:], AX.X, ALU.min).then_inc(s_r3, 1)
                dve.wait_ge(s_r3, n + 4)
                nc.vector.tensor_tensor(oh[:, k], iot0[:].unsqueeze(1).to_broadcast([P, G, E]),
                                        idx[:, k].unsqueeze(2).to_broadcast([P, G, E]), ALU.is_equal).then_inc(s_oh, 1)

            def ranks_of(i):
                n = 5 * (i - 3)
                dve.wait_ge(s_rkd, i - 2)
                if not (isinstance(i, int) and i < 4):
                    dve.wait_ge(s_r4, n)
                nc.vector.tensor_tensor(rank[:], pV[:, RK:RK + G * E].rearrange("p (g e) -> p g e", g=G),
                                        run[:].unsqueeze(1).to_broadcast([P, G, E]), ALU.add).then_inc(s_r4, 1)
                dve.wait_ge(s_r4, n + 1)
                nc.vector.tensor_tensor(run[:], pV[:, RK + G * E:RK + (G + 1) * E], run[:], ALU.add).then_inc(s_r4, 1)

            def place_of(i, k, q2):
                n = 5 * (i - 3)
                dve.wait_ge(s_r4, n + 2)
                nc.vector.tensor_tensor(mine[:], rank[:], oh[:, 1 - k], ALU.mult).then_inc(s_r4, 1)
                dve.wait_ge(s_r4, n + 3)
                nc.vector.tensor_reduce(rk[:], mine[:], AX.X, ALU.add).then_inc(s_r4, 1)
                dve.wait_ge(s_r4, n + 4)
                nc.vector.scalar_tensor_tensor(pos[:], idx[:, 1 - k], float(CAP), rk[:], ALU.mult, ALU.add).then_inc(s_r4, 1)
                dve.wait_ge(s_r4, n + 5)
                if not (isinstance(i, int) and i < 5):
                    dve.wait_ge(s_sc4[1 - k], 16 * G * (q2 - 2 + k))
                nc.vector.tensor_copy(pidx[:, 1 - k], pos[:]).then_inc(s_pos, 1)
                nc.vector.tensor_copy(before[:, bass.ds((i - 3) * G, G)], rk[:]).then_inc(s_pos, 1)
                nc.vector.tensor_copy(expert[:, bass.ds((i - 3) * G, G)], idx[:, 1 - k]).then_inc(s_pos, 1)

            def route(i):
                if 3 <= i < NQ + 3:
                    place_of(i, i % 2, i // 2)
                if 2 <= i < NQ + 2:
                    expert_of(i, i % 2)

            def step(i, k, q2, first, second, third, fourth):
                if second:
                    dve.wait_ge(s_pt, i)
                    wait_if(dve, s_o, i, 1, -1)
                    nc.vector.tensor_copy(prT[:, 2:4], pS[:, 2:4, 1]).then_inc(s_ptd, 1)
                if first:
                    dve.wait_ge(s_v, i + 1)
                    wait_if(dve, s_o, i, 1, -1)
                    nc.vector.tensor_copy(v[:, k, :, :, 0:HD],
                                          pV[:, 0:T].rearrange("p (g h d) -> p g h d", g=G, h=NH)).then_inc(s_vc, 1)
                if second:
                    dve.wait_ge(s_o, i)
                    o3 = pO[:, 0:G * NH * C].rearrange("p (g d) -> p g d", d=C)
                    nc.vector.reciprocal(rin[:], o3[:, :, HD]).then_inc(s_rin, 1)
                    dve.wait_ge(s_rin, i)
                    wait_if(dve, s_ot, i, 1, -1)
                    nc.vector.tensor_tensor(on[:].rearrange("p g (h d) -> p (g h) d", h=NH), o3[:, :, 0:HD],
                                            rin[:].unsqueeze(2).to_broadcast([P, G * NH, HD]), ALU.mult).then_inc(s_on, 1)
                if isinstance(i, int):
                    route(i - 1)
                elif k == 0:
                    place_of(i - 1, 1, q2 - 1)
                    expert_of(i - 1, 1)
                else:
                    place_of(i - 1, 0, q2)
                    expert_of(i - 1, 0)
                if first:
                    dve.wait_ge(s_sc, i + 1)
                    view = pS[:, :, 0].rearrange("p h (g k) -> p h g k", g=G)
                    nc.vector.tensor_reduce(mx[:], view, AX.X, ALU.max).then_inc(s_mx, 1)
                    dve.wait_ge(s_mx, i + 1)
                    wait_if(dve, s_ex, i, 1, 0)
                    nc.vector.tensor_tensor(sh[:].rearrange("p h (g k) -> p h g k", g=G), view,
                                            mx[:].unsqueeze(3).to_broadcast([P, NH, G, P]), ALU.subtract).then_inc(s_sh, 1)
                if third:
                    dve.wait_ge(s_l, i - 1)
                    if fourth:
                        dve.wait_ge(s_rkd, i - 2)
                    nc.vector.tensor_copy(lg[:, k],
                                          pV[:, T:T + G * E].rearrange("p (g e) -> p g e", g=G)).then_inc(s_lc, 1)
                if fourth:
                    ranks_of(i)
                if second:
                    dve.wait_ge(s_po, i)
                    dve.wait_ge(s_xb, i)
                    nc.vector.tensor_tensor(ro[:].rearrange("p g d -> p (g d)"), pO[:, 0:T],
                                            xb[:, 1 - k].rearrange("p g d -> p (g d)"), ALU.add).then_inc(s_out, 1)
                    dve.wait_ge(s_out, i)
                    for t in range(G):
                        nc.vector.bn_stats(st[:, t], ro[:, t]).then_inc(s_st, 1)
                    dve.wait_ge(s_st, i * G)
                    dve.sem_inc(s_gate, 1)
                    for t in range(G):
                        nc.vector.bn_aggr(mv[:, t], st[:, t]).then_inc(s_mv, 1)
                    dve.wait_ge(s_mv, i * G)
                    nc.vector.tensor_scalar(ve[:], mv[:, :, 1], EPS, None, ALU.add).then_inc(s_ve, 1)
                    dve.wait_ge(s_rs, i)
                    wait_if(dve, s_ym, i, 1, -1)
                    for t in range(G):
                        nc.vector.tensor_scalar(yn[:, t], ro[:, t], mv[:, t, 0:1], rs[:, t:t + 1], ALU.subtract,
                                                ALU.mult).then_inc(s_yn, 1)

            steps(dve, step)
            route(NQ + 2)

            step_c = [0]

            def link(ins):
                step_c[0] += 1
                ins.then_inc(s_c, 1)
                dve.wait_ge(s_c, step_c[0])

            dve.wait_ge(s_r4, 5 * NQ)
            dve.wait_ge(s_pos, 3 * NQ)
            link(nc.vector.tensor_tensor(pad[:], erow[:], run[:], ALU.add))
            nc.vector.tensor_copy(pad_i[:], pad[:]).then_inc(s_row, 1)
            link(nc.vector.tensor_tensor(cmp_[:], run[:].unsqueeze(2).to_broadcast([P, E, NG]),
                                         thr[:].unsqueeze(1).to_broadcast([P, E, NG]), ALU.is_gt))
            link(nc.vector.tensor_reduce(nt[:], cmp_[:], AX.X, ALU.add))
            link(nc.vector.tensor_tensor_scan(ntc[:], one8[:], nt[:], 0.0, ALU.mult, ALU.add))
            link(nc.vector.tensor_tensor(base[:], ntc[:], nt[:], ALU.subtract))
            each = [P, NT, E]
            link(nc.vector.tensor_tensor(ended[:], ntc[:].unsqueeze(1).to_broadcast(each),
                                         tl[:].unsqueeze(2).to_broadcast(each), ALU.is_le))
            link(nc.vector.tensor_tensor(begun[:], base[:].unsqueeze(1).to_broadcast(each),
                                         tl[:].unsqueeze(2).to_broadcast(each), ALU.is_le))
            link(nc.vector.tensor_tensor(begun[:], begun[:], ended[:], ALU.subtract))
            link(nc.vector.scalar_tensor_tensor(w[:], base[:], -float(P), erow[:], ALU.mult, ALU.add))
            link(nc.vector.tensor_scalar(w[:], w[:], -float(SPARE - P * NG), None, ALU.add))
            link(nc.vector.tensor_tensor(begun[:], begun[:], w[:].unsqueeze(1).to_broadcast(each), ALU.mult))
            link(nc.vector.tensor_reduce(trow[:], begun[:], AX.X, ALU.add))
            link(nc.vector.scalar_tensor_tensor(trow[:], tl[:], float(P), trow[:], ALU.mult, ALU.add))
            link(nc.vector.tensor_scalar(trow[:], trow[:], float(SPARE - P * NG), None, ALU.add))
            nc.vector.tensor_copy(trow_i[:], trow[:]).then_inc(s_row, 1)
            link(nc.vector.tensor_reduce(eid[:], ended[:], AX.X, ALU.add))
            link(nc.vector.tensor_scalar(eid[:], eid[:], float(E - 1), None, ALU.min))
            nc.vector.tensor_copy(eid_i[:], eid[:]).then_inc(s_eid, 1)
            every = [P, NG, E]
            link(nc.vector.tensor_tensor(first_of[:], iot0[:].unsqueeze(1).to_broadcast(every),
                                         expert[:].unsqueeze(2).to_broadcast(every), ALU.is_equal))
            link(nc.vector.tensor_tensor(first_of[:], first_of[:], base[:].unsqueeze(1).to_broadcast(every), ALU.mult))
            link(nc.vector.tensor_reduce(row[:], first_of[:], AX.X, ALU.add))
            link(nc.vector.scalar_tensor_tensor(row[:], row[:], float(P), before[:], ALU.mult, ALU.add))
            link(nc.vector.tensor_copy(pos_u[:], row[:]))

        @block.tensor
        def _(pe):
            def turn_x(i, k, q2):
                pe.wait_ge(s_xg[k], 16 * q2 + 16)
                wait_if(pe, s_qkc, i, 2, 0)
                for g in range(G):
                    mm = nc.tensor.transpose(pA[:, 0, g * P:(g + 1) * P], xg[:, k, g], ident[:])
                mm.then_inc(s_xt, 1)

            pe.wait_ge(s_w, 16 * NW)
            for j in range(4):
                nc.tensor.transpose(pO[:, j * P:(j + 1) * P], wnat[:, j], ident[:]).then_inc(s_wt, 1)
            nc.tensor.transpose(pV[:, 0:E], wgn[:], ident[0:E, 0:E]).then_inc(s_wt, 1)
            turn_x(0, 0, 0)
            pe.wait_ge(s_wc, 2)
            nc.tensor.matmul(pV[0:1, 256:256 + DM], bq[:, 2:3], wT[:, 3], start=True, stop=True).then_inc(s_cp, 1)
            pe.wait_ge(s_cc, 2)
            pe.wait_ge(s_mk, NMK)
            nc.tensor.matmul(pB[:, 0:DM], ones[0:1, :], cst[0:1, :], start=True, stop=True).then_inc(s_cp, 1)
            pe.wait_ge(s_cc, 3)

            def step(i, k, q2, first, second, third, fourth):
                if first:
                    pe.wait_ge(s_xtc, i + 1)
                    for j in range(2):
                        mm = nc.tensor.matmul(pA[:, j], wT[:, j], xT[:], start=True, stop=True)
                    mm.then_inc(s_qk, 1)
                if second:
                    pe.wait_ge(s_ex, i)
                    for h in range(NH):
                        for g in range(G):
                            mm = nc.tensor.transpose(pS[:, h, 1, g * P:(g + 1) * P], pr[:, h, g * P:(g + 1) * P], ident[:])
                    mm.then_inc(s_pt, 1)
                if first:
                    wait_if(pe, s_vc, i, 1, 0)
                    wait_if(pe, s_lc, i, 1, -2)
                    wait_if(pe, s_r4, i, 5, -18)
                    for g in range(G):
                        mm = nc.tensor.matmul(pV[:, g * P:(g + 1) * P], xT[:, g * P:(g + 1) * P], wT[:, 2], start=True,
                                              stop=True)
                    mm.then_inc(s_v, 1)
                if second:
                    pe.wait_ge(s_pta, i)
                    pe.wait_ge(s_ptd, i)
                    wait_if(pe, s_out, i, 1, -1)
                    for g in range(G):
                        for h in range(NH):
                            c = (g * NH + h) * C
                            mm = nc.tensor.matmul(pO[:, c:c + C], prT[:, h, g * P:(g + 1) * P], v[:, 1 - k, g, h],
                                                  start=True, stop=True)
                    mm.then_inc(s_o, 1)
                if third:
                    pe.wait_ge(s_y, i - 1)
                    pe.wait_ge(s_otc, i - 1)
                    for g in range(G):
                        mm = nc.tensor.transpose(pB[:, g * P:(g + 1) * P], yq[:, g], ident[:])
                    mm.then_inc(s_yt, 1)
                if first:
                    pe.wait_ge(s_qkc, 2 * i + 2)
                    wait_if(pe, s_sh, i, 1, 0)
                    for h in range(NH):
                        nc.tensor.matmul(pS[:, h, 0], identb[:], mask[:].rearrange("p g k -> p (g k)"), start=True,
                                         stop=False, skip_group_check=True)
                    for g in range(G):
                        for h in range(NH):
                            c = slice(g * P, (g + 1) * P)
                            hh = slice(h * HD, (h + 1) * HD)
                            mm = nc.tensor.matmul(pS[:, h, 0, c], qT[hh, c], kT[hh, c], start=False, stop=(g == G - 1),
                                                  skip_group_check=True, tile_position=(h * HD, 0))
                    mm.then_inc(s_sc, 1)
                if third:
                    pe.wait_ge(s_ytc, i - 1)
                    if first:
                        pe.wait_ge(s_vc, i + 1)
                    else:
                        wait_if(pe, s_lc, i, 1, -2)
                    for g in range(G):
                        mm = nc.tensor.matmul(pV[:, T + g * E:T + (g + 1) * E], yT[:, g * P:(g + 1) * P], wgT[:], start=True,
                                              stop=True)
                    mm.then_inc(s_l, 1)
                if fourth:
                    pe.wait_ge(s_oh, i - 2)
                    if first:
                        pe.wait_ge(s_vc, i + 1)
                    wait_if(pe, s_r4, i, 5, -18)
                    if not third:
                        pe.wait_ge(s_lc, i - 2)
                    o = [oh[:, 1 - k, g] for g in range(G)]
                    nc.tensor.matmul(pV[:, RK:RK + E], tri[:], o[0], start=True, stop=True)
                    nc.tensor.matmul(pV[:, RK + E:RK + 2 * E], tri[:], o[1], start=True, stop=False)
                    nc.tensor.matmul(pV[:, RK + E:RK + 2 * E], onesb[:], o[0], start=False, stop=True)
                    nc.tensor.matmul(pV[:, RK + 2 * E:RK + 3 * E], onesb[:], o[0], start=True, stop=False)
                    nc.tensor.matmul(pV[:, RK + 2 * E:RK + 3 * E], onesb[:], o[1], start=False, stop=True).then_inc(s_rkd, 1)
                if second:
                    pe.wait_ge(s_on, i)
                    for g in range(G):
                        mm = nc.tensor.transpose(pB[:, g * P:(g + 1) * P], on[:, g], ident[:])
                    mm.then_inc(s_ot, 1)
                if first and not is_last(i):
                    turn_x(i + 1, 1 - k, q2 + k)
                if second:
                    pe.wait_ge(s_otc, i)
                    for g in range(G):
                        c = slice(g * P, (g + 1) * P)
                        mm = nc.tensor.matmul(pO[:, c], oT[:, c], wT[:, 3], start=True, stop=True)
                    mm.then_inc(s_po, 1)

            steps(pe, step)


def build_moe(nc, shared, ident, x1_d, g2, be2, W1, b1, W2, b2, ysort_d, osort_d, CAP, NT, out):
    NG, _, DM = x1_d.shape
    E, _, DF = W1.shape
    SPARE = E * CAP
    NB = DF // P
    S = out.shape[0]
    TT = P // S
    G = 4
    NQ = NG // G
    yall, eid_i, trow_i, pos_u = (shared[n] for n in ("yall", "eid_i", "trow_i", "pos_u"))
    w1, w2, b1b, b2b = shared["w1"], shared["w2"], shared["b1b"], shared["b2b"]
    s_ew = shared["s_ew"]
    NEW = NG // 2 + 2

    with ExitStack() as ctx:
        def sb(name, shape, dt=F32):
            return ctx.enter_context(nc.sbuf_tensor(name, shape, dt))

        def ps(name, shape, dt=F32):
            return ctx.enter_context(nc.psum_tensor(name, shape, dt))

        def sem(name):
            return ctx.enter_context(nc.semaphore(name))

        mhalf = sb("m_mhalf", [P, G])
        ys = sb("m_ys", [P, 2, DM])
        yT = sb("m_yT", [P, 2, P])
        hh = sb("m_hh", [P, 2, DF])
        hT = sb("m_hT", [P, 2, NB, P])
        ob = sb("m_ob", [P, 2, DM])
        gp = sb("m_gp", [P, 2, G], U32)
        gb = sb("m_gb", [P, 2, G, DM])
        xg = sb("m_xg", [P, 2, G, DM])
        g2b = sb("m_g2b", [P, DM])
        be2b = sb("m_be2b", [P, DM])
        ra, rb = [sb(f"m_r{c}", [P, G, DM]) for c in "ab"]
        sta, stb = [sb(f"m_st{c}", [P, G, 6]) for c in "ab"]
        mva, mvb = [sb(f"m_mv{c}", [P, G, 2]) for c in "ab"]
        vea, veb = [sb(f"m_ve{c}", [P, G]) for c in "ab"]
        rsa, rsb = [sb(f"m_rs{c}", [P, G]) for c in "ab"]
        zn = sb("m_zn", [P, G, DM])
        zm = sb("m_zm", [P, G, DM])
        z = sb("m_z", [P, G, DM])
        fo = sb("m_fo", [P, 2, G, DM])

        pY = ps("m_pY", [P, 2, 512])
        pH = ps("m_pH", [P, 2, DF])
        pHT = ps("m_pHT", [P, 2, NB * P])

        s_gate = sem("m_gate_passed")
        s_k = sem("m_consts")
        s_w = sem("m_weights")
        s_ysl = [sem(f"m_tile_loaded{k}") for k in range(2)]
        s_ty = sem("m_tile_transposed")
        s_yc = sem("m_tileT_copied")
        s_h = sem("m_hidden_ready")
        s_hb = sem("m_hidden_biased")
        s_ht = sem("m_hidden_transposed")
        s_hc = sem("m_hiddenT_copied")
        s_o = sem("m_out_ready")
        s_ob = sem("m_out_biased")
        s_osd = [sem(f"m_out_stored{k}") for k in range(2)]
        s_gst = sem("m_gather_staged")
        s_g = [sem(f"m_gathered{k}") for k in range(2)]
        s_xg = [sem(f"m_x_loaded{k}") for k in range(2)]
        s_ra, s_rb = [sem(f"m_res_ready_{c}") for c in "ab"]
        s_sta, s_stb = [sem(f"m_stats_{c}") for c in "ab"]
        s_mva, s_mvb = [sem(f"m_meanvar_{c}") for c in "ab"]
        s_vea, s_veb = [sem(f"m_vareps_{c}") for c in "ab"]
        s_rsa, s_rsb = [sem(f"m_rstd_{c}") for c in "ab"]
        s_zn = sem("m_normalised")
        s_zm = sem("m_scaled")
        s_z = sem("m_z_ready")
        s_fo = sem("m_final_ready")
        s_out = [sem(f"m_stored{k}") for k in range(2)]

        block = ctx.enter_context(nc.Block())
        NTP = NT // 2

        @block.sync
        def _(sp):
            sp.dma_start(g2b[:], g2.rearrange("(o d) -> o d", o=1).broadcast_to([P, DM])).then_inc(s_w, 16)
            sp.dma_start(be2b[:], be2.rearrange("(o d) -> o d", o=1).broadcast_to([P, DM])).then_inc(s_w, 16)
            def tile(j, k):
                wait_if(sp, s_ty, j, 1, -1)
                r = sp.value_load(trow_i[0:1, bass.ds(j, 1)], min_val=0, max_val=SPARE + (NT - NG - 1) * P)
                sp.dma_start(ys[:, k], ysort_d[bass.ds(r, P), :]).then_inc(s_ysl[k], 16)

            for k in range(2):
                tile(k, k)
            with sp.Fori(1, NTP) as n:
                for k in range(2):
                    tile(2 * n + k, k)

            def xload(q, k):
                wait_if(sp, s_rb, q, 1, -1)
                sp.dma_start(xg[:, k], x1_d[bass.ds(q * G, G)].rearrange("g p d -> p g d")).then_inc(s_xg[k], 16)

            def put(q, k):
                sp.wait_ge(s_fo, q + 1)
                for s in range(S):
                    sp.dma_start(out[s, bass.ds(q * G * TT, G * TT), :].rearrange("(g t) d -> t g d", g=G),
                                 fo[s * TT:(s + 1) * TT, k]).then_inc(s_out[k], 16)

            for k in range(2):
                xload(k, k)
            with sp.Fori(1, NQ // 2) as q2:
                for k in range(2):
                    xload(2 * q2 + k, k)
                    put(2 * q2 + k - 2, k)
            for k in range(2):
                put(NQ - 2 + k, k)
            for k in range(2):
                sp.wait_ge(s_out[k], 16 * S * (NQ // 2))

        def final_steps(eng, step):
            for k in range(2):
                step(k, k, 0, True, k >= 1, True)
            with eng.Fori(1, NQ // 2 - 1) as q2:
                for k in range(2):
                    step(2 * q2 + k, k, q2, True, True, True)
            for k in range(2):
                step(NQ - 2 + k, k, NQ // 2 - 1, True, True, False)
            step(NQ, 0, NQ // 2, False, True, False)

        @block.gpsimd
        def _(pool):
            nc.gpsimd.memset(mhalf[:], -0.5).then_inc(s_k, 1)
            for k in range(2):
                pool.wait_ge(s_osd[k], 16 * NTP)

            def gather(k, ts):
                for t in ts:
                    nc.gpsimd.indirect_dma_start(
                        out=gb[:, k, t], out_offset=None, in_=osort_d,
                        in_offset=bass.IndirectOffsetOnAxis(ap=gp[:, k, t:t + 1], axis=0)).then_inc(s_g[k], 16)

            def step(i, k, q2, first, second, more):
                if first:
                    pool.wait_ge(s_vea, i + 1)
                    wait_if(pool, s_zn, i, G, 0)
                    nc.gpsimd.tensor_tensor(rsa[:], vea[:], mhalf[:], ALU.pow).then_inc(s_rsa, 1)
                if second:
                    pool.wait_ge(s_veb, i)
                    wait_if(pool, s_fo, i, 1, -1)
                    nc.gpsimd.tensor_tensor(rsb[:], veb[:], mhalf[:], ALU.pow).then_inc(s_rsb, 1)
                if more:
                    pool.wait_ge(s_gst, i + 3)
                    pool.sem_inc(s_gate, 1)
                    gather(k, range(G // 2))
                if first:
                    pool.wait_ge(s_zm, i + 1)
                    wait_if(pool, s_rb, i, 1, 0)
                    nc.gpsimd.tensor_tensor(z[:], zm[:], be2b[:].unsqueeze(1).to_broadcast([P, G, DM]),
                                            ALU.add).then_inc(s_z, 1)
                if more:
                    gather(k, range(G // 2, G))

            pool.wait_ge(s_w, 32)
            pool.wait_ge(s_k, 1)
            pool.wait_ge(s_gst, 2)
            for k in range(2):
                gather(k, range(G))
            final_steps(pool, step)

        @block.vector
        def _(dve):
            dve.wait_ge(s_ew, 16 * NEW)

            def hidden(j, k, e):
                dve.wait_ge(s_h, j + 1)
                wait_if(dve, s_ht, j, 1, -1)
                nc.vector.tensor_tensor(hh[:, k], pH[:, k], b1b[:, bass.ds(e, 1)].rearrange("p o f -> p (o f)"),
                                        ALU.add).then_inc(s_hb, 1)

            def outb(j, k, e, j2):
                dve.wait_ge(s_o, j + 1)
                wait_if(dve, s_osd[k], j2, 16, 0)
                nc.vector.tensor_tensor(ob[:, k], pY[:, k, P:2 * P], b2b[:, bass.ds(e, 1)].rearrange("p o f -> p (o f)"),
                                        ALU.add).then_inc(s_ob, 1)

            def expert(j):
                return dve.value_load(eid_i[0:1, bass.ds(j, 1)], min_val=0, max_val=E - 1)

            def pair(n, last=False):
                if not last:
                    for k in range(2):
                        hidden(2 * n + 2 + k, k, expert(2 * n + 2 + k))
                for k in range(2):
                    outb(2 * n + k, k, expert(2 * n + k), n)

            for k in range(2):
                hidden(k, k, expert(k))
            pair(0)
            with dve.Fori(1, NTP - 1) as n:
                pair(n)
            pair(NTP - 1, last=True)

            def stage_index(q, k):
                nc.vector.tensor_copy(gp[:, k], pos_u[:, bass.ds(q * G, G)]).then_inc(s_gst, 1)

            def stats(n, src, st, s_st, mv, s_mv, ve, s_ve):
                for t in range(G):
                    nc.vector.bn_stats(st[:, t], src[:, t]).then_inc(s_st, 1)
                dve.wait_ge(s_st, G * n)
                dve.sem_inc(s_gate, 1)
                for t in range(G):
                    nc.vector.bn_aggr(mv[:, t], st[:, t]).then_inc(s_mv, 1)
                dve.wait_ge(s_mv, G * n)
                nc.vector.tensor_scalar(ve[:], mv[:, :, 1], EPS, None, ALU.add).then_inc(s_ve, 1)

            def step(i, k, q2, first, second, more):
                if first:
                    dve.wait_ge(s_g[k], 16 * G * q2 + 16 * G)
                    wait_if(dve, s_zn, i, G, 0)
                    nc.vector.tensor_tensor(ra[:], gb[:, k], yall[:, bass.ds(i * G, G)], ALU.add).then_inc(s_ra, 1)
                    dve.wait_ge(s_ra, i + 1)
                    if more:
                        stage_index(i + 2, k)
                    wait_if(dve, s_rsa, i, 1, 0)
                    stats(i + 1, ra, sta, s_sta, mva, s_mva, vea, s_vea)
                if second:
                    dve.wait_ge(s_z, i)
                    if k == 0:
                        dve.wait_ge(s_xg[1], 16 * q2)
                    else:
                        dve.wait_ge(s_xg[0], 16 * q2 + 16)
                    wait_if(dve, s_fo, i, 1, -1)
                    nc.vector.tensor_tensor(rb[:], z[:], xg[:, 1 - k], ALU.add).then_inc(s_rb, 1)
                    dve.wait_ge(s_rb, i)
                    wait_if(dve, s_rsb, i, 1, -1)
                    stats(i, rb, stb, s_stb, mvb, s_mvb, veb, s_veb)
                if first:
                    dve.wait_ge(s_rsa, i + 1)
                    wait_if(dve, s_zm, i, 1, 0)
                    for t in range(G):
                        nc.vector.tensor_scalar(zn[:, t], ra[:, t], mva[:, t, 0:1], rsa[:, t:t + 1], ALU.subtract,
                                                ALU.mult).then_inc(s_zn, 1)
                    dve.wait_ge(s_zn, G * (i + 1))
                    wait_if(dve, s_z, i, 1, 0)
                    nc.vector.tensor_tensor(zm[:], zn[:], g2b[:].unsqueeze(1).to_broadcast([P, G, DM]),
                                            ALU.mult).then_inc(s_zm, 1)
                if second:
                    dve.wait_ge(s_rsb, i)
                    if k == 0 and not (isinstance(q2, int) and q2 <= 1):
                        dve.wait_ge(s_out[1], 16 * S * (q2 - 1))
                    if k == 1 and not (isinstance(q2, int) and q2 == 0):
                        dve.wait_ge(s_out[0], 16 * S * q2)
                    for t in range(G):
                        ins = nc.vector.tensor_scalar(fo[:, 1 - k, t], rb[:, t], mvb[:, t, 0:1], rsb[:, t:t + 1],
                                                      ALU.subtract, ALU.mult)
                    ins.then_inc(s_fo, 1)

            dve.wait_ge(s_w, 32)
            for k in range(2):
                stage_index(k, k)
            final_steps(dve, step)

        @block.scalar
        def _(act):

            def tile(j, k):
                act.wait_ge(s_ty, j + 1)
                wait_if(act, s_h, j, 1, -1)
                nc.scalar.copy(yT[:, k], pY[:, k, 0:P]).then_inc(s_yc, 1)

            def relu(j, k):
                act.wait_ge(s_ht, j + 1)
                wait_if(act, s_o, j, 1, -1)
                nc.scalar.activation(hT[:, k], pHT[:, k].rearrange("p (b t) -> p b t", b=NB), ACT.Relu).then_inc(s_hc, 1)

            def store(j, k):
                act.wait_ge(s_ob, j + 1)
                act.dma_start(osort_d[bass.ds(j * P, P), :], ob[:, k]).then_inc(s_osd[k], 16)

            def pair(n, first=False, last=False):
                for k in range(2):
                    if not last:
                        tile(2 * n + 2 + k, k)
                for k in range(2):
                    if not first:
                        store(2 * n - 2 + k, k)
                for k in range(2):
                    relu(2 * n + k, k)

            for k in range(2):
                tile(k, k)
            pair(0, first=True)
            with act.Fori(1, NTP - 1) as n:
                pair(n)
            pair(NTP - 1, last=True)
            for k in range(2):
                store(NT - 2 + k, k)

        @block.tensor
        def _(pe):
            pe.wait_ge(s_ew, 16 * NEW)

            def turn(j, k, j2):
                pe.wait_ge(s_ysl[k], 16 * j2 + 16)
                wait_if(pe, s_ob, j, 1, -3)
                nc.tensor.transpose(pY[:, k, 0:P], ys[:, k], ident[:]).then_inc(s_ty, 1)

            def up(j, k, e):
                pe.wait_ge(s_yc, j + 1)
                wait_if(pe, s_hb, j, 1, -1)
                nc.tensor.matmul(pH[:, k], yT[:, k], w1[:, bass.ds(e, 1)].rearrange("p o f -> p (o f)"), start=True,
                                 stop=True).then_inc(s_h, 1)

            def turn_hidden(j, k):
                pe.wait_ge(s_hb, j + 1)
                wait_if(pe, s_hc, j, 1, -1)
                for b in range(NB):
                    mm = nc.tensor.transpose(pHT[:, k, b * P:(b + 1) * P], hh[:, k, b * P:(b + 1) * P], ident[:])
                mm.then_inc(s_ht, 1)

            def down(j, k, e):
                pe.wait_ge(s_hc, j + 1)
                for b in range(NB):
                    mm = nc.tensor.matmul(pY[:, k, P:2 * P], hT[:, k, b],
                                          w2[:, bass.ds(e, 1), b * DM:(b + 1) * DM].rearrange("p o d -> p (o d)"),
                                          start=(b == 0), stop=(b == NB - 1))
                mm.then_inc(s_o, 1)

            def expert(j):
                return pe.value_load(eid_i[0:1, bass.ds(j, 1)], min_val=0, max_val=E - 1)

            def pair(n, last=False):
                if not last:
                    for k in range(2):
                        turn(2 * n + 2 + k, k, n + 1)
                for k in range(2):
                    turn_hidden(2 * n + k, k)
                if not last:
                    for k in range(2):
                        up(2 * n + 2 + k, k, expert(2 * n + 2 + k))
                for k in range(2):
                    down(2 * n + k, k, expert(2 * n + k))

            for k in range(2):
                turn(k, k, 0)
            for k in range(2):
                up(k, k, expert(k))
            pair(0)
            with pe.Fori(1, NTP - 1) as n:
                pair(n)
            pair(NTP - 1, last=True)


def build_ffn(nc, aw, x1_d, g2, be2, W1, b1, W2, b2, out):
    NG, _, DM = x1_d.shape
    E, _, DF = W1.shape
    NT = -(-(NG + E - 1) // 2) * 2
    CAP = NG * P + P
    ysort_d = nc.dram_tensor("ysort", [E * CAP + (NT - NG) * P, DM], F32).ap()
    osort_d = nc.dram_tensor("osort", [NT * P, DM], F32).ap()
    with ExitStack() as ctx:
        def sb(name, shape, dt=F32):
            return ctx.enter_context(nc.sbuf_tensor(name, shape, dt))

        shared = {
            "yall": sb("yall", [P, NG, DM]),
            "w1": sb("w1", [P, E, DF]), "w2": sb("w2", [P, E, DF]),
            "b1b": sb("b1b", [P, E, DF]), "b2b": sb("b2b", [P, E, DM]),
            "s_ew": ctx.enter_context(nc.semaphore("expert_weights")),
            "run": sb("tokens_so_far", [P, E]),
            "expert": sb("expert", [P, NG]),
            "before": sb("before", [P, NG]),
            "zero": sb("zero", [P, DM]),
            "iot0": sb("iota0", [P, E]),
            "erow": sb("expert_row", [P, E]),
            "thr": sb("thresholds", [P, NG]),
            "tl": sb("tile_numbers", [P, NT]),
            "one8": sb("one8", [P, E]),
            "pad_i": sb("padding_rows", [P, E], I32),
            "eid_i": sb("tile_experts", [P, NT], I32),
            "trow_i": sb("tile_rows", [P, NT], I32),
            "pos_u": sb("output_rows", [P, NG], U32),
        }
        e_i = sb("iota_e", [P, E], I32)
        thr_i = sb("iota_thr", [P, NG], I32)
        tl_i = sb("iota_tile", [P, NT], I32)
        s_iota = ctx.enter_context(nc.semaphore("iotas_ready"))
        s_const = ctx.enter_context(nc.semaphore("routing_consts"))
        with nc.Block() as block:
            @block.gpsimd
            def _(pool):
                nc.gpsimd.iota(e_i[:], pattern=[[1, E]], base=0, channel_multiplier=0).then_inc(s_iota, 1)
                nc.gpsimd.iota(thr_i[:], pattern=[[P, NG]], base=0, channel_multiplier=0).then_inc(s_iota, 1)
                nc.gpsimd.iota(tl_i[:], pattern=[[1, NT]], base=0, channel_multiplier=0).then_inc(s_iota, 1)

            @block.vector
            def _(dve):
                nc.vector.memset(shared["zero"][:], 0.0).then_inc(s_const, 1)
                nc.vector.memset(shared["one8"][:], 1.0).then_inc(s_const, 1)
                dve.wait_ge(s_iota, 3)
                nc.vector.tensor_copy(shared["iot0"][:], e_i[:]).then_inc(s_const, 1)
                nc.vector.tensor_scalar(shared["erow"][:], e_i[:], float(CAP), None, ALU.mult).then_inc(s_const, 1)
                nc.vector.tensor_copy(shared["thr"][:], thr_i[:]).then_inc(s_const, 1)
                nc.vector.tensor_copy(shared["tl"][:], tl_i[:]).then_inc(s_const, 1)
                dve.wait_ge(s_const, 6)

        build_attention(nc, shared, aw, x1_d, E, W1, b1, W2, b2, ysort_d, CAP, NT)
        build_moe(nc, shared, aw["ident"], x1_d, g2, be2, W1, b1, W2, b2, ysort_d, osort_d, CAP, NT, out)


def build(nc, ins, out):
    x = ins["L0_attn_x"]
    NS, L, DM = x.shape
    x1_d = nc.dram_tensor("x1_grouped", [NS * L // P, P, DM], F32).ap()
    ffn = {n: ins["L0_ffn_" + n] for n in ("Wqkv", "bqkv", "Wo", "bo", "g1", "be1", "g2", "be2", "Wg", "W1", "b1", "W2", "b2")}
    with ExitStack() as ctx:
        aw = attention_weights(nc, ctx, DM, ffn["Wg"].shape[0])

        def load_next(sp):
            load_attention_weights(nc, sp, aw, *(ffn[n] for n in ("Wqkv", "bqkv", "Wo", "bo", "g1", "be1", "Wg")))

        build_mamba(nc, x, *(ins["L0_attn_" + n] for n in
                             ("norm_w", "norm_b", "W_in", "conv_w", "conv_b", "W_x", "W_dt", "b_dt", "A_log", "D", "W_out")),
                    x1_d, aw["ident"], load_next)
        build_ffn(nc, aw, x1_d, *(ffn[n] for n in ("g2", "be2", "W1", "b1", "W2", "b2")), out)


_INS = ["L0_attn_x", "L0_attn_norm_w", "L0_attn_norm_b", "L0_attn_W_in", "L0_attn_conv_w", "L0_attn_conv_b",
        "L0_attn_W_x", "L0_attn_W_dt", "L0_attn_b_dt", "L0_attn_A_log", "L0_attn_D", "L0_attn_W_out", "L0_ffn_Wqkv",
        "L0_ffn_bqkv", "L0_ffn_Wo", "L0_ffn_bo", "L0_ffn_g1", "L0_ffn_be1", "L0_ffn_g2", "L0_ffn_be2", "L0_ffn_Wg",
        "L0_ffn_W1", "L0_ffn_b1", "L0_ffn_W2", "L0_ffn_b2"]


def kernel(**inputs):
    import concourse.bacc as bacc
    from concourse.bass_utils import run_bass_kernel_spmd

    nc = bacc.Bacc("TRN2", target_bir_lowering=False, num_devices=1)
    arrays, ins = {}, {}
    for name in _INS:
        a = np.ascontiguousarray(inputs[name])
        arrays[f"in_{name}"] = a
        ins[name] = nc.dram_tensor(f"in_{name}", a.shape, mybir.dt.from_np(a.dtype), kind="ExternalInput").ap()
    out = nc.dram_tensor("out", arrays["in_L0_attn_x"].shape, F32, kind="ExternalOutput").ap()
    build(nc, ins, out)
    r = run_bass_kernel_spmd(nc, [arrays], core_ids=[0])
    return r.results[0]["out"]
```
